# Optimizing a Trainium2 kernel written in Bass

```python
import numpy as np
import jax
import jax.numpy as jnp

def _softmax(x, axis=-1):
    return jax.nn.softmax(x, axis=axis)

def _gelu(x):
    return jax.nn.gelu(x, approximate=True)

def _silu(x):
    return jax.nn.silu(x)

def _sigmoid(x):
    return jax.nn.sigmoid(x)

def _layernorm(x, axis=-1, eps=1e-05):
    m = jnp.mean(x, axis=axis, keepdims=True)
    v = jnp.var(x, axis=axis, keepdims=True)
    return (x - m) / jnp.sqrt(v + eps)

def _scatter_add(tgt, idx, src, axis=0):
    return tgt.at[idx].add(src)

def _segment_sum(src, seg, n):
    return jax.ops.segment_sum(src, seg, n)
kernel_name = 'mk_xattn_ffn_d4_seqx_r8_783672'

def setup_inputs(seed: int=0):
    np.random.seed(seed)
    _w = jnp.asarray

    def _rec_inputs():
        import jax
        import jax.numpy as jnp
        _rk = jax.random.key(seed)
        x = -0.0002928 + 1 * jax.random.normal(jax.random.fold_in(_rk, 1), (16, 128, 128), jnp.float32)
        _lenS = 128 - jax.random.randint(jax.random.fold_in(_rk, 7), (16,), 0, max(1, 128 // 4) + 1, jnp.int32)
        _lenS2 = 128 - jax.random.randint(jax.random.fold_in(_rk, 8), (16,), 0, max(1, 128 // 4) + 1, jnp.int32)
        _ctx_1024P = jax.random.normal(jax.random.fold_in(_rk, 11), (16, 16, 128), jnp.float32)
        _ctx_1024c = jax.random.dirichlet(jax.random.fold_in(_rk, 511), 0.3 * jnp.ones((16,), jnp.float32), (16, 128))
        _ctx_1024t = jnp.einsum('bsk,bkd->bsd', _ctx_1024c, _ctx_1024P)
        _ctx_1024t = _ctx_1024t * jax.lax.rsqrt(jnp.mean(jnp.square(_ctx_1024t)) + 1e-12) * 0.953939
        ctx_1024 = -1.39393e-06 + 0.999914 * (_ctx_1024t + 0.3 * jax.random.normal(jax.random.fold_in(_rk, 611), (16, 128, 128), jnp.float32))
        _ctxb_2048x32P = jax.random.normal(jax.random.fold_in(_rk, 13), (16, 16, 32), jnp.float32)
        _ctxb_2048x32c = jax.random.dirichlet(jax.random.fold_in(_rk, 513), 0.3 * jnp.ones((16,), jnp.float32), (16, 128))
        _ctxb_2048x32t = jnp.einsum('bsk,bkd->bsd', _ctxb_2048x32c, _ctxb_2048x32P)
        _ctxb_2048x32t = _ctxb_2048x32t * jax.lax.rsqrt(jnp.mean(jnp.square(_ctxb_2048x32t)) + 1e-12) * 0.953939
        ctxb_2048x32 = 0.000843197 + 0.998132 * (_ctxb_2048x32t + 0.3 * jax.random.normal(jax.random.fold_in(_rk, 613), (16, 128, 32), jnp.float32))
        _validS = jnp.arange(128)[None, :] < _lenS[:, None]
        _validS2 = jnp.arange(128)[None, :] < _lenS2[:, None]
        _causal = jnp.tril(jnp.ones((128, 128), dtype=bool))
        mask_BxSxS2_bk1 = jnp.broadcast_to(_validS2[:, None, :], (16, 128, 128))
        return (x, ctx_1024, ctxb_2048x32, mask_BxSxS2_bk1)
    x, ctx_1024, ctxb_2048x32, mask_BxSxS2_bk1 = _rec_inputs()

    def _L0_xattn_setup():
        import jax, jax.numpy as jnp
        import numpy as np
        DIM = 128
        HEADS = 16
        DIM_HEAD = 64
        INNER = HEADS * DIM_HEAD
        B, N = (2, 256)
        key = jax.random.key(seed)
        ks = jax.random.split(key, 8)
        q = jax.random.normal(ks[0], (B, N, DIM), dtype=jnp.float32)
        k = jax.random.normal(ks[1], (B, N, DIM), dtype=jnp.float32)
        v = jax.random.normal(ks[2], (B, N, DIM), dtype=jnp.float32)
        causal = jnp.triu(jnp.ones((N, N), dtype=jnp.bool_), k=1)
        mask = jnp.broadcast_to(causal, (B, N, N))
        s = 0.02
        Wq = jax.random.normal(ks[3], (DIM, INNER), dtype=jnp.float32) * s
        Wk = jax.random.normal(ks[4], (DIM, INNER), dtype=jnp.float32) * s
        Wv = jax.random.normal(ks[5], (DIM, INNER), dtype=jnp.float32) * s
        Wo = jax.random.normal(ks[6], (INNER, DIM), dtype=jnp.float32) * s
        bo = jnp.zeros((DIM,), dtype=jnp.float32)
        return {'q': q, 'k': k, 'v': v, 'mask': mask, 'Wq': Wq, 'Wk': Wk, 'Wv': Wv, 'Wo': Wo, 'bo': bo}
    _L0_xattn_all = _L0_xattn_setup()
    _L0_xattn_in = {k: v for k, v in _L0_xattn_all.items() if k in ('Wq', 'Wk', 'Wv', 'Wo', 'bo')}
    del _L0_xattn_all

    def _L0_ffn_setup():
        import jax, jax.numpy as jnp
        import numpy as np
        B, S, D, F, E = (2, 256, 128, 512, 8)
        LN_EPS = 1e-05

        def _layer_norm(x, gamma, beta):
            mu = jnp.mean(x, axis=-1, keepdims=True)
            var = jnp.mean(jnp.square(x - mu), axis=-1, keepdims=True)
            return (x - mu) * jax.lax.rsqrt(var + LN_EPS) * gamma + beta
        key = jax.random.key(seed)
        ks = jax.random.split(key, 8)

        def xavier(k, shape):
            fan_in, fan_out = (shape[-1], shape[-2])
            a = jnp.sqrt(6.0 / (fan_in + fan_out))
            return jax.random.uniform(k, shape, jnp.float32, -a, a)
        return {'tgt': jax.random.normal(ks[0], (B, S, D), jnp.float32), 'Wr': xavier(ks[1], (E, D)), 'br': jnp.zeros((E,), jnp.float32), 'W1': xavier(ks[2], (E, F, D)), 'b1': jnp.zeros((E, F), jnp.float32), 'W2': xavier(ks[3], (E, D, F)), 'b2': jnp.zeros((E, D), jnp.float32), 'gamma': jnp.ones((D,), jnp.float32), 'beta': jnp.zeros((D,), jnp.float32)}
    _L0_ffn_all = _L0_ffn_setup()
    _L0_ffn_in = {k: v for k, v in _L0_ffn_all.items() if k in ('Wr', 'br', 'W1', 'b1', 'W2', 'b2', 'gamma', 'beta')}
    del _L0_ffn_all

    def _L1_xattn_setup():
        import jax, jax.numpy as jnp
        import numpy as np
        from jax import lax
        NUM_HEADS = 16
        DIM = 128
        BATCH = 4
        SEQ = 256
        key = jax.random.key(seed)
        ks = jax.random.split(key, 12)
        f32 = jnp.float32
        q = jax.random.normal(ks[0], (BATCH, SEQ, DIM), dtype=f32)
        k = jax.random.normal(ks[1], (BATCH, SEQ, DIM), dtype=f32)
        v = jax.random.normal(ks[2], (BATCH, SEQ, DIM), dtype=f32)
        lim = 1.0 / np.sqrt(DIM)
        Wi = jax.random.uniform(ks[3], (DIM, DIM), minval=-lim, maxval=lim, dtype=f32)
        bi = jax.random.uniform(ks[4], (DIM,), minval=-lim, maxval=lim, dtype=f32)
        Wg = jax.random.uniform(ks[5], (DIM, DIM), minval=-lim, maxval=lim, dtype=f32)
        bg = jax.random.uniform(ks[6], (DIM,), minval=-lim, maxval=lim, dtype=f32)
        Wo = jax.random.uniform(ks[7], (DIM, DIM), minval=-lim, maxval=lim, dtype=f32)
        bo = jax.random.uniform(ks[8], (DIM,), minval=-lim, maxval=lim, dtype=f32)
        A = jax.random.normal(ks[9], (DIM, DIM), dtype=f32) * 0.1
        Bm = jax.random.normal(ks[10], (DIM, DIM), dtype=f32) * 0.1
        decay = jnp.full((1, NUM_HEADS, 1), 0.9, dtype=f32)
        return dict(q=q, k=k, v=v, Wi=Wi, bi=bi, Wg=Wg, bg=bg, A=A, Bm=Bm, Wo=Wo, bo=bo, decay=decay)
    _L1_xattn_all = _L1_xattn_setup()
    _L1_xattn_in = {k: v for k, v in _L1_xattn_all.items() if k in ('Wi', 'bi', 'Wg', 'bg', 'A', 'Bm', 'Wo', 'bo', 'decay')}
    del _L1_xattn_all

    def _L1_ffn_setup():
        import jax, jax.numpy as jnp
        import numpy as np
        E = 8
        H = 128
        D = 128
        TOP_K = 2
        key = jax.random.key(seed)
        k0, k1, k2, k3 = jax.random.split(key, 4)
        x = jax.random.normal(k0, (1, 256, H), dtype=jnp.float32)
        router_w = jax.random.normal(k1, (E, H), dtype=jnp.float32) * (1.0 / np.sqrt(H))
        up_proj = jax.random.normal(k2, (E, H, 2 * D), dtype=jnp.float32) * (1.0 / np.sqrt(H))
        down_proj = jax.random.normal(k3, (E, D, H), dtype=jnp.float32) * (1.0 / np.sqrt(D))
        return {'x': x, 'router_w': router_w, 'up_proj': up_proj, 'down_proj': down_proj}
    _L1_ffn_all = _L1_ffn_setup()
    _L1_ffn_in = {k: v for k, v in _L1_ffn_all.items() if k in ('router_w', 'up_proj', 'down_proj')}
    del _L1_ffn_all

    def _L2_xattn_setup():
        import jax, jax.numpy as jnp
        import numpy as np
        B, L, D, H, NF = (4, 256, 128, 16, 32)
        THRESHOLD = 0.1
        key = jax.random.key(seed)
        ks = jax.random.split(key, 12)
        s = 1.0 / np.sqrt(D)
        return {'q_x': jax.random.normal(ks[0], (B, L, D), jnp.float32), 'k_x': jax.random.normal(ks[1], (B, L, D), jnp.float32), 'v_x': jax.random.normal(ks[2], (B, L, D), jnp.float32), 'energy_coeffs': jax.random.normal(ks[3], (B, L, NF), jnp.float32), 'Wq': jax.random.normal(ks[4], (D, D), jnp.float32) * s, 'bq': jnp.zeros((D,), jnp.float32), 'Wk': jax.random.normal(ks[5], (D, D), jnp.float32) * s, 'bk': jnp.zeros((D,), jnp.float32), 'Wv': jax.random.normal(ks[6], (D, D), jnp.float32) * s, 'bv': jnp.zeros((D,), jnp.float32), 'Wo': jax.random.normal(ks[7], (D, D), jnp.float32) * s, 'bo': jnp.zeros((D,), jnp.float32)}
    _L2_xattn_all = _L2_xattn_setup()
    _L2_xattn_in = {k: v for k, v in _L2_xattn_all.items() if k in ('Wq', 'bq', 'Wk', 'bk', 'Wv', 'bv', 'Wo', 'bo')}
    del _L2_xattn_all

    def _L2_ffn_setup():
        import jax, jax.numpy as jnp
        import numpy as np
        TOP_K = 2
        NUM_EXPERTS = 8
        DIM = 128
        HIDDEN = 352
        BS, SLEN = (2, 128)

        def _grouped_ffn(x, w1, w2, w3, counts):
            num_experts = w1.shape[0]
            ends = jnp.cumsum(counts)
            starts = ends - counts
            t = jnp.arange(x.shape[0])
            out = jnp.zeros((x.shape[0], w2.shape[-1]), x.dtype)
            for e in range(num_experts):
                m = ((t >= starts[e]) & (t < ends[e])).astype(x.dtype)[:, None]
                xe = x * m
                h = jax.nn.silu(xe @ w1[e]) * (xe @ w3[e])
                out = out + h @ w2[e] * m
            return out
        key = jax.random.key(seed)
        k = jax.random.split(key, 5)
        std = 0.02
        return {'x': jax.random.normal(k[0], (BS, SLEN, DIM), jnp.float32), 'gate_w': jax.random.normal(k[1], (NUM_EXPERTS, DIM), jnp.float32) * std, 'expert_bias': jnp.zeros((NUM_EXPERTS,), jnp.float32), 'w1': jax.random.normal(k[2], (NUM_EXPERTS, DIM, HIDDEN), jnp.float32) * std, 'w2': jax.random.normal(k[3], (NUM_EXPERTS, HIDDEN, DIM), jnp.float32) * std, 'w3': jax.random.normal(k[4], (NUM_EXPERTS, DIM, HIDDEN), jnp.float32) * std}
    _L2_ffn_all = _L2_ffn_setup()
    _L2_ffn_in = {k: v for k, v in _L2_ffn_all.items() if k in ('gate_w', 'expert_bias', 'w1', 'w2', 'w3')}
    del _L2_ffn_all

    def _L3_xattn_setup():
        import jax, jax.numpy as jnp
        import numpy as np
        from math import sqrt
        D_MODEL = 128
        N_HEADS = 16
        E = D_MODEL // N_HEADS
        key = jax.random.key(seed)
        ks = jax.random.split(key, 11)
        B, L, S = (2, 256, 256)
        s = 1.0 / sqrt(D_MODEL)
        return {'queries': jax.random.normal(ks[0], (B, L, D_MODEL), jnp.float32), 'keys': jax.random.normal(ks[1], (B, S, D_MODEL), jnp.float32), 'values': jax.random.normal(ks[2], (B, S, D_MODEL), jnp.float32), 'Wq': jax.random.normal(ks[3], (D_MODEL, D_MODEL), jnp.float32) * s, 'bq': jnp.zeros((D_MODEL,), jnp.float32), 'Wk': jax.random.normal(ks[4], (D_MODEL, D_MODEL), jnp.float32) * s, 'bk': jnp.zeros((D_MODEL,), jnp.float32), 'Wv': jax.random.normal(ks[5], (D_MODEL, D_MODEL), jnp.float32) * s, 'bv': jnp.zeros((D_MODEL,), jnp.float32), 'Wo': jax.random.normal(ks[6], (D_MODEL, D_MODEL), jnp.float32) * s, 'bo': jnp.zeros((D_MODEL,), jnp.float32)}
    _L3_xattn_all = _L3_xattn_setup()
    _L3_xattn_in = {k: v for k, v in _L3_xattn_all.items() if k in ('Wq', 'bq', 'Wk', 'bk', 'Wv', 'bv', 'Wo', 'bo')}
    del _L3_xattn_all

    def _L3_ffn_setup():
        import jax, jax.numpy as jnp
        import numpy as np
        E = 8
        key = jax.random.key(seed)
        k0, k1, k2, k3 = jax.random.split(key, 4)
        B, S, H, F = (4, 512, 128, 512)
        x = jax.random.normal(k0, (B, S, H), jnp.float32)
        Wr = jax.random.normal(k1, (E, H), jnp.float32) * 0.02
        W1 = jax.random.normal(k2, (E, H, F), jnp.float32) * 0.02
        b1 = jnp.zeros((E, F), jnp.float32)
        W2 = jax.random.normal(k3, (E, F, H), jnp.float32) * 0.02
        b2 = jnp.zeros((E, H), jnp.float32)
        return {'x': x, 'Wr': Wr, 'W1': W1, 'b1': b1, 'W2': W2, 'b2': b2}
    _L3_ffn_all = _L3_ffn_setup()
    _L3_ffn_in = {k: v for k, v in _L3_ffn_all.items() if k in ('Wr', 'W1', 'b1', 'W2', 'b2')}
    del _L3_ffn_all
    return {'x': x, 'ctx_1024': ctx_1024, 'ctxb_2048x32': ctxb_2048x32, 'mask_BxSxS2_bk1': mask_BxSxS2_bk1, 'L0_xattn_Wq': _L0_xattn_in['Wq'], 'L0_xattn_Wk': _L0_xattn_in['Wk'], 'L0_xattn_Wv': _L0_xattn_in['Wv'], 'L0_xattn_Wo': _L0_xattn_in['Wo'], 'L0_xattn_bo': _L0_xattn_in['bo'], 'L0_ffn_Wr': _L0_ffn_in['Wr'], 'L0_ffn_br': _L0_ffn_in['br'], 'L0_ffn_W1': _L0_ffn_in['W1'], 'L0_ffn_b1': _L0_ffn_in['b1'], 'L0_ffn_W2': _L0_ffn_in['W2'], 'L0_ffn_b2': _L0_ffn_in['b2'], 'L0_ffn_gamma': _L0_ffn_in['gamma'], 'L0_ffn_beta': _L0_ffn_in['beta'], 'L1_xattn_Wi': _L1_xattn_in['Wi'], 'L1_xattn_bi': _L1_xattn_in['bi'], 'L1_xattn_Wg': _L1_xattn_in['Wg'], 'L1_xattn_bg': _L1_xattn_in['bg'], 'L1_xattn_A': _L1_xattn_in['A'], 'L1_xattn_Bm': _L1_xattn_in['Bm'], 'L1_xattn_Wo': _L1_xattn_in['Wo'], 'L1_xattn_bo': _L1_xattn_in['bo'], 'L1_xattn_decay': _L1_xattn_in['decay'], 'L1_ffn_router_w': _L1_ffn_in['router_w'], 'L1_ffn_up_proj': _L1_ffn_in['up_proj'], 'L1_ffn_down_proj': _L1_ffn_in['down_proj'], 'L2_xattn_Wq': _L2_xattn_in['Wq'], 'L2_xattn_bq': _L2_xattn_in['bq'], 'L2_xattn_Wk': _L2_xattn_in['Wk'], 'L2_xattn_bk': _L2_xattn_in['bk'], 'L2_xattn_Wv': _L2_xattn_in['Wv'], 'L2_xattn_bv': _L2_xattn_in['bv'], 'L2_xattn_Wo': _L2_xattn_in['Wo'], 'L2_xattn_bo': _L2_xattn_in['bo'], 'L2_ffn_gate_w': _L2_ffn_in['gate_w'], 'L2_ffn_expert_bias': _L2_ffn_in['expert_bias'], 'L2_ffn_w1': _L2_ffn_in['w1'], 'L2_ffn_w2': _L2_ffn_in['w2'], 'L2_ffn_w3': _L2_ffn_in['w3'], 'L3_xattn_Wq': _L3_xattn_in['Wq'], 'L3_xattn_bq': _L3_xattn_in['bq'], 'L3_xattn_Wk': _L3_xattn_in['Wk'], 'L3_xattn_bk': _L3_xattn_in['bk'], 'L3_xattn_Wv': _L3_xattn_in['Wv'], 'L3_xattn_bv': _L3_xattn_in['bv'], 'L3_xattn_Wo': _L3_xattn_in['Wo'], 'L3_xattn_bo': _L3_xattn_in['bo'], 'L3_ffn_Wr': _L3_ffn_in['Wr'], 'L3_ffn_W1': _L3_ffn_in['W1'], 'L3_ffn_b1': _L3_ffn_in['b1'], 'L3_ffn_W2': _L3_ffn_in['W2'], 'L3_ffn_b2': _L3_ffn_in['b2']}

def reference(x, ctx_1024, ctxb_2048x32, mask_BxSxS2_bk1, L0_xattn_Wq, L0_xattn_Wk, L0_xattn_Wv, L0_xattn_Wo, L0_xattn_bo, L0_ffn_Wr, L0_ffn_br, L0_ffn_W1, L0_ffn_b1, L0_ffn_W2, L0_ffn_b2, L0_ffn_gamma, L0_ffn_beta, L1_xattn_Wi, L1_xattn_bi, L1_xattn_Wg, L1_xattn_bg, L1_xattn_A, L1_xattn_Bm, L1_xattn_Wo, L1_xattn_bo, L1_xattn_decay, L1_ffn_router_w, L1_ffn_up_proj, L1_ffn_down_proj, L2_xattn_Wq, L2_xattn_bq, L2_xattn_Wk, L2_xattn_bk, L2_xattn_Wv, L2_xattn_bv, L2_xattn_Wo, L2_xattn_bo, L2_ffn_gate_w, L2_ffn_expert_bias, L2_ffn_w1, L2_ffn_w2, L2_ffn_w3, L3_xattn_Wq, L3_xattn_bq, L3_xattn_Wk, L3_xattn_bk, L3_xattn_Wv, L3_xattn_bv, L3_xattn_Wo, L3_xattn_bo, L3_ffn_Wr, L3_ffn_W1, L3_ffn_b1, L3_ffn_W2, L3_ffn_b2):
    import jax
    import jax.numpy as jnp

    def _L0_xattn_ref(q, k, v, mask, Wq, Wk, Wv, Wo, bo):
        import jax, jax.numpy as jnp
        import numpy as np
        DIM = 128
        HEADS = 16
        DIM_HEAD = 64
        INNER = HEADS * DIM_HEAD
        B, N = (2, 256)
        h, d = (HEADS, DIM_HEAD)
        scale = d ** (-0.5)
        b, n, _ = q.shape

        def heads_split(x):
            return x.reshape(b, -1, h, d).transpose(0, 2, 1, 3)
        qh = heads_split(q @ Wq)
        kh = heads_split(k @ Wk)
        vh = heads_split(v @ Wv)
        dots = jnp.einsum('bhid,bhjd->bhij', qh, kh) * scale
        mask_value = -jnp.finfo(dots.dtype).max
        dots = jnp.where(mask[:, None, :, :], mask_value, dots)
        attn = jax.nn.softmax(dots, axis=-1)
        out = jnp.einsum('bhij,bhjd->bhid', attn, vh)
        out = out.transpose(0, 2, 1, 3).reshape(b, n, h * d)
        out = out @ Wo + bo
        return out

    def _L0_ffn_ref(tgt, Wr, br, W1, b1, W2, b2, gamma, beta):
        import jax, jax.numpy as jnp
        import numpy as np
        B, S, D, F, E = (2, 256, 128, 512, 8)
        LN_EPS = 1e-05

        def _layer_norm(x, gamma, beta):
            mu = jnp.mean(x, axis=-1, keepdims=True)
            var = jnp.mean(jnp.square(x - mu), axis=-1, keepdims=True)
            return (x - mu) * jax.lax.rsqrt(var + LN_EPS) * gamma + beta
        logits = jnp.einsum('bsd,ed->bse', tgt, Wr) + br
        top_v, top_i = jax.lax.top_k(logits, 2)
        top_w = jax.nn.softmax(top_v, axis=-1)
        n_exp = logits.shape[-1]
        router_w = jnp.sum(jax.nn.one_hot(top_i, n_exp, dtype=top_w.dtype) * top_w[..., None], axis=-2)
        h = jnp.einsum('bsd,efd->bsef', tgt, W1) + b1
        h = jax.nn.relu(h)
        o = jnp.einsum('bsef,edf->bsed', h, W2) + b2
        tgt2 = jnp.einsum('bsed,bse->bsd', o, router_w)
        return _layer_norm(tgt + tgt2, gamma, beta)

    def _L1_xattn_ref(q, k, v, Wi, bi, Wg, bg, A, Bm, Wo, bo, decay):
        import jax, jax.numpy as jnp
        import numpy as np
        from jax import lax
        NUM_HEADS = 16
        DIM = 128
        BATCH = 4
        SEQ = 256
        B, S, D = q.shape
        H = decay.shape[1]
        hd = D // H
        qh = jnp.moveaxis(q.reshape(B, S, H, hd), 1, 0)
        kh = jnp.moveaxis(k.reshape(B, S, H, hd), 1, 0)
        vh = jnp.moveaxis(v.reshape(B, S, H, hd), 1, 0)

        def step(carry, xs):
            r, state = carry
            qt, kt, vt = xs
            r = decay * r + kt * vt
            retained = (qt * r).reshape(B, D)
            inp = retained @ Wi.T + bi
            gate = jax.nn.sigmoid(inp @ Wg.T + bg)
            blended = gate * state + (1.0 - gate) * inp
            state = jnp.tanh(blended @ A.T + inp @ Bm.T)
            out = state @ Wo.T + bo
            return ((r, state), out)
        r0 = jnp.zeros((B, H, hd), dtype=q.dtype)
        s0 = jnp.zeros((B, D), dtype=q.dtype)
        _, outs = lax.scan(step, (r0, s0), (qh, kh, vh))
        return jnp.moveaxis(outs, 0, 1)

    def _L1_ffn_ref(x, router_w, up_proj, down_proj):
        import jax, jax.numpy as jnp
        import numpy as np
        E = 8
        H = 128
        D = 128
        TOP_K = 2
        B, T, _ = x.shape
        xt = x.reshape(-1, H)
        N = xt.shape[0]
        logits = jnp.einsum('nh,eh->ne', xt, router_w)
        probs = jax.nn.softmax(logits, axis=-1)
        scores, expert_idx = jax.lax.top_k(probs, TOP_K)
        scores = scores / jnp.sum(scores, axis=-1, keepdims=True)
        gate = jnp.zeros((N, E), dtype=xt.dtype).at[jnp.arange(N)[:, None], expert_idx].add(scores)
        h = jnp.einsum('nh,ehd->end', xt, up_proj)
        hidden = jax.nn.silu(h[..., :D]) * h[..., D:]
        out_e = jnp.einsum('end,edh->enh', hidden, down_proj)
        out = jnp.einsum('ne,enh->nh', gate, out_e)
        return out.reshape(B, T, H)

    def _L2_xattn_ref(q_x, k_x, v_x, energy_coeffs, Wq, bq, Wk, bk, Wv, bv, Wo, bo):
        import jax, jax.numpy as jnp
        import numpy as np
        B, L, D, H, NF = (4, 256, 128, 16, 32)
        THRESHOLD = 0.1
        Bq, Lq, Dm = q_x.shape
        Dh = Dm // H
        Q = (q_x @ Wq + bq).reshape(Bq, Lq, H, Dh).transpose(0, 2, 1, 3)
        K = (k_x @ Wk + bk).reshape(Bq, -1, H, Dh).transpose(0, 2, 1, 3)
        V = (v_x @ Wv + bv).reshape(Bq, -1, H, Dh).transpose(0, 2, 1, 3)
        scores = jnp.einsum('bhqd,bhkd->bhqk', Q, K) / jnp.sqrt(jnp.float32(Dh))
        energy = jnp.abs(energy_coeffs).mean(axis=-1)
        energy = energy / (energy.max(axis=-1, keepdims=True) + 1e-08)
        gate = (energy > THRESHOLD).astype(scores.dtype) * 0.9 + 0.1
        scores = scores * gate[:, None, None, :]
        attn = jax.nn.softmax(scores, axis=-1)
        attn = jnp.nan_to_num(attn, nan=0.0)
        out = jnp.einsum('bhqk,bhkd->bhqd', attn, V)
        out = out.transpose(0, 2, 1, 3).reshape(Bq, Lq, Dm)
        return out @ Wo + bo

    def _L2_ffn_ref(x, gate_w, expert_bias, w1, w2, w3):
        import jax, jax.numpy as jnp
        import numpy as np
        TOP_K = 2
        NUM_EXPERTS = 8
        DIM = 128
        HIDDEN = 352
        BS, SLEN = (2, 128)

        def _grouped_ffn(x, w1, w2, w3, counts):
            num_experts = w1.shape[0]
            ends = jnp.cumsum(counts)
            starts = ends - counts
            t = jnp.arange(x.shape[0])
            out = jnp.zeros((x.shape[0], w2.shape[-1]), x.dtype)
            for e in range(num_experts):
                m = ((t >= starts[e]) & (t < ends[e])).astype(x.dtype)[:, None]
                xe = x * m
                h = jax.nn.silu(xe @ w1[e]) * (xe @ w3[e])
                out = out + h @ w2[e] * m
            return out
        bs, slen, dim = x.shape
        num_experts = gate_w.shape[0]
        xf = x.reshape(bs * slen, dim)
        scores = jax.nn.softmax((xf @ gate_w.T).astype(jnp.float32), axis=-1)
        _, sel = jax.lax.top_k(scores + expert_bias, TOP_K)
        top_scores = jnp.take_along_axis(scores, sel, axis=1).reshape(-1)
        sel_flat = sel.reshape(-1)
        counts = jnp.zeros((num_experts,), jnp.int32).at[sel_flat].add(1)
        order = jnp.argsort(sel_flat, stable=True)
        top_scores_sorted = top_scores[order]
        token_idx = order // TOP_K
        routed = xf[token_idx] * top_scores_sorted[:, None].astype(xf.dtype)
        routed_out = _grouped_ffn(routed, w1, w2, w3, counts)
        out = jnp.zeros_like(xf).at[token_idx].add(routed_out)
        return out.reshape(bs, slen, dim)

    def _L3_xattn_ref(queries, keys, values, Wq, bq, Wk, bk, Wv, bv, Wo, bo):
        import jax, jax.numpy as jnp
        import numpy as np
        from math import sqrt
        D_MODEL = 128
        N_HEADS = 16
        E = D_MODEL // N_HEADS
        B, L, _ = queries.shape
        S = keys.shape[1]
        H = N_HEADS
        q = (queries @ Wq + bq).reshape(B, L, H, E)
        k = (keys @ Wk + bk).reshape(B, S, H, E)
        v = (values @ Wv + bv).reshape(B, S, H, E)
        scale = 1.0 / sqrt(E)
        scores = jnp.einsum('blhe,bshe->bhls', q, k)
        A = jax.nn.softmax(scale * scores, axis=-1)
        V = jnp.einsum('bhls,bshd->blhd', A, v)
        out = V.reshape(B, L, H * E) @ Wo + bo
        return out

    def _L3_ffn_ref(x, Wr, W1, b1, W2, b2):
        import jax, jax.numpy as jnp
        import numpy as np
        E = 8
        B, S, H = x.shape
        xf = x.reshape(-1, H)
        probs = jax.nn.softmax(xf @ Wr.T, axis=-1)
        eid = E - 1
        h = jax.nn.gelu(xf @ W1[eid] + b1[eid], approximate=False)
        y = (h @ W2[eid] + b2[eid]) * probs[:, eid:eid + 1]
        return y.reshape(B, S, H)
    x = x + _L0_xattn_ref(_layernorm(x, axis=-1), ctx_1024, ctx_1024, mask_BxSxS2_bk1, L0_xattn_Wq, L0_xattn_Wk, L0_xattn_Wv, L0_xattn_Wo, L0_xattn_bo)
    x = x + _L0_ffn_ref(_layernorm(x, axis=-1), L0_ffn_Wr, L0_ffn_br, L0_ffn_W1, L0_ffn_b1, L0_ffn_W2, L0_ffn_b2, L0_ffn_gamma, L0_ffn_beta)
    x = x + _L1_xattn_ref(_layernorm(x, axis=-1), ctx_1024, ctx_1024, L1_xattn_Wi, L1_xattn_bi, L1_xattn_Wg, L1_xattn_bg, L1_xattn_A, L1_xattn_Bm, L1_xattn_Wo, L1_xattn_bo, L1_xattn_decay)
    x = x + _L1_ffn_ref(_layernorm(x, axis=-1), L1_ffn_router_w, L1_ffn_up_proj, L1_ffn_down_proj)
    x = x + _L2_xattn_ref(_layernorm(x, axis=-1), ctx_1024, ctx_1024, ctxb_2048x32, L2_xattn_Wq, L2_xattn_bq, L2_xattn_Wk, L2_xattn_bk, L2_xattn_Wv, L2_xattn_bv, L2_xattn_Wo, L2_xattn_bo)
    x = x + _L2_ffn_ref(_layernorm(x, axis=-1), L2_ffn_gate_w, L2_ffn_expert_bias, L2_ffn_w1, L2_ffn_w2, L2_ffn_w3)
    x = x + _L3_xattn_ref(_layernorm(x, axis=-1), ctx_1024, ctx_1024, L3_xattn_Wq, L3_xattn_bq, L3_xattn_Wk, L3_xattn_bk, L3_xattn_Wv, L3_xattn_bv, L3_xattn_Wo, L3_xattn_bo)
    x = x + _L3_ffn_ref(_layernorm(x, axis=-1), L3_ffn_Wr, L3_ffn_W1, L3_ffn_b1, L3_ffn_W2, L3_ffn_b2)
    return x

_drawn_inputs = setup_inputs


def setup_inputs(seed=0):
    import zlib

    import numpy as np

    out = dict(_drawn_inputs(seed))
    spreads = {'L0_xattn_bo': (0.0, 0.1),
     'L0_ffn_br': (0.0, 0.1),
     'L0_ffn_b1': (0.0, 0.1),
     'L0_ffn_b2': (0.0, 0.1),
     'L0_ffn_gamma': (1.0, 0.2),
     'L0_ffn_beta': (0.0, 0.1),
     'L1_xattn_decay': (0.8999999761581421, 0.2),
     'L2_xattn_bq': (0.0, 0.784),
     'L2_xattn_bk': (0.0, 0.8),
     'L2_xattn_bv': (0.0, 0.1),
     'L2_xattn_bo': (0.0, 0.1),
     'L2_ffn_expert_bias': (0.0, 0.8),
     'L3_xattn_bq': (0.0, 0.739),
     'L3_xattn_bk': (0.0, 0.8),
     'L3_xattn_bv': (0.0, 0.1),
     'L3_xattn_bo': (0.0, 0.1),
     'L3_ffn_b1': (0.0, 0.8),
     'L3_ffn_b2': (0.0, 0.8)}
    factors = {'L0_xattn_Wk': 2.808,
     'L1_xattn_bi': 8.0,
     'L1_xattn_bg': 8.0,
     'L2_ffn_gate_w': 8.0,
     'L2_ffn_w1': 8.0,
     'L2_ffn_w2': 8.0,
     'L2_ffn_w3': 8.0,
     'L3_ffn_Wr': 8.0,
     'L3_ffn_W1': 8.0,
     'L3_ffn_W2': 8.0}
    for name, (base, spread) in spreads.items():
        noise = np.random.default_rng([zlib.crc32(name.encode()), seed]).standard_normal(out[name].shape)
        drawn = base * np.exp(spread * noise) if base else spread * noise
        out[name] = jnp.asarray(drawn.astype(out[name].dtype))
    for name, factor in factors.items():
        out[name] = (out[name] * factor).astype(out[name].dtype)
    return out
```

```python
from contextlib import ExitStack

import concourse.bass as bass
from concourse import mybir

ALU = mybir.AluOpType
ACT = mybir.ActivationFunctionType
AX = mybir.AxisListType
F32 = mybir.dt.float32
F32R = mybir.dt.float32r
BF16 = mybir.dt.bfloat16
U8 = mybir.dt.uint8
I32 = mybir.dt.int32
ds = bass.ds

B, S, D = 16, 128, 128
T = B * S
E = 8
CH = 512
NCH = T // CH
TPC = CH // S
BANK = 512
EPS = 1e-5
BIG = 1e30
NB3 = 3
HEADS = 16


class Bag:
    pass



def sb(nc, ctx, name, cols, dt=F32, rows=128):
    return ctx.enter_context(nc.sbuf_tensor(name, [rows, cols], dt))


def sems(nc, prefix, names):
    bag = {}
    for n in names.split():
        bag[n] = nc.alloc_semaphore(name=prefix + n)
    return bag


def bank(g, k, n=1):
    return g.psum[:, k * BANK:(k + n) * BANK]


def product3(pe, out, w_hi, w_lo, m_hi, m_lo, first=True, last=True):
    pe.matmul(out, w_hi, m_hi, start=first, stop=False)
    pe.matmul(out, w_hi, m_lo, start=False, stop=False)
    return pe.matmul(out, w_lo, m_hi, start=False, stop=last)


def ln_alloc(nc, ctx, p):
    n = Bag()
    n.stats = sb(nc, ctx, p + "ln_stats", 6 * B)
    n.mv = sb(nc, ctx, p + "ln_mv", 2 * B)
    n.var = sb(nc, ctx, p + "ln_var", B)
    n.rstd = sb(nc, ctx, p + "ln_rstd", B)
    n.rows = sb(nc, ctx, p + "ln_rows", T)
    n.hi = sb(nc, ctx, p + "xn_hi", T, F32R)
    n.lo = sb(nc, ctx, p + "xn_lo", T, F32R)
    n.sem = sems(nc, p + "ln_", "stats_done aggr_done var_ready rstd_ready rows_ready turned hi_ready lo_ready")
    return n


def ln_rows_vector(dve, g, n, src):
    s = n.sem
    with dve.Fori(0, NCH) as c:
        for j in range(TPC):
            t = c * TPC + j
            dve.bn_stats(n.stats[:, ds(t * 6, 6)], src[:, ds(t * D, D)]).then_inc(s["stats_done"], 1)
    dve.wait_ge(s["stats_done"], B)
    for t in range(B):
        dve.bn_aggr(n.mv[:, t * 2:t * 2 + 2], n.stats[:, t * 6:t * 6 + 6]).then_inc(s["aggr_done"], 1)
    dve.wait_ge(s["aggr_done"], B)
    dve.tensor_scalar(n.var[:, :], n.mv[:, :].rearrange("p (t s) -> p t s", s=2)[:, :, 1], EPS, None,
                      ALU.add).then_inc(s["var_ready"], 1)
    dve.wait_ge(s["rstd_ready"], 1)
    with dve.Fori(0, NCH) as c:
        for j in range(TPC):
            t = c * TPC + j
            dve.tensor_scalar(n.rows[:, ds(t * D, D)], src[:, ds(t * D, D)], n.mv[:, ds(t * 2, 1)],
                              n.rstd[:, ds(t, 1)], ALU.subtract, ALU.mult).then_inc(s["rows_ready"], 1)


def ln_gpsimd(pool, g, n):
    pool.wait_ge(n.sem["var_ready"], 1)
    pool.tensor_tensor(n.rstd[:, :], n.var[:, :], g.minus_half[:, :], ALU.pow).then_inc(n.sem["rstd_ready"], 1)


def ln_tensor(pe, g, n):
    for c in range(NCH):
        pe.wait_ge(n.sem["rows_ready"], TPC * (c + 1))
        for j in range(TPC):
            t = c * TPC + j
            last = pe.transpose(bank(g, c)[:, j * D:(j + 1) * D], n.rows[:, t * D:(t + 1) * D], g.ident[:, :])
        last.then_inc(n.sem["turned"], 1)


def ln_scalar(act, g, n):
    with act.Fori(0, NCH) as c:
        act.wait_ge(n.sem["turned"], c + 1)
        act.activation(n.hi[:, ds(c * CH, CH)], g.psum[:, ds(c * BANK, CH)], ACT.Copy).then_inc(n.sem["hi_ready"], 1)


def ln_lo_vector(dve, g, n):
    with dve.Fori(0, NCH) as c:
        dve.wait_ge(n.sem["hi_ready"], c + 1)
        dve.tensor_tensor(n.lo[:, ds(c * CH, CH)], g.psum[:, ds(c * BANK, CH)],
                          n.hi[:, ds(c * CH, CH)].bitcast(F32), ALU.subtract).then_inc(n.sem["lo_ready"], 1)


def router_alloc(nc, ctx, p):
    def per_expert(name, dt=F32):
        return sb(nc, ctx, p + "rt_" + name, B * E, dt)

    def per_token(name):
        return sb(nc, ctx, p + "rt_" + name, B)

    m = Bag()
    m.raw = sb(nc, ctx, p + "rt_raw", E)
    m.w_hi = sb(nc, ctx, p + "rt_whi", E, F32R)
    m.w_lo = sb(nc, ctx, p + "rt_wlo", E, F32R)
    m.bias = sb(nc, ctx, p + "rt_bias", E)
    m.logit = per_expert("logit")
    m.score = per_expert("score")
    m.eq = per_expert("eq")
    m.oh1 = per_expert("oh1")
    m.oh2 = per_expert("oh2")
    m.rest = per_expert("rest")
    m.gate = per_expert("gate")
    m.prob = per_expert("prob")
    m.top1 = per_token("top1")
    m.top2 = per_token("top2")
    m.pick = per_token("pick")
    m.diff = per_token("diff")
    m.ratio = per_token("ratio")
    m.w1 = per_token("w1")
    m.w2 = per_token("w2")
    m.den = per_token("den")
    m.gate3 = sb(nc, ctx, p + "gate3", B * NB3 * E, BF16)
    m.gate_t = sb(nc, ctx, p + "gate_t", T, BF16, NB3 * E)
    m.wide = sb(nc, ctx, p + "gate_wide", E * T)
    m.sem = sems(nc, p + "rt_", "loaded w_hi w_lo logits step diff expd gate3 turned copied wide evac_act evac_dve")
    return m


def router_sync(sp, r, w_dram, bias_dram):
    sp.dma_start(r.raw[:, :], w_dram).then_inc(r.sem["loaded"], 16)
    if bias_dram is not None:
        sp.dma_start(r.bias[:, :], bias_dram.partition_broadcast(128)).then_inc(r.sem["loaded"], 16)


def router_split_vector(dve, r, has_bias):
    s = r.sem
    dve.wait_ge(s["loaded"], 32 if has_bias else 16)
    dve.tensor_copy(r.w_hi[:, :], r.raw[:, :]).then_inc(s["w_hi"], 1)
    dve.wait_ge(s["w_hi"], 1)
    dve.tensor_tensor(r.w_lo[:, :], r.raw[:, :], r.w_hi[:, :].bitcast(F32), ALU.subtract).then_inc(s["w_lo"], 1)


def router_tensor(pe, g, n, r, where):
    pe.wait_ge(r.sem["w_lo"], 1)
    for t in range(B):
        if t % TPC == 0:
            pe.wait_ge(n.sem["lo_ready"], t // TPC + 1)
        tok = slice(t * D, (t + 1) * D)
        last = product3(pe, bank(g, where)[:, t * E:(t + 1) * E], n.hi[:, tok], n.lo[:, tok], r.w_hi[:, :], r.w_lo[:, :])
    last.then_inc(r.sem["logits"], 1)


def by_expert(a):
    return a[:, 0:B * E].rearrange("p (t e) -> p t e", e=E)


def over_experts(a):
    return a[:, 0:B].unsqueeze(2).to_broadcast([128, B, E])


def over_tokens(a):
    return a[:, 0:E].unsqueeze(1).to_broadcast([128, B, E])


def router_pick(link, dve, g, r, score, top, onehot):
    link(dve.tensor_reduce(top[:, :], by_expert(score), AX.X, ALU.max))
    link(dve.tensor_tensor(by_expert(r.eq), by_expert(score), over_experts(top), ALU.is_ge))
    link(dve.tensor_tensor(by_expert(r.eq), by_expert(r.eq), over_tokens(g.priority), ALU.mult))
    link(dve.tensor_reduce(r.pick[:, :], by_expert(r.eq), AX.X, ALU.max))
    link(dve.tensor_tensor(by_expert(onehot), by_expert(r.eq), over_experts(r.pick), ALU.is_equal))


def router_vector(dve, g, r, kind, where):
    s = r.sem
    count = [0]

    def link(ins):
        count[0] += 1
        ins.then_inc(s["step"], 1)
        dve.wait_ge(s["step"], count[0])

    dve.wait_ge(s["logits"], 1)
    psum_logits = by_expert(bank(g, where))
    if kind == "pair_bias":
        link(dve.tensor_tensor(by_expert(r.logit), psum_logits, over_tokens(r.bias), ALU.add))
    else:
        link(dve.tensor_copy(r.logit[:, :], bank(g, where)[:, 0:B * E]))
    score = r.logit
    if kind in ("bias", "all"):
        link(dve.tensor_reduce(r.top1[:, :], by_expert(r.logit), AX.X, ALU.max))
        dve.tensor_tensor(by_expert(r.rest), by_expert(r.logit), over_experts(r.top1),
                          ALU.subtract).then_inc(s["diff"], 1)
        dve.wait_ge(s["expd"], 1)
        link(dve.tensor_reduce(r.den[:, :], by_expert(r.prob), AX.X, ALU.add))
        link(dve.reciprocal(r.w1[:, :], r.den[:, :]))
        link(dve.tensor_tensor(by_expert(r.prob), by_expert(r.prob), over_experts(r.w1), ALU.mult))
        if kind == "bias":
            link(dve.tensor_tensor(by_expert(r.score), by_expert(r.prob), over_tokens(r.bias), ALU.add))
            score = r.score
    if kind == "all":
        link(dve.tensor_copy(r.gate[:, :], r.prob[:, :]))
        split_gate(link, dve, r)
        return
    router_pick(link, dve, g, r, score, r.top1, r.oh1)
    link(dve.scalar_tensor_tensor(out=r.rest[:, :], in0=r.oh1[:, :], scalar=-BIG, in1=score[:, :],
                                  op0=ALU.mult, op1=ALU.add))
    router_pick(link, dve, g, r, r.rest, r.top2, r.oh2)
    if kind == "bias":
        link(dve.tensor_tensor(r.oh1[:, :], r.oh1[:, :], r.oh2[:, :], ALU.add))
        link(dve.tensor_tensor(r.gate[:, :], r.oh1[:, :], r.prob[:, :], ALU.mult))
    else:
        dve.tensor_tensor(r.diff[:, :], r.top2[:, :], r.top1[:, :], ALU.subtract).then_inc(s["diff"], 1)
        dve.wait_ge(s["expd"], 1)
        link(dve.tensor_scalar(r.den[:, :], r.ratio[:, :], 1.0, None, ALU.add))
        link(dve.reciprocal(r.w1[:, :], r.den[:, :]))
        link(dve.tensor_tensor(r.w2[:, :], r.w1[:, :], r.ratio[:, :], ALU.mult))
        link(dve.tensor_tensor(by_expert(r.oh1), by_expert(r.oh1), over_experts(r.w1), ALU.mult))
        link(dve.tensor_tensor(by_expert(r.oh2), by_expert(r.oh2), over_experts(r.w2), ALU.mult))
        link(dve.tensor_tensor(r.gate[:, :], r.oh1[:, :], r.oh2[:, :], ALU.add))
    split_gate(link, dve, r)


def split_gate(link, dve, r):
    parts = r.gate3[:, :].rearrange("p (t n e) -> p n t e", n=NB3, e=E)
    link(dve.tensor_copy(parts[:, 0], by_expert(r.gate)))
    link(dve.tensor_tensor(by_expert(r.rest), by_expert(r.gate), parts[:, 0], ALU.subtract))
    link(dve.tensor_copy(parts[:, 1], by_expert(r.rest)))
    link(dve.tensor_tensor(by_expert(r.eq), by_expert(r.rest), parts[:, 1], ALU.subtract))
    dve.tensor_copy(parts[:, 2], by_expert(r.eq)).then_inc(r.sem["gate3"], 1)


def router_scalar(act, r, kind):
    act.wait_ge(r.sem["diff"], 1)
    if kind in ("bias", "all"):
        act.activation(r.prob[:, :], r.rest[:, :], ACT.Exp).then_inc(r.sem["expd"], 1)
    else:
        act.activation(r.ratio[:, :], r.diff[:, :], ACT.Exp).then_inc(r.sem["expd"], 1)


GATE_BANKS = (5, 6)


def widen_tensor(pe, g, r, experts=range(E)):
    s = r.sem
    pe.wait_ge(s["gate3"], 1)
    for t in range(B):
        out = bank(g, GATE_BANKS[t // 8]).bitcast(BF16)[0:NB3 * E, (t % 8) * D:(t % 8 + 1) * D]
        last = pe.transpose(out, r.gate3[:, t * NB3 * E:(t + 1) * NB3 * E], g.ident_b[:, :])
    last.then_inc(s["turned"], 1)
    pe.wait_ge(s["copied"], 2)
    even, odd = [e for e in experts if e % 2 == 0], [e for e in experts if e % 2]
    for c in range(NCH):
        for k, e in enumerate(experts):
            if e % 2:
                pe.wait_ge(s["evac_dve"], c * len(odd))
            else:
                pe.wait_ge(s["evac_act"], c * len(even))
            pe.matmul(bank(g, e), g.pick_expert[:, e * 128:(e + 1) * 128], r.gate_t[:, c * CH:(c + 1) * CH],
                      start=True, stop=True).then_inc(s["wide"], 1)
    pe.wait_ge(s["evac_act"], NCH * len(even))
    pe.wait_ge(s["evac_dve"], NCH * len(odd))


def widen_copy(eng, copy, g, r, experts, odd):
    s = r.sem
    done = s["evac_dve"] if odd else s["evac_act"]
    mine = [(k, e) for k, e in enumerate(experts) if e % 2 == odd]
    if not mine:
        return
    with eng.Fori(0, NCH) as c:
        for k, e in mine:
            eng.wait_ge(s["wide"], c * len(experts) + (k + 1))
            copy(r.wide[:, ds(e * T + c * CH, CH)], bank(g, e)).then_inc(done, 1)


def widen_vector(dve, g, r, experts=range(E)):
    s = r.sem
    dve.wait_ge(s["turned"], 1)
    for k in range(2):
        dve.tensor_copy(r.gate_t[:, k * 8 * D:(k + 1) * 8 * D],
                        bank(g, GATE_BANKS[k]).bitcast(BF16)[0:NB3 * E, :]).then_inc(s["copied"], 1)
    widen_copy(dve, dve.tensor_copy, g, r, experts, 1)


def widen_scalar(act, g, r, experts=range(E)):
    widen_copy(act, act.copy, g, r, experts, 0)


def add_alloc(nc, ctx, p):
    a = Bag()
    a.sem = sems(nc, p + "add_", "turned added")
    return a


def add_tensor(pe, g, a, acc, ready):
    for sem, count in ready:
        pe.wait_ge(sem, count)
    for c in range(NCH):
        for j in range(TPC):
            t = c * TPC + j
            last = pe.transpose(bank(g, c)[:, j * D:(j + 1) * D], acc[:, t * D:(t + 1) * D], g.ident[:, :])
        last.then_inc(a.sem["turned"], 1)


def add_vector(dve, g, a, out, base):
    with dve.Fori(0, NCH) as c:
        dve.wait_ge(a.sem["turned"], c + 1)
        dve.tensor_tensor(out[:, ds(c * CH, CH)], g.psum[:, ds(c * BANK, CH)], base[:, ds(c * CH, CH)],
                          ALU.add).then_inc(a.sem["added"], 1)
def steps_of(ep, n_experts):
    return [(ep, i, c) for i in range(min(2, n_experts)) for c in range(NCH)]


def next_step(ep, i, c):
    return (ep, i, c + 1) if c < NCH - 1 else (ep, 1, 0) if i == 0 else (ep + 1, 0, 0)


def index(ep, i, c):
    return ep * (2 * NCH) + (i * NCH + c)


def turn(ep, i, c):
    return ep * NCH + (i * (NCH // 2) + c // 2)


def over_experts_loop(eng, n_experts, body):
    if n_experts > 2:
        with eng.Fori(0, n_experts // 2 - 1) as ep:
            body(ep, False)
        body(n_experts // 2 - 1, True)
    else:
        body(0, True)


def load_expert_weights(sp, s, raw, dram, n_experts):
    def load(ep, i):
        sp.wait_ge(s[f"w_lo{i}"], ep)
        sp.dma_start(raw[i][:, :], dram[ds(ep * 2 + i, 1)].rearrange("o p n -> p (o n)")).then_inc(s[f"raw{i}"], 16)

    if n_experts == 1:
        load(0, 0)
        return
    with sp.Fori(0, n_experts // 2) as ep:
        for i in range(2):
            load(ep, i)


def split_weights_hi(dve, s, w_hi, raw, ep, i, bias=None):
    dve.wait_ge(s[f"raw{i}"], 16 * (ep + 1))
    if i or not isinstance(ep, int) or ep:
        dve.wait_ge(s["down1"], ep * NCH + (2 * i - 2))
    words = w_hi[i].shape[1]
    if bias is not None:
        if i or not isinstance(ep, int) or ep:
            dve.wait_ge(s["part1"], ep * NCH + (2 * i - 2))
        dve.tensor_copy(bias[i][:, :], raw[i][:, words:]).then_inc(s[f"bias{i}"], 1)
    dve.tensor_copy(w_hi[i][:, :], raw[i][:, 0:words]).then_inc(s[f"w_hi{i}"], 1)


def split_weights_lo(pool, s, w_hi, w_lo, raw, ep, i):
    pool.wait_ge(s[f"w_hi{i}"], ep + 1)
    pool.tensor_tensor(w_lo[i][:, :], raw[i][:, 0:w_hi[i].shape[1]], w_hi[i][:, :].bitcast(F32),
                       ALU.subtract).then_inc(s[f"w_lo{i}"], 1)


FB = 4
W_DENSE = 2 * FB * D
OUT0 = 4


def dense_alloc(nc, ctx, p, n_experts):
    two = range(2)
    m = Bag()
    m.raw = [sb(nc, ctx, f"{p}raw{i}", W_DENSE + FB + 1) for i in two]
    m.w_hi = [sb(nc, ctx, f"{p}w_hi{i}", W_DENSE, F32R) for i in two]
    m.w_lo = [sb(nc, ctx, f"{p}w_lo{i}", W_DENSE, F32R) for i in two]
    m.h = [sb(nc, ctx, f"{p}h{i}", FB * CH) for i in two]
    m.h_hi = [sb(nc, ctx, f"{p}h_hi{i}", FB * CH, F32R) for i in two]
    m.h_lo = [sb(nc, ctx, f"{p}h_lo{i}", FB * CH, F32R) for i in two]
    m.part = [sb(nc, ctx, f"{p}part{i}", CH) for i in two]
    m.acc = sb(nc, ctx, p + "acc", T)
    m.bias = [sb(nc, ctx, f"{p}bias{i}", FB + 1) for i in two]
    m.sem = sems(nc, p, "bias0 bias1 raw0 raw1 w_hi0 w_hi1 w_lo0 w_lo1 up act0 act1 act2 act3 "
                             "h_hi h_lo0 h_lo1 down0 down1 part0 part1 zeroed acc0 acc1")
    return m


def dense_tensor(pe, g, n, m, n_experts):
    s = m.sem

    def up(ep, i, c):
        pe.wait_ge(s[f"w_lo{i}"], ep + 1)
        for f in range(FB):
            pe.wait_ge(s[f"act{f}"], index(ep, i, c))
            w = slice(f * D, (f + 1) * D)
            tok = slice(c * CH, (c + 1) * CH)
            product3(pe, bank(g, f), m.w_hi[i][:, w], m.w_lo[i][:, w], n.hi[:, tok], n.lo[:, tok]).then_inc(s["up"], 1)

    def down(ep, i, c):
        q = c % 2
        pe.wait_ge(s[f"part{q}"], turn(ep, i, c))
        for f in range(FB):
            pe.wait_ge(s[f"h_lo{q}"], turn(ep, i, c) * FB + (f + 1))
            w = slice((FB + f) * D, (FB + f + 1) * D)
            h = slice(f * CH, (f + 1) * CH)
            last = product3(pe, bank(g, OUT0 + q), m.w_hi[i][:, w], m.w_lo[i][:, w], m.h_hi[q][:, h],
                            m.h_lo[q][:, h], first=f == 0, last=f == FB - 1)
        last.then_inc(s[f"down{q}"], 1)

    def body(ep, last):
        steps = steps_of(ep, n_experts)
        for step in steps:
            if not (last and step == steps[-1]):
                up(*next_step(*step))
            down(*step)

    up(0, 0, 0)
    over_experts_loop(pe, n_experts, body)


def dense_scalar(act, g, m, func, n_experts):
    s = m.sem

    def activate(ep, i, c, f):
        q = c % 2
        act.wait_ge(s["up"], index(ep, i, c) * FB + (f + 1))
        if f == 0:
            act.wait_ge(s[f"h_lo{q}"], turn(ep, i, c) * FB)
        if f == 0 and c == 0:
            act.wait_ge(s[f"bias{i}"], ep + 1)
        act.activation(m.h[q][:, f * CH:(f + 1) * CH], bank(g, f), func,
                       bias=m.bias[i][:, f:f + 1]).then_inc(s[f"act{f}"], 1)

    def split_hi(ep, i, c, f):
        q = c % 2
        if f == 0:
            act.wait_ge(s[f"down{q}"], turn(ep, i, c))
        act.wait_ge(s[f"act{f}"], index(ep, i, c) + 1)
        h = slice(f * CH, (f + 1) * CH)
        act.activation(m.h_hi[q][:, h], m.h[q][:, h], ACT.Copy).then_inc(s["h_hi"], 1)

    def body(ep, last):
        for step in steps_of(ep, n_experts):
            activate(*step, 0)
            for f in range(1, FB):
                activate(*step, f)
                split_hi(*step, f - 1)
            split_hi(*step, FB - 1)

    over_experts_loop(act, n_experts, body)


def dense_vector(dve, g, r, m, n_experts, first_gate):
    s = m.sem

    def split_lo(ep, i, c):
        q = c % 2
        for f in range(FB):
            dve.wait_ge(s["h_hi"], index(ep, i, c) * FB + (f + 1))
            h = slice(f * CH, (f + 1) * CH)
            dve.tensor_tensor(m.h_lo[q][:, h], m.h[q][:, h], m.h_hi[q][:, h].bitcast(F32),
                              ALU.subtract).then_inc(s[f"h_lo{q}"], 1)

    def gated(ep, i, c):
        q = c % 2
        if c == 0:
            dve.wait_ge(s[f"bias{i}"], ep + 1)
        dve.wait_ge(s[f"down{q}"], turn(ep, i, c) + 1)
        dve.wait_ge(s[f"acc{q}"], turn(ep, i, c))
        dve.scalar_tensor_tensor(out=m.part[q][:, :], in0=bank(g, OUT0 + q), scalar=m.bias[i][:, FB:FB + 1],
                                 in1=r.wide[:, ds(ep * (2 * T) + (i + first_gate) * T + c * CH, CH)],
                                 op0=ALU.add, op1=ALU.mult).then_inc(s[f"part{q}"], 1)

    def body(ep, last):
        steps = steps_of(ep, n_experts)
        for step in steps:
            _, i, c = step
            if not (last and step == steps[-1]):
                split_lo(*next_step(*step))
            if c == 1 and i == 0 and n_experts > 1:
                split_weights_hi(dve, s, m.w_hi, m.raw, ep, 1, m.bias)
            if c == 1 and i == 1 and not last:
                split_weights_hi(dve, s, m.w_hi, m.raw, ep + 1, 0, m.bias)
            gated(*step)

    split_lo(0, 0, 0)
    over_experts_loop(dve, n_experts, body)


def dense_gpsimd(pool, m, n_experts):
    s = m.sem

    def accumulate(ep, i, c):
        q = c % 2
        pool.wait_ge(s[f"part{q}"], turn(ep, i, c) + 1)
        pool.wait_ge(s[f"acc{q}"], turn(ep, i, c))
        tok = slice(c * CH, (c + 1) * CH)
        pool.tensor_tensor(m.acc[:, tok], m.acc[:, tok], m.part[q][:, :], ALU.add).then_inc(s[f"acc{q}"], 1)

    def body(ep, last):
        for step in steps_of(ep, n_experts):
            _, i, c = step
            if c == 1 and i == 0 and n_experts > 1:
                split_weights_lo(pool, s, m.w_hi, m.w_lo, m.raw, ep, 1)
            if c == 1 and i == 1 and not last:
                split_weights_lo(pool, s, m.w_hi, m.w_lo, m.raw, ep + 1, 0)
            accumulate(*step)

    pool.memset(m.acc[:, :], 0.0).then_inc(s["zeroed"], 1)
    pool.wait_ge(s["zeroed"], 1)
    split_weights_lo(pool, s, m.w_hi, m.w_lo, m.raw, 0, 0)
    over_experts_loop(pool, n_experts, body)


def stage_l0_ffn(nc, g, w):
    p = "f0_"
    with ExitStack() as ctx:
        n, r, a = ln_alloc(nc, ctx, p), router_alloc(nc, ctx, p), add_alloc(nc, ctx, p)
        m = dense_alloc(nc, ctx, p, E)
        gamma, beta = sb(nc, ctx, p + "gamma", D), sb(nc, ctx, p + "beta", D)
        s = sems(nc, p, "affine z_stats z_aggr z_var z_rstd z_step")
        z = m.raw
        block = ctx.enter_context(nc.Block())

        @block.sync
        def _(sp):
            router_sync(sp, r, w["f0_wr"], w["f0_br"])
            sp.dma_start(gamma[:, :], w["f0_gamma"].partition_broadcast(128)).then_inc(s["affine"], 16)
            sp.dma_start(beta[:, :], w["f0_beta"].partition_broadcast(128)).then_inc(s["affine"], 16)
            load_expert_weights(sp, m.sem, m.raw, w["f0_w"], E)

        @block.gpsimd
        def _(pool):
            ln_gpsimd(pool, g, n)
            dense_gpsimd(pool, m, E)
            pool.wait_ge(s["z_var"], 1)
            pool.tensor_tensor(n.rstd[:, :], n.var[:, :], g.minus_half[:, :], ALU.pow).then_inc(s["z_rstd"], 1)

        @block.tensor
        def _(pe):
            ln_tensor(pe, g, n)
            router_tensor(pe, g, n, r, 4)
            widen_tensor(pe, g, r)
            dense_tensor(pe, g, n, m, E)
            add_tensor(pe, g, a, m.acc, [(m.sem["acc0"], 2 * E), (m.sem["acc1"], 2 * E)])

        @block.scalar
        def _(act):
            ln_scalar(act, g, n)
            router_scalar(act, r, "pair_bias")
            widen_scalar(act, g, r)
            dense_scalar(act, g, m, ACT.Relu, E)

        @block.vector
        def _(dve):
            router_split_vector(dve, r, True)
            ln_rows_vector(dve, g, n, g.x)
            ln_lo_vector(dve, g, n)
            router_vector(dve, g, r, "pair_bias", 4)
            widen_vector(dve, g, r)
            split_weights_hi(dve, m.sem, m.w_hi, m.raw, 0, 0, m.bias)
            dve.wait_ge(m.sem["bias0"], 1)
            dense_vector(dve, g, r, m, E, 0)
            add_vector(dve, g, a, n.rows, n.rows)
            dve.wait_ge(a.sem["added"], NCH)
            with dve.Fori(0, B) as t:
                dve.bn_stats(n.stats[:, ds(t * 6, 6)], n.rows[:, ds(t * D, D)]).then_inc(s["z_stats"], 1)
            dve.wait_ge(s["z_stats"], B)
            for t in range(B):
                dve.bn_aggr(n.mv[:, t * 2:t * 2 + 2], n.stats[:, t * 6:t * 6 + 6]).then_inc(s["z_aggr"], 1)
            dve.wait_ge(s["z_aggr"], B)
            dve.tensor_scalar(n.var[:, :], n.mv[:, :].rearrange("p (t s) -> p t s", s=2)[:, :, 1], EPS, None,
                              ALU.add).then_inc(s["z_var"], 1)
            dve.wait_ge(s["z_rstd"], 1)
            with dve.Fori(0, B) as t:
                dve.tensor_scalar(n.rows[:, ds(t * D, D)], n.rows[:, ds(t * D, D)], n.mv[:, ds(t * 2, 1)],
                                  n.rstd[:, ds(t, 1)], ALU.subtract, ALU.mult).then_inc(s["z_step"], 1)
            dve.wait_ge(s["z_step"], B)
            dve.wait_ge(s["affine"], 32)
            rows = n.rows[:, :].rearrange("p (t d) -> p t d", d=D)
            dve.tensor_tensor(rows, rows, gamma[:, :].unsqueeze(1).to_broadcast([128, B, D]), ALU.mult).then_inc(s["z_step"], 1)
            dve.wait_ge(s["z_step"], B + 1)
            dve.tensor_tensor(rows, rows, beta[:, :].unsqueeze(1).to_broadcast([128, B, D]), ALU.add).then_inc(s["z_step"], 1)
            dve.wait_ge(s["z_step"], B + 2)
            dve.tensor_tensor(g.x[:, :], g.x[:, :], n.rows[:, :], ALU.add).then_inc(s["z_step"], 1)
            dve.wait_ge(s["z_step"], B + 3)


def stage_l3_ffn(nc, g, w):
    p = "f3_"
    with ExitStack() as ctx:
        n, r, a = ln_alloc(nc, ctx, p), router_alloc(nc, ctx, p), add_alloc(nc, ctx, p)
        m = dense_alloc(nc, ctx, p, 1)
        block = ctx.enter_context(nc.Block())

        @block.sync
        def _(sp):
            router_sync(sp, r, w["f3_wr"], None)
            load_expert_weights(sp, m.sem, m.raw, w["f3_w"], 1)

        @block.gpsimd
        def _(pool):
            ln_gpsimd(pool, g, n)
            dense_gpsimd(pool, m, 1)

        @block.tensor
        def _(pe):
            ln_tensor(pe, g, n)
            router_tensor(pe, g, n, r, 4)
            widen_tensor(pe, g, r, [E - 1])
            dense_tensor(pe, g, n, m, 1)
            add_tensor(pe, g, a, m.acc, [(m.sem["acc0"], 2), (m.sem["acc1"], 2)])

        @block.scalar
        def _(act):
            ln_scalar(act, g, n)
            router_scalar(act, r, "all")
            widen_scalar(act, g, r, [E - 1])
            dense_scalar(act, g, m, ACT.Gelu, 1)

        @block.vector
        def _(dve):
            router_split_vector(dve, r, False)
            ln_rows_vector(dve, g, n, g.x)
            ln_lo_vector(dve, g, n)
            router_vector(dve, g, r, "all", 4)
            widen_vector(dve, g, r, [E - 1])
            split_weights_hi(dve, m.sem, m.w_hi, m.raw, 0, 0, m.bias)
            dense_vector(dve, g, r, m, 1, E - 1)
            add_vector(dve, g, a, g.x, g.x)
            dve.wait_ge(a.sem["added"], NCH)


ACC0 = 4


def gated_alloc(nc, ctx, p, hidden, scale_input):
    two = range(2)
    sizes = [min(128, hidden - k) for k in range(0, hidden, 128)]
    nb = len(sizes)
    words = 2 * hidden + nb * D
    m = Bag()
    m.sizes = sizes
    m.nb = nb
    m.hidden = hidden
    m.scale_input = scale_input
    m.raw = [sb(nc, ctx, f"{p}raw{i}", words) for i in two]
    m.w_hi = [sb(nc, ctx, f"{p}w_hi{i}", words, F32R) for i in two]
    m.w_lo = [sb(nc, ctx, f"{p}w_lo{i}", words, F32R) for i in two]
    m.silu = [sb(nc, ctx, f"{p}silu{i}", CH) for i in two]
    m.ungated = [sb(nc, ctx, f"{p}ungated{i}", CH) for i in two]
    m.h = [sb(nc, ctx, f"{p}h{i}", nb * CH) for i in two]
    m.h_hi = [sb(nc, ctx, f"{p}h_hi{i}", nb * CH, F32R) for i in two]
    m.h_lo = [sb(nc, ctx, f"{p}h_lo{i}", nb * CH, F32R) for i in two]
    m.x = [sb(nc, ctx, f"{p}xg{i}", CH) for i in two]
    m.x_hi = [sb(nc, ctx, f"{p}xg_hi{i}", CH, F32R) for i in two]
    m.x_lo = [sb(nc, ctx, f"{p}xg_lo{i}", CH, F32R) for i in two]
    m.x_all = sb(nc, ctx, p + "x_all", T) if scale_input else None
    m.acc = sb(nc, ctx, p + "acc", T)
    m.sem = sems(nc, p, "raw0 raw1 w_hi0 w_hi1 w_lo0 w_lo1 up silu used0 used1 gated0 gated1 h_hi h_lo0 h_lo1 "
                             "down0 down1 x_all x0 x1 x_hi0 x_hi1 x_lo0 x_lo1 acc")
    return m


def gated_tensor(pe, g, n, m):
    s, nb = m.sem, m.nb

    def up(ep, i, c):
        pe.wait_ge(s[f"w_lo{i}"], ep + 1)
        q = c % 2
        if m.scale_input:
            pe.wait_ge(s[f"x_lo{q}"], turn(ep, i, c) + 1)
            x_hi, x_lo = m.x_hi[q][:, :], m.x_lo[q][:, :]
        else:
            x_hi, x_lo = n.hi[:, c * CH:(c + 1) * CH], n.lo[:, c * CH:(c + 1) * CH]
        for j, size in enumerate(m.sizes):
            k = (i * NCH + c) * nb + j
            pe.wait_ge(s[f"used{k % 2}"], ep * (nb * NCH) + k // 2)
            for half in range(2):
                cols = slice(half * m.hidden + j * 128, half * m.hidden + j * 128 + size)
                last = product3(pe, bank(g, 2 * (k % 2) + half)[0:size, :], m.w_hi[i][:, cols], m.w_lo[i][:, cols],
                                x_hi, x_lo)
            last.then_inc(s["up"], 1)

    def down(ep, i, c):
        q = c % 2
        for j, size in enumerate(m.sizes):
            pe.wait_ge(s[f"h_lo{q}"], turn(ep, i, c) * nb + (j + 1))
            cols = slice(2 * m.hidden + j * D, 2 * m.hidden + (j + 1) * D)
            h = slice(j * CH, (j + 1) * CH)
            for k, (x, y) in enumerate(((m.w_hi, m.h_hi), (m.w_hi, m.h_lo), (m.w_lo, m.h_hi))):
                last = pe.matmul(bank(g, ACC0 + c), x[i][0:size, cols], y[q][0:size, h], start=False, stop=False,
                                 skip_group_check=True)
        last.then_inc(s[f"down{q}"], 1)

    def body(ep, last):
        steps = steps_of(ep, E)
        for step in steps:
            if not (last and step == steps[-1]):
                up(*next_step(*step))
            down(*step)

    for c in range(NCH):
        pe.matmul(bank(g, ACC0 + c), g.zeros_b[0:32, :], g.zeros_wide[0:32, :], start=True, stop=False, skip_group_check=True)
    up(0, 0, 0)
    over_experts_loop(pe, E, body)


def gated_scalar(act, g, m):
    s, nb = m.sem, m.nb

    def silu(ep, i, c, j):
        k = (i * NCH + c) * nb + j
        pair = ep * (2 * nb * NCH) + k
        size = m.sizes[j]
        act.wait_ge(s["up"], pair + 1)
        act.wait_ge(s[f"used{k % 2}"], ep * (nb * NCH) + k // 2)
        act.activation(m.silu[k % 2][0:size, :], bank(g, 2 * (k % 2))[0:size, :], ACT.Silu).then_inc(s["silu"], 1)

    def split_hi(ep, i, c, j):
        q = c % 2
        size, h = m.sizes[j], slice(j * CH, (j + 1) * CH)
        if j == 0:
            act.wait_ge(s[f"down{q}"], turn(ep, i, c))
        k = (i * NCH + c) * nb + j
        if m.scale_input:
            act.wait_ge(s[f"used{k % 2}"], ep * (nb * NCH) + (k // 2 + 1))
        else:
            act.wait_ge(s[f"gated{q}"], turn(ep, i, c) + 1)
        act.activation(m.h_hi[q][0:size, h], m.h[q][0:size, h], ACT.Copy).then_inc(s["h_hi"], 1)

    def input_hi(ep, i, c):
        q = c % 2
        act.wait_ge(s[f"x{q}"], turn(ep, i, c) + 1)
        if i or c or not isinstance(ep, int) or ep:
            act.wait_ge(s["up"], index(ep, i, c) * nb - nb)
        act.activation(m.x_hi[q][:, :], m.x[q][:, :], ACT.Copy).then_inc(s[f"x_hi{q}"], 1)

    def body(ep, last):
        steps = steps_of(ep, E)
        for step in steps:
            for j in range(nb):
                silu(*step, j)
                if j == 0 and m.scale_input and not (last and step == steps[-1]):
                    input_hi(*next_step(*step))
                if j > 0:
                    split_hi(*step, j - 1)
            split_hi(*step, nb - 1)

    if m.scale_input:
        input_hi(0, 0, 0)
    over_experts_loop(act, E, body)
    act.wait_ge(s["down0"], 2 * E)
    act.wait_ge(s["down1"], 2 * E)
    for c in (0, 2):
        act.activation(m.acc[:, c * CH:(c + 1) * CH], bank(g, ACC0 + c), ACT.Copy).then_inc(s["acc"], 1)


def gated_vector(dve, g, m):
    s, nb = m.sem, m.nb

    def multiply(ep, i, c, j):
        q, k = c % 2, (i * NCH + c) * nb + j
        size, h = m.sizes[j], slice(j * CH, (j + 1) * CH)
        dve.wait_ge(s["silu"], ep * (2 * nb * NCH) + k + 1)
        if m.scale_input:
            dve.wait_ge(s[f"h_lo{q}"], turn(ep, i, c) * nb)
            out = m.h[q][0:size, h]
        else:
            dve.wait_ge(s[f"gated{q}"], turn(ep, i, c))
            out = m.ungated[q][:, :]
        dve.tensor_tensor(out, m.silu[k % 2][0:size, :], bank(g, 2 * (k % 2) + 1)[0:size, :],
                          ALU.mult).then_inc(s[f"used{k % 2}"], 1)

    def split_lo(ep, i, c, j):
        q = c % 2
        size, h = m.sizes[j], slice(j * CH, (j + 1) * CH)
        dve.wait_ge(s["h_hi"], index(ep, i, c) * nb + (j + 1))
        dve.tensor_tensor(m.h_lo[q][0:size, h], m.h[q][0:size, h], m.h_hi[q][0:size, h].bitcast(F32),
                          ALU.subtract).then_inc(s[f"h_lo{q}"], 1)

    def body(ep, last):
        for step in steps_of(ep, E):
            _, i, c = step
            for j in range(nb):
                multiply(*step, j)
                if j > 0:
                    split_lo(*step, j - 1)
            if c == 1 and i == 0:
                split_weights_hi(dve, s, m.w_hi, m.raw, ep, 1)
            if c == 1 and i == 1 and not last:
                split_weights_hi(dve, s, m.w_hi, m.raw, ep + 1, 0)
            split_lo(*step, nb - 1)

    over_experts_loop(dve, E, body)
    dve.wait_ge(s["down0"], 2 * E)
    dve.wait_ge(s["down1"], 2 * E)
    for c in (1, 3):
        dve.tensor_copy(m.acc[:, c * CH:(c + 1) * CH], bank(g, ACC0 + c)).then_inc(s["acc"], 1)


def gated_gpsimd(pool, g, n, r, m):
    s, nb = m.sem, m.nb

    def scale_input(ep, i, c):
        q = c % 2
        pool.wait_ge(s[f"x_lo{q}"], turn(ep, i, c))
        pool.tensor_tensor(m.x[q][:, :], m.x_all[:, c * CH:(c + 1) * CH], r.wide[:, ds(ep * (2 * T) + i * T + c * CH, CH)],
                           ALU.mult).then_inc(s[f"x{q}"], 1)

    def input_lo(ep, i, c):
        q = c % 2
        pool.wait_ge(s[f"x_hi{q}"], turn(ep, i, c) + 1)
        pool.tensor_tensor(m.x_lo[q][:, :], m.x[q][:, :], m.x_hi[q][:, :].bitcast(F32),
                           ALU.subtract).then_inc(s[f"x_lo{q}"], 1)

    def gate(ep, i, c):
        q = c % 2
        pool.wait_ge(s[f"used{q}"], turn(ep, i, c) + 1)
        pool.wait_ge(s[f"h_lo{q}"], turn(ep, i, c))
        pool.tensor_tensor(m.h[q][:, :], m.ungated[q][:, :], r.wide[:, ds(ep * (2 * T) + i * T + c * CH, CH)],
                           ALU.mult).then_inc(s[f"gated{q}"], 1)

    def body(ep, last):
        steps = steps_of(ep, E)
        for step in steps:
            _, i, c = step
            if m.scale_input:
                if not (last and step == steps[-1]):
                    scale_input(*next_step(*step))
                    input_lo(*next_step(*step))
            else:
                gate(*step)
            if c == 1 and i == 0:
                split_weights_lo(pool, s, m.w_hi, m.w_lo, m.raw, ep, 1)
            if c == 1 and i == 1 and not last:
                split_weights_lo(pool, s, m.w_hi, m.w_lo, m.raw, ep + 1, 0)

    split_weights_lo(pool, s, m.w_hi, m.w_lo, m.raw, 0, 0)
    pool.wait_ge(r.sem["evac_act"], NCH * E // 2)
    pool.wait_ge(r.sem["evac_dve"], NCH * E // 2)
    if m.scale_input:
        pool.wait_ge(n.sem["lo_ready"], NCH)
        pool.tensor_tensor(m.x_all[:, :], n.hi[:, :].bitcast(F32), n.lo[:, :].bitcast(F32), ALU.add).then_inc(s["x_all"], 1)
        pool.wait_ge(s["x_all"], 1)
        scale_input(0, 0, 0)
        input_lo(0, 0, 0)
    over_experts_loop(pool, E, body)


def stage_gated(nc, g, w, p, hidden, kind):
    with ExitStack() as ctx:
        n, r, a = ln_alloc(nc, ctx, p), router_alloc(nc, ctx, p), add_alloc(nc, ctx, p)
        m = gated_alloc(nc, ctx, p, hidden, kind == "bias")
        block = ctx.enter_context(nc.Block())

        @block.sync
        def _(sp):
            router_sync(sp, r, w[p + "wr"], w[p + "br"] if kind == "bias" else None)
            load_expert_weights(sp, m.sem, m.raw, w[p + "w"], E)

        @block.gpsimd
        def _(pool):
            ln_gpsimd(pool, g, n)
            gated_gpsimd(pool, g, n, r, m)

        @block.tensor
        def _(pe):
            ln_tensor(pe, g, n)
            router_tensor(pe, g, n, r, 4)
            widen_tensor(pe, g, r)
            gated_tensor(pe, g, n, m)
            add_tensor(pe, g, a, m.acc, [(m.sem["acc"], NCH)])

        @block.scalar
        def _(act):
            ln_scalar(act, g, n)
            router_scalar(act, r, kind)
            widen_scalar(act, g, r)
            gated_scalar(act, g, m)

        @block.vector
        def _(dve):
            router_split_vector(dve, r, kind == "bias")
            ln_rows_vector(dve, g, n, g.x)
            ln_lo_vector(dve, g, n)
            router_vector(dve, g, r, kind, 4)
            widen_vector(dve, g, r)
            split_weights_hi(dve, m.sem, m.w_hi, m.raw, 0, 0)
            gated_vector(dve, g, m)
            add_vector(dve, g, a, g.x, g.x)
            dve.wait_ge(a.sem["added"], NCH)


HIDDEN1, HIDDEN2 = 128, 352


def stage_l1_ffn(nc, g, w):
    stage_gated(nc, g, w, "f1_", HIDDEN1, "pair")


def stage_l2_ffn(nc, g, w):
    stage_gated(nc, g, w, "f2_", HIDDEN2, "bias")


TB = BANK // B
UN = 4
W_IN, W_GATE, W_STATE, W_INPUT, W_OUT = range(5)


def stage_l1_recurrence(nc, g, w):
    p = "a1_"
    with ExitStack() as ctx:
        n, a = ln_alloc(nc, ctx, p), add_alloc(nc, ctx, p)
        raw = sb(nc, ctx, p + "w_raw", 5 * D)
        w_hi, w_lo = sb(nc, ctx, p + "w_hi", 5 * D, F32R), sb(nc, ctx, p + "w_lo", 5 * D, F32R)
        bias = sb(nc, ctx, p + "bias", 5)
        ctxt, kv, r = sb(nc, ctx, p + "ctx", T), sb(nc, ctx, p + "kv", T), sb(nc, ctx, p + "r", T)
        ret = sb(nc, ctx, p + "ret", T)
        inp, inp_hi, inp_lo = sb(nc, ctx, p + "inp", T), sb(nc, ctx, p + "inp_hi", T, F32R), sb(nc, ctx, p + "inp_lo", T, F32R)
        tanh, gate, keep = sb(nc, ctx, p + "tanh", T), sb(nc, ctx, p + "gate", T), sb(nc, ctx, p + "keep", T)
        u = kv
        state = sb(nc, ctx, p + "state", B * (S + 1))
        gs = [sb(nc, ctx, f"{p}gs{i}", B) for i in range(2)]
        part_hi, part_lo = n.hi, n.lo
        s = sems(nc, p, "w raw bias ctx kv r w_hi w_lo half zero ret ret_hi ret_lo inp_mm inp inp_hi inp_lo gate_mm "
                             "tanh gate keep u u_hi u_lo fixed gs step state st_hi st_lo out_mm out")
        states = state[:, :].rearrange("p (b t) -> p b t", t=S + 1)
        gates = gate[:, :].rearrange("p (b t) -> p b t", t=S)
        acc = inp
        block = ctx.enter_context(nc.Block())

        def weight(x, k):
            return x[:, k * D:(k + 1) * D]

        def by_time(x, k):
            return x[:, :].rearrange("p (b t) -> p t b", t=S)[:, k * TB:(k + 1) * TB, :]

        def chunk(x, c):
            return x[:, ds(c * CH, CH)]

        @block.sync
        def _(sp):
            sp.dma_start(raw[:, :], w["a1_w"]).then_inc(s["raw"], 16)
            sp.dma_start(bias[:, 0:4], w["a1_bias"]).then_inc(s["bias"], 16)
            sp.dma_start(ctxt[:, :], w["ctx_t"]).then_inc(s["ctx"], 16)

        @block.gpsimd
        def _(pool):
            ln_gpsimd(pool, g, n)
            pool.wait_ge(s["w_hi"], 1)
            pool.tensor_tensor(w_lo[:, :], raw[:, :], w_hi[:, :].bitcast(F32), ALU.subtract).then_inc(s["w_lo"], 1)
            with pool.Fori(0, NCH) as c:
                pool.wait_ge(s["keep"], c + 1)
                pool.tensor_tensor(chunk(u, c), chunk(keep, c), chunk(inp, c), ALU.mult).then_inc(s["u"], 1)
                pool.wait_ge(s["u_hi"], c + 1)
                pool.tensor_tensor(chunk(part_lo, c), chunk(u, c), chunk(part_hi, c).bitcast(F32),
                                   ALU.subtract).then_inc(s["u_lo"], 1)

        @block.vector
        def _(dve):
            dve.wait_ge(s["raw"], 16)
            dve.tensor_copy(w_hi[:, :], raw[:, :]).then_inc(s["w_hi"], 1)
            dve.memset(states[:, :, 0], 0.0).then_inc(s["zero"], 1)
            dve.wait_ge(s["bias"], 16)
            dve.tensor_scalar(bias[:, 4:5], bias[:, 1:2], 0.5, None, ALU.mult).then_inc(s["half"], 1)
            dve.wait_ge(s["ctx"], 16)
            dve.tensor_tensor(kv[:, :], ctxt[:, :], ctxt[:, :], ALU.mult).then_inc(s["kv"], 1)
            dve.wait_ge(s["kv"], 1)
            with dve.Fori(0, B) as b:
                dve.tensor_tensor_scan(r[:, ds(b * S, S)], bias[:, 3:4].to_broadcast([128, S]), kv[:, ds(b * S, S)],
                                       0.0, ALU.mult, ALU.add).then_inc(s["r"], 1)
            ln_rows_vector(dve, g, n, g.x)
            dve.wait_ge(s["r"], B)
            with dve.Fori(0, NCH) as c:
                dve.wait_ge(n.sem["turned"], c + 1)
                dve.tensor_tensor(chunk(ret, c), g.psum[:, ds(c * BANK, CH)], chunk(r, c), ALU.mult).then_inc(s["ret"], 1)
                dve.wait_ge(s["ret_hi"], c + 1)
                dve.tensor_tensor(chunk(part_lo, c), chunk(ret, c), chunk(part_hi, c).bitcast(F32),
                                  ALU.subtract).then_inc(s["ret_lo"], 1)
            with dve.Fori(0, NCH) as c:
                dve.wait_ge(s["inp_hi"], c + 1)
                dve.tensor_tensor(chunk(inp_lo, c), chunk(inp, c), chunk(inp_hi, c).bitcast(F32),
                                  ALU.subtract).then_inc(s["inp_lo"], 1)
                dve.wait_ge(s["tanh"], c + 1)
                dve.tensor_scalar(chunk(gate, c), chunk(tanh, c), 0.5, 0.5, ALU.mult, ALU.add).then_inc(s["gate"], 1)
                dve.tensor_scalar(chunk(keep, c), chunk(tanh, c), -0.5, 0.5, ALU.mult, ALU.add).then_inc(s["keep"], 1)
            dve.wait_ge(s["gate"], NCH)
            dve.wait_ge(s["zero"], 1)
            with dve.Fori(0, S // UN) as tt:
                for k in range(UN):
                    t = tt * UN + k
                    dve.wait_ge(s["state"], t)
                    dve.tensor_tensor(gs[k % 2][:, :], gates[:, :, ds(t, 1)].rearrange("p b o -> p (b o)"),
                                      states[:, :, ds(t, 1)].rearrange("p b o -> p (b o)"), ALU.mult).then_inc(s["gs"], 1)
            for c in range(NCH):
                dve.wait_ge(s["st_hi"], c + 1)
                dve.tensor_tensor(part_lo[:, c * CH:(c + 1) * CH].rearrange("p (b t) -> p b t", t=S),
                                  states[:, c * TPC:(c + 1) * TPC, 1:],
                                  part_hi[:, c * CH:(c + 1) * CH].rearrange("p (b t) -> p b t", t=S).bitcast(F32),
                                  ALU.subtract).then_inc(s["st_lo"], 1)
            add_vector(dve, g, a, g.x, g.x)
            dve.wait_ge(a.sem["added"], NCH)

        @block.scalar
        def _(act):
            with act.Fori(0, NCH) as c:
                act.wait_ge(s["ret"], c + 1)
                act.activation(chunk(part_hi, c), chunk(ret, c), ACT.Copy).then_inc(s["ret_hi"], 1)
            act.wait_ge(s["half"], 1)
            with act.Fori(0, NCH) as c:
                act.wait_ge(s["inp_mm"], c + 1)
                act.activation(chunk(inp, c), g.psum[:, ds(c * BANK, CH)], ACT.Identity, bias=bias[:, 0:1]).then_inc(s["inp"], 1)
                act.wait_ge(s["inp"], c + 1)
                act.activation(chunk(inp_hi, c), chunk(inp, c), ACT.Copy).then_inc(s["inp_hi"], 1)
                act.wait_ge(s["gate_mm"], c + 1)
                act.activation(chunk(tanh, c), g.psum[:, ds((c + NCH) * BANK, CH)], ACT.Tanh, bias=bias[:, 4:5],
                               scale=0.5).then_inc(s["tanh"], 1)
                act.wait_ge(s["u"], c + 1)
                act.activation(chunk(part_hi, c), chunk(u, c), ACT.Copy).then_inc(s["u_hi"], 1)
            with act.Fori(0, S // UN) as tt:
                for k in range(UN):
                    t = tt * UN + k
                    act.wait_ge(s["step"], t + 1)
                    act.activation(states[:, :, ds(t + 1, 1)].rearrange("p b o -> p (b o)"),
                                   g.psum[:, ds(NCH * BANK + t * B, B)], ACT.Tanh).then_inc(s["state"], 1)
            act.wait_ge(s["state"], S)
            for c in range(NCH):
                act.activation(part_hi[:, c * CH:(c + 1) * CH].rearrange("p (b t) -> p b t", t=S),
                               states[:, c * TPC:(c + 1) * TPC, 1:], ACT.Copy).then_inc(s["st_hi"], 1)
            for c in range(NCH):
                act.wait_ge(s["out_mm"], c + 1)
                act.activation(acc[:, c * CH:(c + 1) * CH], bank(g, c), ACT.Identity, bias=bias[:, 2:3]).then_inc(s["out"], 1)

        @block.tensor
        def _(pe):
            ln_tensor(pe, g, n)
            pe.wait_ge(s["w_lo"], 1)
            with pe.Fori(0, NCH) as c:
                pe.wait_ge(s["ret_lo"], c + 1)
                product3(pe, g.psum[:, ds(c * BANK, CH)], weight(w_hi, W_IN), weight(w_lo, W_IN),
                         chunk(part_hi, c), chunk(part_lo, c)).then_inc(s["inp_mm"], 1)
                pe.wait_ge(s["inp_lo"], c + 1)
                product3(pe, g.psum[:, ds((c + NCH) * BANK, CH)], weight(w_hi, W_GATE), weight(w_lo, W_GATE),
                         chunk(inp_hi, c), chunk(inp_lo, c)).then_inc(s["gate_mm"], 1)
            pe.wait_ge(s["u_lo"], NCH)
            for k in range(NCH):
                out = bank(g, NCH + k)
                pe.matmul(out, weight(w_hi, W_INPUT), by_time(inp_hi, k), start=True, stop=False, skip_group_check=True)
                for x, y in ((weight(w_hi, W_INPUT), inp_lo), (weight(w_lo, W_INPUT), inp_hi),
                             (weight(w_hi, W_STATE), part_hi), (weight(w_hi, W_STATE), part_lo),
                             (weight(w_lo, W_STATE), part_hi)):
                    pe.matmul(out, x, by_time(y, k), start=False, stop=False, skip_group_check=True)
            with pe.Fori(0, S // UN) as tt:
                for k in range(UN):
                    t = tt * UN + k
                    pe.wait_ge(s["gs"], t + 1)
                    pe.matmul(g.psum[:, ds(NCH * BANK + t * B, B)], weight(raw, W_STATE), gs[k % 2][:, :],
                              start=False, stop=False, skip_group_check=True).then_inc(s["step"], 1)
            for c in range(NCH):
                pe.wait_ge(s["st_lo"], c + 1)
                product3(pe, bank(g, c), weight(w_hi, W_OUT), weight(w_lo, W_OUT), part_hi[:, c * CH:(c + 1) * CH],
                         part_lo[:, c * CH:(c + 1) * CH]).then_inc(s["out_mm"], 1)
            add_tensor(pe, g, a, acc, [(s["out"], NCH)])


HG = 4
NG = HEADS // HG
DH = D // HEADS
ST = 3 * HG * DH
VW = 32
UP = 2 * NG
PAIRS = B // 2
WQ, WK, WV, WO = 0, NG * ST, 2 * NG * ST, 2 * NG * ST + D
W_SMALL = WO + D


def stage_small_attention(nc, g, w, p, gated):
    with ExitStack() as ctx:
        n = ln_alloc(nc, ctx, p)
        raw = sb(nc, ctx, p + "w_raw", W_SMALL)
        w_hi, w_lo = sb(nc, ctx, p + "w_hi", W_SMALL, F32R), sb(nc, ctx, p + "w_lo", W_SMALL, F32R)
        bias = sb(nc, ctx, p + "bias", 2 * NG + 1)
        bv = sb(nc, ctx, p + "bv", D)
        ctxt = sb(nc, ctx, p + "ctx", T)
        ctx_hi, ctx_lo = sb(nc, ctx, p + "ctx_hi", T, F32R), sb(nc, ctx, p + "ctx_lo", T, F32R)
        qk = [sb(nc, ctx, f"{p}qk{i}", CH, rows=ST) for i in range(2)]
        q_all, k_all = (sb(nc, ctx, p + x, NG * T, F32R, ST) for x in ("q_all", "k_all"))
        v_all = sb(nc, ctx, p + "v_all", T)
        q_now = [sb(nc, ctx, f"{p}q_now{i}", NG * S, F32R, ST) for i in range(2)]
        k_now = [sb(nc, ctx, f"{p}k_now{i}", HG * S, F32R, ST) for i in range(4)]
        v_now = [sb(nc, ctx, f"{p}v_now{i}", HEADS * VW) for i in range(2)]
        top = [sb(nc, ctx, f"{p}top{i}", HG) for i in range(2)]
        probs = [sb(nc, ctx, f"{p}probs{i}", HG * S) for i in range(2)]
        probs_t = [sb(nc, ctx, f"{p}probs_t{i}", HG * S) for i in range(2)]
        pv = [sb(nc, ctx, f"{p}pv{i}", NG * S) for i in range(2)]
        rden = [sb(nc, ctx, f"{p}rden{i}", HEADS) for i in range(2)]
        o_rows = [sb(nc, ctx, f"{p}o_rows{i}", D) for i in range(2)]
        o_hi, o_lo = sb(nc, ctx, p + "o_hi", 2 * S, F32R), sb(nc, ctx, p + "o_lo", 2 * S, F32R)
        y = sb(nc, ctx, p + "y", 2 * S)
        s = sems(nc, p, "raw bias ctx w_hi w_lo c_hi c_lo qk_mm q_in k_in qk_hi qk_lo v_mm v_all v_init "
                             "q_now k_now v_now scores top shifted probs turned probs_t pv pv_out back rden o_rows "
                             "o_turned o_hi o_lo y_mm y y_turned added")
        e = Bag()
        if gated:
            e = Bag()
            e.raw = sb(nc, ctx, p + "e_raw", B * 32)
            e.rows = sb(nc, ctx, p + "e_rows", B)
            e.cols = sb(nc, ctx, p + "e_cols", S, rows=B)
            e.top = sb(nc, ctx, p + "e_top", 1, rows=B)
            e.rtop = sb(nc, ctx, p + "e_rtop", 1, rows=B)
            e.gate = sb(nc, ctx, p + "e_gate", S, rows=B)
            e.wide = sb(nc, ctx, p + "e_wide", T)
            e.sem = sems(nc, p + "e_", "raw rows turned step gate spread wide")
        block = ctx.enter_context(nc.Block())
        S_BANK, PV_BANK, T_BANK, M_BANK, N_BANK = 0, 2, 4, 6, 7
        softmax_scale = float(DH) ** -0.5

        def heads(a, width):
            return a[:, :].rearrange("p (h c) -> p h c", c=width)

        @block.sync
        def _(sp):
            sp.dma_start(raw[:, :], w[p + "w"]).then_inc(s["raw"], 16)
            sp.dma_start(ctxt[:, :], w["ctx_t"]).then_inc(s["ctx"], 16)
            sp.dma_start(bias[:, :], w[p + "bias"]).then_inc(s["bias"], 16)
            sp.dma_start(bv[:, :], w[p + "bv"].partition_broadcast(128)).then_inc(s["bias"], 16)
            if gated:
                sp.dma_start(e.raw[:, :].rearrange("p (b f) -> p b f", b=B), w["energy"].rearrange("b s f -> s b f")).then_inc(e.sem["raw"], 16)

        def seq_of(i, k):
            return i * 2 + k // NG

        def add_bias(eng, c, j):
            eng.wait_ge(s["qk_mm"], c * (2 * NG) + (j + 1))
            eng.wait_ge(s["qk_lo"], c * (2 * NG) + (j - 1)) if j >= 2 else eng.wait_ge(s["qk_lo"], c * (2 * NG))
            out, psum, col = qk[j % 2][:, :], bank(g, j % 4)[0:ST, :], bias[0:ST, j:j + 1]
            if gated and j >= NG:
                ins = eng.scalar_tensor_tensor(out=out, in0=psum, scalar=col, in1=e.wide[0:ST, ds(c * CH, CH)],
                                               op0=ALU.add, op1=ALU.mult)
            else:
                ins = eng.activation(out, psum, ACT.Identity, bias=col)
            ins.then_inc(s["q_in" if j < NG else "k_in"], 1)

        @block.gpsimd
        def _(pool):
            ln_gpsimd(pool, g, n)
            pool.wait_ge(s["w_hi"], 1)
            pool.tensor_tensor(w_lo[:, :], raw[:, :], w_hi[:, :].bitcast(F32), ALU.subtract).then_inc(s["w_lo"], 1)
            with pool.Fori(0, NCH) as c:
                pool.wait_ge(s["c_hi"], c + 1)
                pool.tensor_tensor(ctx_lo[:, ds(c * CH, CH)], ctxt[:, ds(c * CH, CH)], ctx_hi[:, ds(c * CH, CH)].bitcast(F32),
                                   ALU.subtract).then_inc(s["c_lo"], 1)
            pool.wait_ge(s["qk_lo"], 2 * NG * NCH)
            with pool.Fori(0, PAIRS) as i:
                for k in range(UP):
                    if k < 4:
                        pool.wait_ge(s["scores"], i * UP)
                    else:
                        pool.wait_ge(s["scores"], i * UP + (k - 3))
                    u = k % NG
                    keys = k_all[:, ds(u * T + seq_of(i, k) * S, S)].unsqueeze(1).to_broadcast([ST, HG, S])
                    own = g.head_rows[0:ST, :].unsqueeze(2).to_broadcast([ST, HG, S])
                    pool.tensor_tensor(heads(k_now[k % 4], S), keys.bitcast(F32), own, ALU.mult).then_inc(s["k_now"], 1)

        @block.tensor
        def _(pe):
            if gated:
                pe.wait_ge(e.sem["rows"], 1)
                pe.transpose(bank(g, N_BANK)[0:B, 0:S], e.rows[:, :], g.ident[:, :]).then_inc(e.sem["turned"], 1)
                pe.wait_ge(e.sem["gate"], 1)
                for b in range(B):
                    last = pe.matmul(bank(g, b // TPC)[:, (b % TPC) * S:(b % TPC + 1) * S],
                                     g.ident[0:B, b:b + 1].to_broadcast([B, 128]), e.gate[:, :], start=True, stop=True)
                    if b % TPC == TPC - 1:
                        last.then_inc(e.sem["spread"], 1)
                pe.wait_ge(e.sem["wide"], NCH)
            pe.wait_ge(s["w_lo"], 1)
            for b in range(B):
                if b % TPC == 0:
                    pe.wait_ge(s["c_lo"], b // TPC + 1)
                tok = slice(b * S, (b + 1) * S)
                last = product3(pe, bank(g, 4 + b // TPC)[:, (b % TPC) * D:(b % TPC + 1) * D], ctx_hi[:, tok], ctx_lo[:, tok],
                                w_hi[:, WV:WV + D], w_lo[:, WV:WV + D])
                if b % TPC == TPC - 1:
                    last.then_inc(s["v_mm"], 1)
            ln_tensor(pe, g, n)
            pe.wait_ge(n.sem["lo_ready"], NCH)
            pe.wait_ge(s["v_all"], NCH)
            with pe.Fori(0, NCH) as c:
                for j in range(2 * NG):
                    pe.wait_ge(s["q_in"], c * NG + (j - NG + 1)) if j >= NG else pe.wait_ge(s["k_in"], c * NG)
                    x_hi, x_lo = (n.hi, n.lo) if j < NG else (ctx_hi, ctx_lo)
                    col = j * ST
                    product3(pe, bank(g, j % 4)[0:ST, :], w_hi[:, col:col + ST], w_lo[:, col:col + ST],
                             x_hi[:, ds(c * CH, CH)], x_lo[:, ds(c * CH, CH)]).then_inc(s["qk_mm"], 1)
            pe.wait_ge(s["k_in"], NG * NCH)

            def scores(i, k):
                unit = i * UP + k
                if k % NG == 0:
                    pe.wait_ge(s["q_now"], seq_of(i, k) + 1)
                pe.wait_ge(s["k_now"], unit + 1)
                if not (isinstance(i, int) and i == 0 and k < 2):
                    pe.wait_ge(s["shifted"], unit - 1)
                u = k % NG
                pe.matmul(bank(g, S_BANK + k % 2), q_now[k // NG][:, u * S:(u + 1) * S], k_now[k % 4][:, :],
                          start=True, stop=True).then_inc(s["scores"], 1)

            def turn_probs(i, k):
                unit = i * UP + k
                pe.wait_ge(s["probs"], unit + 1)
                if not (isinstance(i, int) and i == 0 and k < 2):
                    pe.wait_ge(s["probs_t"], unit - 1)
                for j in range(HG):
                    cols = slice(j * S, (j + 1) * S)
                    last = pe.transpose(bank(g, T_BANK + k % 2)[:, cols], probs[k % 2][:, cols], g.ident[:, :])
                last.then_inc(s["turned"], 1)

            def weigh(i, k):
                unit, q, u = i * UP + k, k // NG, k % NG
                pe.wait_ge(s["probs_t"], unit + 1)
                if u == 0:
                    pe.wait_ge(s["v_now"], seq_of(i, k) + 1)
                    if not (isinstance(i, int) and i == 0):
                        pe.wait_ge(s["pv_out"], seq_of(i, k) - 1)
                for j in range(HG):
                    h = u * HG + j
                    last = pe.matmul(bank(g, PV_BANK + q)[j * VW:(j + 1) * VW, u * S:(u + 1) * S],
                                     v_now[q][:, h * VW:(h + 1) * VW], probs_t[k % 2][:, j * S:(j + 1) * S],
                                     start=True, stop=True, tile_position=(0, j * VW))
                last.then_inc(s["pv"], 1)

            def back(i, q):
                pe.wait_ge(s["pv_out"], i * 2 + q + 1)
                for u in range(NG):
                    cols = slice(u * S, (u + 1) * S)
                    last = pe.transpose(bank(g, M_BANK)[:, cols], pv[q][:, cols], g.ident[:, :])
                last.then_inc(s["back"], 1)

            def turn_out(i, q):
                pe.wait_ge(s["o_rows"], i * 2 + q + 1)
                pe.transpose(bank(g, N_BANK)[:, 0:S], o_rows[q][:, :], g.ident[:, :]).then_inc(s["o_turned"], 1)

            def project(i):
                pe.wait_ge(s["o_lo"], i * 2 + 2)
                product3(pe, bank(g, M_BANK)[:, 0:2 * S], w_hi[:, WO:WO + D], w_lo[:, WO:WO + D], o_hi[:, :],
                         o_lo[:, :]).then_inc(s["y_mm"], 1)

            def turn_y(i):
                pe.wait_ge(s["y"], i + 1)
                for q in range(2):
                    last = pe.transpose(bank(g, N_BANK)[:, q * S:(q + 1) * S], y[:, q * S:(q + 1) * S], g.ident[:, :])
                last.then_inc(s["y_turned"], 1)

            def body(i, first, last):
                for k in range(UP):
                    scores(i, k)
                    if k >= 1:
                        turn_probs(i, k - 1)
                    elif not first:
                        turn_probs(i - 1, UP - 1)
                    if k >= 2:
                        weigh(i, k - 2)
                    elif not first:
                        weigh(i - 1, UP - 2 + k)
                    if not first:
                        if k == 2:
                            back(i - 1, 1)
                        if k == 3:
                            turn_out(i - 1, 1)
                        if k == 4:
                            project(i - 1)
                        if k == 5:
                            turn_y(i - 1)
                    if k == 6:
                        back(i, 0)
                    if k == 7:
                        turn_out(i, 0)
                if last:
                    turn_probs(i, UP - 1)
                    weigh(i, UP - 2)
                    weigh(i, UP - 1)
                    back(i, 1)
                    turn_out(i, 1)
                    project(i)
                    turn_y(i)

            in_pairs(pe, body)

        @block.scalar
        def _(act):
            act.wait_ge(s["ctx"], 16)
            with act.Fori(0, NCH) as c:
                act.activation(ctx_hi[:, ds(c * CH, CH)], ctxt[:, ds(c * CH, CH)], ACT.Copy).then_inc(s["c_hi"], 1)
            ln_scalar(act, g, n)
            act.wait_ge(s["bias"], 32)
            with act.Fori(0, NCH) as c:
                for j in range(NG if gated else 2 * NG):
                    add_bias(act, c, j)

            def exponentials(i, k):
                unit = i * UP + k
                act.wait_ge(s["shifted"], unit + 1)
                act.activation(probs[k % 2][:, :], probs[k % 2][:, :], ACT.Exp, scale=softmax_scale).then_inc(s["probs"], 1)

            def copy_turned(i, k):
                unit = i * UP + k
                act.wait_ge(s["turned"], unit + 1)
                if not (isinstance(i, int) and i == 0 and k < 2):
                    act.wait_ge(s["pv"], unit - 1)
                act.activation(probs_t[k % 2][:, :], bank(g, T_BANK + k % 2), ACT.Copy).then_inc(s["probs_t"], 1)

            def place_values(i, q):
                if not (isinstance(i, int) and i == 0):
                    act.wait_ge(s["pv"], i * UP + (q - 1) * NG)
                act.activation(heads(v_now[q], VW)[:, :, 0:DH], v_all[:, ds(i * (2 * S) + q * S, D)].rearrange("p (h c) -> p h c", c=DH),
                               ACT.Copy).then_inc(s["v_now"], 1)

            def copy_weighed(i, q):
                act.wait_ge(s["pv"], i * UP + (q + 1) * NG)
                act.activation(pv[q][:, :], bank(g, PV_BANK + q), ACT.Copy).then_inc(s["pv_out"], 1)

            def out_hi(i, q):
                act.wait_ge(s["o_turned"], i * 2 + q + 1)
                act.activation(o_hi[:, q * S:(q + 1) * S], bank(g, N_BANK)[:, 0:S], ACT.Copy).then_inc(s["o_hi"], 1)

            def copy_y(i):
                act.wait_ge(s["y_mm"], i + 1)
                act.activation(y[:, :], bank(g, M_BANK)[:, 0:2 * S], ACT.Identity, bias=bias[:, 2 * NG:2 * NG + 1]).then_inc(s["y"], 1)

            def body(i, first, last):
                for k in range(UP):
                    if k >= 1:
                        copy_turned(i, k - 1)
                    elif not first:
                        copy_turned(i - 1, UP - 1)
                    if k in (1, 5):
                        place_values(i, k // NG)
                    exponentials(i, k)
                    if not first:
                        if k == 1:
                            copy_weighed(i - 1, 1)
                        if k == 3:
                            out_hi(i - 1, 1)
                        if k == 4:
                            copy_y(i - 1)
                    if k == 5:
                        copy_weighed(i, 0)
                    if k == 7:
                        out_hi(i, 0)
                if last:
                    copy_turned(i, UP - 1)
                    copy_weighed(i, 1)
                    out_hi(i, 1)
                    copy_y(i)

            act.wait_ge(s["v_init"], 2)
            act.wait_ge(s["v_all"], NCH)
            in_pairs(act, body)

        @block.vector
        def _(dve):
            dve.wait_ge(s["raw"], 16)
            dve.tensor_copy(w_hi[:, :], raw[:, :]).then_inc(s["w_hi"], 1)
            if gated:
                es = e.sem
                dve.wait_ge(es["raw"], 16)
                dve.tensor_reduce(e.rows[:, :], e.raw[:, :].rearrange("p (b f) -> p b f", b=B), AX.X, ALU.add,
                                  apply_absolute_value=True).then_inc(es["rows"], 1)
                dve.wait_ge(es["turned"], 1)
                dve.tensor_scalar(e.cols[:, :], bank(g, N_BANK)[0:B, 0:S], 1.0 / 32, None, ALU.mult).then_inc(es["step"], 1)
                dve.wait_ge(es["step"], 1)
                dve.tensor_reduce(e.top[:, :], e.cols[:, :], AX.X, ALU.max).then_inc(es["step"], 1)
                dve.wait_ge(es["step"], 2)
                dve.tensor_scalar(e.top[:, :], e.top[:, :], 1e-8, None, ALU.add).then_inc(es["step"], 1)
                dve.wait_ge(es["step"], 3)
                dve.reciprocal(e.rtop[:, :], e.top[:, :]).then_inc(es["step"], 1)
                dve.wait_ge(es["step"], 4)
                dve.tensor_scalar(e.cols[:, :], e.cols[:, :], e.rtop[:, 0:1], 0.1, ALU.mult, ALU.is_gt).then_inc(es["step"], 1)
                dve.wait_ge(es["step"], 5)
                dve.tensor_scalar(e.gate[:, :], e.cols[:, :], 0.9, 0.1, ALU.mult, ALU.add).then_inc(es["gate"], 1)
                with dve.Fori(0, NCH) as c:
                    dve.wait_ge(es["spread"], c + 1)
                    dve.tensor_copy(e.wide[:, ds(c * CH, CH)], g.psum[:, ds(c * BANK, CH)]).then_inc(es["wide"], 1)
            for q in range(2):
                dve.memset(v_now[q][:, :], 0.0).then_inc(s["v_init"], 1)
            dve.wait_ge(s["v_init"], 2)
            for q in range(2):
                dve.memset(heads(v_now[q], VW)[:, :, DH:DH + 1], 1.0).then_inc(s["v_init"], 1)
            dve.wait_ge(s["v_init"], 4)
            dve.wait_ge(s["bias"], 32)
            ln_rows_vector(dve, g, n, g.x)
            ln_lo_vector(dve, g, n)
            with dve.Fori(0, NCH) as c:
                dve.wait_ge(s["v_mm"], c + 1)
                dve.tensor_tensor(v_all[:, ds(c * CH, CH)].rearrange("p (t d) -> p t d", d=D),
                                  g.psum[:, ds((c + 4) * BANK, CH)].rearrange("p (t d) -> p t d", d=D),
                                  bv[:, :].unsqueeze(1).to_broadcast([128, TPC, D]), ALU.add).then_inc(s["v_all"], 1)
            with dve.Fori(0, NCH) as c:
                for j in range(2 * NG):
                    if gated and j >= NG:
                        add_bias(dve, c, j)
                    in_ = s["q_in" if j < NG else "k_in"]
                    dve.wait_ge(in_, c * NG + (j % NG + 1))
                    all_ = (q_all if j < NG else k_all)[:, ds(c * CH + (j % NG) * T, CH)]
                    dve.tensor_copy(all_, qk[j % 2][:, :]).then_inc(s["qk_hi"], 1)
                    dve.wait_ge(s["qk_hi"], c * (2 * NG) + (j + 1))
                    r0 = ST // 3 * (1 if j < NG else 2)
                    low = (q_all if j < NG else k_all)[r0:r0 + ST // 3, ds(c * CH + (j % NG) * T, CH)]
                    dve.tensor_tensor(low, qk[j % 2][r0:r0 + ST // 3, :], low.bitcast(F32), ALU.subtract).then_inc(s["qk_lo"], 1)

            def place_queries(i, q):
                if not (isinstance(i, int) and i == 0):
                    dve.wait_ge(s["scores"], i * UP + (q - 1) * NG)
                dve.tensor_copy(q_now[q][:, :].rearrange("p (u t) -> p u t", u=NG),
                                q_all[:, :].rearrange("p (u t) -> p u t", u=NG)[:, :, ds(i * (2 * S) + q * S, S)]).then_inc(s["q_now"], 1)

            def shift(i, k):
                unit = i * UP + k
                psum = bank(g, S_BANK + k % 2).rearrange("p (h t) -> p h t", t=S)
                dve.wait_ge(s["scores"], unit + 1)
                dve.tensor_reduce(top[k % 2][:, :], psum, AX.X, ALU.max).then_inc(s["top"], 1)
                dve.wait_ge(s["top"], unit + 1)
                if not (isinstance(i, int) and i == 0 and k < 2):
                    dve.wait_ge(s["turned"], unit - 1)
                dve.tensor_tensor(heads(probs[k % 2], S), psum, top[k % 2][:, :].unsqueeze(2).to_broadcast([128, HG, S]),
                                  ALU.subtract).then_inc(s["shifted"], 1)

            def normalize(i, q):
                back = bank(g, M_BANK).rearrange("p (h c) -> p h c", c=VW)
                seq = i * 2 + q
                dve.wait_ge(s["back"], seq + 1)
                dve.reciprocal(rden[q][:, :], back[:, :, DH]).then_inc(s["rden"], 1)
                dve.wait_ge(s["rden"], seq + 1)
                dve.tensor_tensor(heads(o_rows[q], DH), back[:, :, 0:DH], rden[q][:, :].unsqueeze(2).to_broadcast([128, HEADS, DH]),
                                  ALU.mult).then_inc(s["o_rows"], 1)

            def out_lo(i, q):
                cols = slice(q * S, (q + 1) * S)
                dve.wait_ge(s["o_hi"], i * 2 + q + 1)
                dve.tensor_tensor(o_lo[:, cols], bank(g, N_BANK)[:, 0:S], o_hi[:, cols].bitcast(F32),
                                  ALU.subtract).then_inc(s["o_lo"], 1)

            def add_y(i):
                dve.wait_ge(s["y_turned"], i + 1)
                tok = ds(i * (2 * S), 2 * S)
                dve.tensor_tensor(g.x[:, tok], g.x[:, tok], bank(g, N_BANK)[:, 0:2 * S], ALU.add).then_inc(s["added"], 1)

            def body(i, first, last):
                for k in range(UP):
                    shift(i, k)
                    if not first:
                        if k == 2:
                            normalize(i - 1, 1)
                        if k == 3:
                            out_lo(i - 1, 1)
                        if k == 5:
                            add_y(i - 1)
                    if k == 1:
                        place_queries(i, 1)
                    if k == 6:
                        normalize(i, 0)
                        if not last:
                            place_queries(i + 1, 0)
                    if k == 7:
                        out_lo(i, 0)
                if last:
                    normalize(i, 1)
                    out_lo(i, 1)
                    add_y(i)

            dve.wait_ge(s["qk_lo"], 2 * NG * NCH)
            place_queries(0, 0)
            in_pairs(dve, body)
            dve.wait_ge(s["added"], PAIRS)


def in_pairs(eng, body):
    body(0, True, False)
    with eng.Fori(1, PAIRS - 1) as i:
        body(i, False, False)
    body(PAIRS - 1, False, True)


def stage_l2_attention(nc, g, w):
    stage_small_attention(nc, g, w, "a2_", True)


def stage_l3_attention(nc, g, w):
    stage_small_attention(nc, g, w, "a3_", False)


D0 = 64
INNER = HEADS * D0
NBLK = INNER // 128
UG = 4
UNITS = 2 * HEADS // UG
RUNS = UNITS // 2
GROUPS = 12
MASKED = -2.0 ** 100
WQ0, WK0, WV0, WO0 = 0, INNER, 2 * INNER, 3 * INNER
S0, T0, O0, J0, Y0 = 0, 2, 4, 5, 7


def floor0(count):
    return max(count, 0) if isinstance(count, int) else count


def stage_l0_attention(nc, g, w):
    p = "a0_"
    with ExitStack() as ctx:
        n = ln_alloc(nc, ctx, p)
        ctxt = sb(nc, ctx, p + "ctx", T)
        ctx_hi, ctx_lo = sb(nc, ctx, p + "ctx_hi", T, F32R), sb(nc, ctx, p + "ctx_lo", T, F32R)
        w_hi, w_lo = sb(nc, ctx, p + "w_hi", 4 * INNER, F32R), sb(nc, ctx, p + "w_lo", 4 * INNER, F32R)
        qk = [sb(nc, ctx, f"{p}qk{i}", 2 * NBLK * 2 * S) for i in range(2)]
        v = [sb(nc, ctx, f"{p}v{i}", 2 * INNER) for i in range(2)]
        ctx_now = [[sb(nc, ctx, f"{p}ctx_now{x}{i}", 2 * S, F32R) for x in ("hi", "lo")] for i in range(2)]
        raw = qk[1]
        bo = sb(nc, ctx, p + "bo", 1)
        mask_words, mask = sb(nc, ctx, p + "mask_words", T // 4, I32), sb(nc, ctx, p + "mask", T, BF16)
        neg_top = [sb(nc, ctx, f"{p}neg_top{i}", UG) for i in range(2)]
        den = [sb(nc, ctx, f"{p}den{i}", UG) for i in range(2)]
        rden = [sb(nc, ctx, f"{p}rden{i}", UG) for i in range(2)]
        probs = [sb(nc, ctx, f"{p}probs{i}", UG * S) for i in range(4)]
        probs_t = [sb(nc, ctx, f"{p}probs_t{i}", UG * S) for i in range(4)]
        o_hi, o_lo = sb(nc, ctx, p + "o_hi", NBLK * 2 * S, F32R), sb(nc, ctx, p + "o_lo", NBLK * 2 * S, F32R)
        y = sb(nc, ctx, p + "y", 2 * S)
        s = sems(nc, p, "raw ctx bo mask w_hi w_lo c_hi c_lo c_now masked proj proj_act proj_dve scores neg_top probs rden "
                             "normed turned probs_t weighed o_hi o_lo y_mm y y_turned added")
        block = ctx.enter_context(nc.Block())

        def q_of(par):
            return qk[par][:, 0:NBLK * 2 * S].rearrange("p (b q t) -> p b q t", b=NBLK, q=2)

        def k_of(par):
            return qk[par][:, NBLK * 2 * S:].rearrange("p (b q t) -> p b q t", b=NBLK, q=2)

        def group_out(par, m):
            if m < 8:
                c0 = (m % 2) * NBLK * 2 * S + (m // 2) * CH
                return qk[par][:, c0:c0 + CH]
            return v[par][:, (m - 8) * CH:(m - 7) * CH]

        def blocks4(o, k):
            return o[:, :].rearrange("p (b q t) -> p b q t", b=NBLK, q=2)[:, 4 * (k // 2):4 * (k // 2) + 4, k % 2]

        def four(a):
            return a.rearrange("p (h t) -> p h t", t=S)

        def in_two_pairs(eng, body):
            body(0, True, False)
            with eng.Fori(1, PAIRS // 2 - 1) as dp:
                body(dp, False, False)
            body(PAIRS // 2 - 1, False, True)

        @block.sync
        def _(sp):
            sp.dma_start(ctxt[:, :], w["ctx_t"]).then_inc(s["ctx"], 16)
            for k in range(4):
                cols = slice(k * INNER, (k + 1) * INNER)
                sp.dma_start(raw[:, cols], w["a0_w"][:, cols]).then_inc(s["raw"], 16)
            sp.dma_start(bo[:, :], w["a0_bo"]).then_inc(s["bo"], 16)
            sp.dma_start(mask_words[:, :].rearrange("p (b t) -> p b t", b=B), w["mask"].rearrange("b s t -> s b t")).then_inc(s["mask"], 16)

        @block.gpsimd
        def _(pool):
            with pool.Fori(0, NCH) as c:
                pool.wait_ge(s["c_hi"], c + 1)
                pool.tensor_tensor(ctx_lo[:, ds(c * CH, CH)], ctxt[:, ds(c * CH, CH)], ctx_hi[:, ds(c * CH, CH)].bitcast(F32),
                                   ALU.subtract).then_inc(s["c_lo"], 1)
            ln_gpsimd(pool, g, n)
            for k in range(4):
                cols = slice(k * INNER, (k + 1) * INNER)
                pool.wait_ge(s["w_hi"], k + 1)
                pool.tensor_tensor(w_lo[:, cols], raw[:, cols], w_hi[:, cols].bitcast(F32), ALU.subtract).then_inc(s["w_lo"], 1)

            def normalize(c, k):
                pool.wait_ge(s["rden"], c + (k + 1))
                pool.wait_ge(s["probs"], c + (k + 1))
                pool.tensor_tensor(four(probs[k % 4][:, :]), four(probs[k % 4][:, :]),
                                   rden[k % 2][:, :].unsqueeze(2).to_broadcast([128, UG, S]), ALU.mult).then_inc(s["normed"], 1)

            with pool.Fori(0, PAIRS) as i:
                for k in range(UNITS):
                    normalize(i * UNITS, k)

        @block.tensor
        def _(pe):
            ln_tensor(pe, g, n)
            pe.wait_ge(n.sem["lo_ready"], NCH)
            pe.wait_ge(s["c_lo"], NCH)
            pe.wait_ge(s["w_lo"], 3)

            def project(pair, par, m):
                out = bank(g, J0 + m % 2)
                done = s["proj_dve"] if m % 2 else s["proj_act"]
                pe.wait_ge(done, floor0(pair * (GROUPS // 2) + m // 2))
                if m < 8:
                    x_hi, x_lo = (ctx_hi, ctx_lo) if m % 2 else (n.hi, n.lo)
                    for b in range(2):
                        col = (m % 2) * INNER + (2 * (m // 2) + b) * 128
                        tok = ds(pair * (2 * S), 2 * S)
                        last = product3(pe, out[:, b * 2 * S:(b + 1) * 2 * S], w_hi[:, col:col + 128], w_lo[:, col:col + 128],
                                        x_hi[:, tok], x_lo[:, tok])
                else:
                    q, half = (m - 8) // 2, m % 2
                    pe.wait_ge(s["c_now"], pair * 2 + 2)
                    c_hi, c_lo = ctx_now[par][0][:, q * S:(q + 1) * S], ctx_now[par][1][:, q * S:(q + 1) * S]
                    cols = slice(WV0 + half * CH, WV0 + (half + 1) * CH)
                    last = product3(pe, out, c_hi, c_lo, w_hi[:, cols], w_lo[:, cols])
                last.then_inc(s["proj"], 1)

            def scores(pair, par, k):
                unit = pair * UNITS + k
                pe.wait_ge(s["probs"], floor0(unit - 1))
                if k == 0:
                    pe.wait_ge(s["proj_act"], pair * (GROUPS // 2) + 4)
                    pe.wait_ge(s["proj_dve"], pair * (GROUPS // 2) + 4)
                q, half, out = k // 2 % 2, k % 2, bank(g, S0 + k % 2)
                hide = mask[:, ds(pair * (2 * S) + q * S, S)].unsqueeze(1).to_broadcast([128, UG, S])
                pe.matmul(four(out), g.ident_b[:, :], hide, start=True, stop=False, skip_group_check=True)
                rows = slice(half * D0, (half + 1) * D0)
                for j in range(UG):
                    b = 4 * (k // 4) + j
                    last = pe.matmul(out[:, j * S:(j + 1) * S], q_of(par)[rows, b, q], k_of(par)[rows, b, q],
                                     start=False, stop=True, skip_group_check=True)
                last.then_inc(s["scores"], 1)

            def turn_probs(pair, k):
                unit = pair * UNITS + k
                pe.wait_ge(s["normed"], unit + 1)
                pe.wait_ge(s["probs_t"], floor0(unit - 1))
                for j in range(UG):
                    cols = slice(j * S, (j + 1) * S)
                    last = pe.transpose(bank(g, T0 + k % 2)[:, cols], probs[k % 4][:, cols], g.ident[:, :])
                last.then_inc(s["turned"], 1)

            def weigh(pair, par, r):
                pe.wait_ge(s["probs_t"], pair * UNITS + (2 * r + 2))
                if r == 0:
                    pe.wait_ge(s["proj_act"], pair * (GROUPS // 2) + GROUPS // 2)
                    pe.wait_ge(s["proj_dve"], pair * (GROUPS // 2) + GROUPS // 2)
                pe.wait_ge(s["o_lo"], floor0(pair * RUNS + r))
                for j in range(UG):
                    for half in range(2):
                        h = 2 * (4 * (r // 2) + j) + half
                        col = (r % 2) * INNER + h * D0
                        last = pe.matmul(bank(g, O0)[half * D0:(half + 1) * D0, j * S:(j + 1) * S], v[par][:, col:col + D0],
                                         probs_t[2 * (r % 2) + half][:, j * S:(j + 1) * S], start=True, stop=True,
                                         tile_position=(0, half * D0))
                last.then_inc(s["weighed"], 1)

            def project_out(pair):
                pe.wait_ge(s["o_lo"], pair * RUNS + RUNS)
                pe.wait_ge(s["added"], floor0(pair * 1))
                for b in range(NBLK):
                    ws, cols = slice(WO0 + b * D, WO0 + (b + 1) * D), slice(b * 2 * S, (b + 1) * 2 * S)
                    last = product3(pe, bank(g, Y0)[:, 0:2 * S], w_hi[:, ws], w_lo[:, ws], o_hi[:, cols], o_lo[:, cols],
                                    first=b == 0, last=b == NBLK - 1)
                last.then_inc(s["y_mm"], 1)

            def turn_y(pair):
                pe.wait_ge(s["y"], pair + 1)
                for q in range(2):
                    last = pe.transpose(bank(g, Y0)[:, (2 + q) * S:(3 + q) * S], y[:, q * S:(q + 1) * S], g.ident[:, :])
                last.then_inc(s["y_turned"], 1)

            def one_pair(pair, par, first, last):
                for k in range(UNITS):
                    scores(pair, par, k)
                    if not last:
                        for m in groups_at(k):
                            project(pair + 1, 1 - par, m)
                    if k >= 2:
                        turn_probs(pair, k - 2)
                    elif not first:
                        turn_probs(pair - 1, UNITS - 2 + k)
                    if k in (0, 2) and not first:
                        weigh(pair - 1, 1 - par, 2 + k // 2)
                    if k in (4, 6):
                        weigh(pair, par, k // 2 - 2)
                    if k == 3 and not first:
                        project_out(pair - 1)
                    if k == 5 and not first:
                        turn_y(pair - 1)
                if last:
                    turn_probs(pair, UNITS - 2)
                    turn_probs(pair, UNITS - 1)
                    weigh(pair, par, 2)
                    weigh(pair, par, 3)
                    project_out(pair)
                    turn_y(pair)

            for m in range(GROUPS):
                project(0, 0, m)
            pe.wait_ge(s["masked"], 1)
            pe.wait_ge(s["w_lo"], 4)
            in_two_pairs(pe, lambda dp, first, last: (one_pair(dp * 2, 0, first, False), one_pair(dp * 2 + 1, 1, False, last)))

        @block.scalar
        def _(act):
            act.wait_ge(s["ctx"], 16)
            with act.Fori(0, NCH) as c:
                act.activation(ctx_hi[:, ds(c * CH, CH)], ctxt[:, ds(c * CH, CH)], ACT.Copy).then_inc(s["c_hi"], 1)
            ln_scalar(act, g, n)

            def read_out(pair, par, m, first):
                act.wait_ge(s["proj"], pair * GROUPS + (m + 1))
                act.wait_ge(s["scores"], floor0(pair * UNITS - UNITS)) if m < 8 else act.wait_ge(s["weighed"], floor0(pair * RUNS - RUNS))
                if first and par:
                    act.wait_ge(s["w_lo"], 4)
                act.activation(group_out(par, m), bank(g, J0), ACT.Copy, scale=D0 ** -0.5 if m < 8 else 1.0).then_inc(s["proj_act"], 1)

            def exponentials(pair, k):
                unit = pair * UNITS + k
                act.wait_ge(s["neg_top"], unit + 1)
                act.wait_ge(s["rden"], floor0(unit - 1))
                act.wait_ge(s["turned"], floor0(unit - 3))
                for j in range(UG):
                    cols = slice(j * S, (j + 1) * S)
                    last = act.activation(probs[k % 4][:, cols], bank(g, S0 + k % 2)[:, cols], ACT.Exp,
                                          bias=neg_top[k % 2][:, j:j + 1], accum_out=den[k % 2][:, j:j + 1])
                last.then_inc(s["probs"], 1)

            def copy_turned(pair, k):
                act.wait_ge(s["turned"], pair * UNITS + (k + 1))
                act.wait_ge(s["weighed"], floor0(pair * RUNS + (k // 2 - 1)))
                act.activation(probs_t[k % 4][:, :], bank(g, T0 + k % 2), ACT.Copy).then_inc(s["probs_t"], 1)

            def out_hi(pair, r):
                act.wait_ge(s["weighed"], pair * RUNS + (r + 1))
                act.wait_ge(s["y_mm"], pair * 1)
                act.activation(blocks4(o_hi, r), four(bank(g, O0)), ACT.Copy).then_inc(s["o_hi"], 1)

            def copy_y(pair):
                act.wait_ge(s["y_mm"], pair + 1)
                act.wait_ge(s["y_turned"], pair * 1)
                act.activation(y[:, :], bank(g, Y0)[:, 0:2 * S], ACT.Identity, bias=bo[:, 0:1]).then_inc(s["y"], 1)

            def one_pair(pair, par, first, last):
                for k in range(UNITS):
                    if k >= 2:
                        copy_turned(pair, k - 2)
                    elif not first:
                        copy_turned(pair - 1, UNITS - 2 + k)
                    exponentials(pair, k)
                    if not last:
                        for m in groups_at(k):
                            if m % 2 == 0:
                                read_out(pair + 1, 1 - par, m, first)
                    if k in (0, 2) and not first:
                        out_hi(pair - 1, 2 + k // 2)
                    if k in (4, 6):
                        out_hi(pair, k // 2 - 2)
                    if k == 4 and not first:
                        copy_y(pair - 1)
                if last:
                    copy_turned(pair, UNITS - 2)
                    copy_turned(pair, UNITS - 1)
                    out_hi(pair, 2)
                    out_hi(pair, 3)
                    copy_y(pair)

            for m in range(0, GROUPS, 2):
                read_out(0, 0, m, True)
            act.wait_ge(s["bo"], 16)
            in_two_pairs(act, lambda dp, first, last: (one_pair(dp * 2, 0, first, False), one_pair(dp * 2 + 1, 1, False, last)))

        @block.vector
        def _(dve):
            for k in range(4):
                cols = slice(k * INNER, (k + 1) * INNER)
                dve.wait_ge(s["raw"], 64)
                dve.tensor_copy(w_hi[:, cols], raw[:, cols]).then_inc(s["w_hi"], 1)
            ln_rows_vector(dve, g, n, g.x)
            ln_lo_vector(dve, g, n)

            def context_now(pair, par):
                tok = ds(pair * (2 * S), 2 * S)
                dve.wait_ge(s["proj"], floor0(pair * GROUPS - GROUPS))
                for x, y_ in zip(ctx_now[par], (ctx_hi, ctx_lo)):
                    dve.tensor_copy(x[:, :], y_[:, tok]).then_inc(s["c_now"], 1)

            def read_out(pair, par, m, first):
                dve.wait_ge(s["proj"], pair * GROUPS + (m + 1))
                dve.wait_ge(s["scores"], floor0(pair * UNITS - UNITS)) if m < 8 else dve.wait_ge(s["weighed"], floor0(pair * RUNS - RUNS))
                if first and par:
                    dve.wait_ge(s["w_lo"], 4)
                dve.tensor_copy(group_out(par, m), bank(g, J0 + 1)).then_inc(s["proj_dve"], 1)

            def largest(pair, k):
                unit = pair * UNITS + k
                dve.wait_ge(s["scores"], unit + 1)
                dve.wait_ge(s["probs"], floor0(unit - 1))
                dve.tensor_reduce(neg_top[k % 2][:, :], four(bank(g, S0 + k % 2)), AX.X, ALU.max, negate=True).then_inc(s["neg_top"], 1)

            def invert(pair, k):
                unit = pair * UNITS + k
                dve.wait_ge(s["probs"], unit + 1)
                dve.wait_ge(s["normed"], floor0(unit - 1))
                dve.reciprocal(rden[k % 2][:, :], den[k % 2][:, :]).then_inc(s["rden"], 1)

            def out_lo(pair, r):
                dve.wait_ge(s["o_hi"], pair * RUNS + (r + 1))
                dve.tensor_tensor(blocks4(o_lo, r), four(bank(g, O0)), blocks4(o_hi, r).bitcast(F32), ALU.subtract).then_inc(s["o_lo"], 1)

            def add_y(pair):
                dve.wait_ge(s["y_turned"], pair + 1)
                tok = ds(pair * (2 * S), 2 * S)
                dve.tensor_tensor(g.x[:, tok], g.x[:, tok], bank(g, Y0)[:, 2 * S:4 * S], ALU.add).then_inc(s["added"], 1)

            def one_pair(pair, par, first, last):
                for k in range(UNITS):
                    largest(pair, k)
                    if not last:
                        for m in groups_at(k):
                            if m % 2:
                                read_out(pair + 1, 1 - par, m, first)
                    if k == 1 and not last:
                        context_now(pair + 1, 1 - par)
                    invert(pair, k)
                    if k in (0, 2) and not first:
                        out_lo(pair - 1, 2 + k // 2)
                    if k in (4, 6):
                        out_lo(pair, k // 2 - 2)
                    if k == 5 and not first:
                        add_y(pair - 1)
                if last:
                    out_lo(pair, 2)
                    out_lo(pair, 3)
                    add_y(pair)

            dve.wait_ge(s["mask"], 16)
            dve.tensor_scalar(mask[:, :], mask_words[:, :].bitcast(U8), MASKED, None, ALU.mult).then_inc(s["masked"], 1)
            dve.wait_ge(s["c_lo"], NCH)
            context_now(0, 0)
            for m in range(1, GROUPS, 2):
                read_out(0, 0, m, True)
            in_two_pairs(dve, lambda dp, first, last: (one_pair(dp * 2, 0, first, False), one_pair(dp * 2 + 1, 1, False, last)))
            dve.wait_ge(s["added"], PAIRS)


def groups_at(k):
    return ((0,), (1, 2), (3,), (4, 5), (6,), (7, 8), (9,), (10, 11))[k]

STAGES = {"a0": stage_l0_attention, "f0": stage_l0_ffn, "a1": stage_l1_recurrence, "f1": stage_l1_ffn,
          "a2": stage_l2_attention, "f2": stage_l2_ffn, "a3": stage_l3_attention, "f3": stage_l3_ffn}


def build(nc, w, out, stages):
    with ExitStack() as ctx:
        g = Bag()
        g.psum = ctx.enter_context(nc.psum_tensor("psum", [128, 8 * BANK], F32))
        g.x = sb(nc, ctx, "x_rows", T)
        g.ident = sb(nc, ctx, "ident", 128)
        g.ident_b = sb(nc, ctx, "ident_b", 128, BF16)
        g.pick_expert = sb(nc, ctx, "pick_expert", E * 128, BF16, NB3 * E)
        g.zeros_b = sb(nc, ctx, "zeros_b", 128, BF16)
        g.zeros_wide = sb(nc, ctx, "zeros_wide", CH, BF16)
        g.head_rows = sb(nc, ctx, "head_rows", HG)
        g.priority = sb(nc, ctx, "priority", E)
        g.minus_half = sb(nc, ctx, "minus_half", B)
        loaded, ready = ctx.enter_context(nc.semaphore("g_loaded")), ctx.enter_context(nc.semaphore("g_ready"))
        with ExitStack() as first, nc.Block() as block:
            pick_raw = sb(nc, first, "pick_raw", E * 128, rows=NB3 * E)

            @block.sync
            def _(sp):
                sp.dma_start(g.x[:, :].rearrange("p (b d) -> p b d", b=B), w["x"].rearrange("b s d -> s b d")).then_inc(loaded, 16)
                sp.dma_start(g.ident[:, :], w["ident"]).then_inc(loaded, 16)
                sp.dma_start(pick_raw[:, :], w["pick_expert"]).then_inc(loaded, 16)
                sp.dma_start(g.priority[:, :], w["priority"]).then_inc(loaded, 16)
                sp.dma_start(g.head_rows[:, :], w["head_rows"]).then_inc(loaded, 16)
                sp.wait_ge(loaded, 80)

            @block.vector
            def _(dve):
                dve.memset(g.minus_half[:, :], -0.5).then_inc(ready, 1)
                dve.memset(g.zeros_b[:, :], 0.0).then_inc(ready, 1)
                dve.memset(g.zeros_wide[:, :], 0.0).then_inc(ready, 1)
                dve.wait_ge(loaded, 80)
                dve.tensor_copy(g.ident_b[:, :], g.ident[:, :]).then_inc(ready, 1)
                dve.tensor_copy(g.pick_expert[:, :], pick_raw[:, :]).then_inc(ready, 1)
                dve.wait_ge(ready, 5)
        for name in stages:
            with nc.cleanup_on_exit():
                STAGES[name](nc, g, w)
        stored = ctx.enter_context(nc.semaphore("g_stored"))
        with nc.Block() as block:
            @block.sync
            def _(sp):
                sp.dma_start(out.rearrange("b s d -> s b d"), g.x[:, :].rearrange("p (b d) -> p b d", b=B)).then_inc(stored, 16)
                sp.wait_ge(stored, 16)


def layouts(a):
    import numpy as np
    w = {"x": a["x"]}
    w["ident"] = np.eye(128, dtype=np.float32)
    w["pick_expert"] = np.tile(np.repeat(np.eye(E), 128, axis=1), (NB3, 1)).astype(np.float32)
    w["priority"] = np.tile(np.arange(E, 0, -1, dtype=np.float32), (128, 1))

    def blocks(m):
        return m.reshape(-1, 128, m.shape[-1]).transpose(1, 0, 2).reshape(128, -1)

    w["f0_wr"], w["f0_br"] = a["L0_ffn_Wr"].T, a["L0_ffn_br"]
    w["f0_w"] = np.stack([np.concatenate([a["L0_ffn_W1"][e].T, blocks(a["L0_ffn_W2"][e].T),
                                          a["L0_ffn_b1"][e].reshape(FB, 128).T, a["L0_ffn_b2"][e][:, None]], 1) for e in range(E)])
    w["f0_gamma"], w["f0_beta"] = a["L0_ffn_gamma"], a["L0_ffn_beta"]
    w["ctx_t"] = a["ctx_1024"].reshape(T, D).T
    w["a1_w"] = np.concatenate([a["L1_xattn_" + k].T for k in ("Wi", "Wg", "A", "Bm", "Wo")], 1)
    w["a1_bias"] = np.stack([a["L1_xattn_bi"], a["L1_xattn_bg"], a["L1_xattn_bo"],
                             np.repeat(a["L1_xattn_decay"][0, :, 0], D // HEADS)], 1)
    w["head_rows"] = np.tile(np.repeat(np.eye(HG, dtype=np.float32), DH, axis=0), (128 // (HG * DH), 1))
    w["a0_w"] = np.concatenate([a["L0_xattn_Wq"], a["L0_xattn_Wk"], a["L0_xattn_Wv"], blocks(a["L0_xattn_Wo"])], 1)
    w["a0_bo"] = a["L0_xattn_bo"][:, None]
    w["mask"] = a["mask_BxSxS2_bk1"].view(np.int32)
    w["energy"] = a["ctxb_2048x32"]
    for p, k in (("a2_", "L2_xattn_"), ("a3_", "L3_xattn_")):
        def stacked(m):
            return np.tile(m.reshape(-1, NG, 1, HG * DH), (1, 1, 3, 1)).reshape(m.shape[0], -1)
        w[p + "w"] = np.concatenate([stacked(a[k + "Wq"]), stacked(a[k + "Wk"]), a[k + "Wv"], a[k + "Wo"]], 1)
        bias = np.zeros((128, 2 * NG + 1), np.float32)
        bias[:ST, :NG] = stacked(a[k + "bq"][None]).reshape(NG, ST).T
        bias[:ST, NG:2 * NG] = stacked(a[k + "bk"][None]).reshape(NG, ST).T
        bias[:, 2 * NG] = a[k + "bo"]
        w[p + "bias"], w[p + "bv"] = bias, a[k + "bv"]
    w["f3_wr"] = a["L3_ffn_Wr"].T
    w["f3_w"] = np.concatenate([a["L3_ffn_W1"][E - 1], blocks(a["L3_ffn_W2"][E - 1]),
                                a["L3_ffn_b1"][E - 1].reshape(FB, 128).T, a["L3_ffn_b2"][E - 1][:, None]], 1)[None]
    w["f1_wr"] = a["L1_ffn_router_w"].T
    w["f1_w"] = np.concatenate([a["L1_ffn_up_proj"], a["L1_ffn_down_proj"]], 2)
    w["f2_wr"], w["f2_br"] = a["L2_ffn_gate_w"].T, a["L2_ffn_expert_bias"]
    rows = np.zeros((E, -(-HIDDEN2 // 128) * 128, D), np.float32)
    rows[:, :HIDDEN2] = a["L2_ffn_w2"]
    w["f2_w"] = np.stack([np.concatenate([a["L2_ffn_w1"][e], a["L2_ffn_w3"][e], blocks(rows[e])], 1) for e in range(E)])
    return w


def kernel(**inputs):
    import numpy as np
    from concourse import bacc
    from concourse.bass_utils import run_bass_kernel_spmd

    w = {k: np.ascontiguousarray(v) for k, v in layouts({k: np.asarray(v) for k, v in inputs.items()}).items()}
    nc = bacc.Bacc("TRN2", target_bir_lowering=False, num_devices=1)
    aps = {k: nc.dram_tensor(f"in_{k}", v.shape, mybir.dt.from_np(v.dtype), kind="ExternalInput").ap() for k, v in w.items()}
    out = nc.dram_tensor("out_x", (B, S, D), F32, kind="ExternalOutput").ap()
    build(nc, aps, out, list(STAGES))
    r = run_bass_kernel_spmd(nc, [{f"in_{k}": v for k, v in w.items()}], core_ids=[0])
    return r.results[0]["out_x"]
```

```python
from contextlib import ExitStack

import concourse.bass as bass
from concourse import mybir

ALU = mybir.AluOpType
ACT = mybir.ActivationFunctionType
AX = mybir.AxisListType
F32 = mybir.dt.float32
F32R = mybir.dt.float32r
BF16 = mybir.dt.bfloat16
U8 = mybir.dt.uint8
I32 = mybir.dt.int32
ds = bass.ds

B, S, D = 16, 128, 128
T = B * S
E = 8
CH = 512
NCH = T // CH
TPC = CH // S
BANK = 512
EPS = 1e-5
BIG = 1e30
NB3 = 3
HEADS = 16


class Bag:
    pass



def sb(nc, ctx, name, cols, dt=F32, rows=128):
    return ctx.enter_context(nc.sbuf_tensor(name, [rows, cols], dt))


def sems(nc, prefix, names):
    bag = {}
    for n in names.split():
        bag[n] = nc.alloc_semaphore(name=prefix + n)
    return bag


def bank(g, k, n=1):
    return g.psum[:, k * BANK:(k + n) * BANK]


def floor0(count):
    return max(count, 0) if isinstance(count, int) else count


def product3(pe, out, w_hi, w_lo, m_hi, m_lo, first=True, last=True):
    pe.matmul(out, w_hi, m_hi, start=first, stop=False)
    pe.matmul(out, w_hi, m_lo, start=False, stop=False)
    return pe.matmul(out, w_lo, m_hi, start=False, stop=last)


def ln_alloc(nc, ctx, p):
    n = Bag()
    n.stats = sb(nc, ctx, p + "ln_stats", 6 * B)
    n.mv = sb(nc, ctx, p + "ln_mv", 2 * B)
    n.var = sb(nc, ctx, p + "ln_var", B)
    n.rstd = sb(nc, ctx, p + "ln_rstd", B)
    n.rows = sb(nc, ctx, p + "ln_rows", T)
    n.hi = sb(nc, ctx, p + "xn_hi", T, F32R)
    n.lo = sb(nc, ctx, p + "xn_lo", T, F32R)
    n.sem = sems(nc, p + "ln_", "stats_done aggr_done var_ready rstd_ready rows_ready turned hi_ready lo_ready")
    return n


def ln_stats_vector(dve, n, src, c):
    for t in range(c * TPC, (c + 1) * TPC):
        dve.bn_stats(n.stats[:, t * 6:t * 6 + 6], src[:, t * D:(t + 1) * D]).then_inc(n.sem["stats_done"], 1)
    dve.wait_ge(n.sem["stats_done"], (c + 1) * TPC)
    for t in range(c * TPC, (c + 1) * TPC):
        dve.bn_aggr(n.mv[:, t * 2:t * 2 + 2], n.stats[:, t * 6:t * 6 + 6]).then_inc(n.sem["aggr_done"], 1)
    dve.wait_ge(n.sem["aggr_done"], (c + 1) * TPC)
    dve.tensor_scalar(n.var[:, c * TPC:(c + 1) * TPC], n.mv[:, c * 2 * TPC:(c + 1) * 2 * TPC].rearrange("p (t s) -> p t s", s=2)[:, :, 1],
                      EPS, None, ALU.add).then_inc(n.sem["var_ready"], 1)


def ln_scale_vector(dve, n, src, c):
    dve.wait_ge(n.sem["rstd_ready"], c + 1)
    for t in range(c * TPC, (c + 1) * TPC):
        dve.tensor_scalar(n.rows[:, t * D:(t + 1) * D], src[:, t * D:(t + 1) * D], n.mv[:, t * 2:t * 2 + 1],
                          n.rstd[:, t:t + 1], ALU.subtract, ALU.mult).then_inc(n.sem["rows_ready"], 1)


def ln_rows_vector(dve, g, n, src):
    ln_stats_vector(dve, n, src, 0)
    ln_stats_vector(dve, n, src, 1)
    for c in range(2, NCH):
        ln_stats_vector(dve, n, src, c)
        ln_scale_vector(dve, n, src, c - 2)
    ln_scale_vector(dve, n, src, NCH - 2)
    ln_scale_vector(dve, n, src, NCH - 1)


def ln_gpsimd(pool, g, n):
    for c in range(NCH):
        t = slice(c * TPC, (c + 1) * TPC)
        pool.wait_ge(n.sem["var_ready"], c + 1)
        pool.tensor_tensor(n.rstd[:, t], n.var[:, t], g.minus_half[:, t], ALU.pow).then_inc(n.sem["rstd_ready"], 1)


def ln_tensor(pe, g, n):
    for c in range(NCH):
        pe.wait_ge(n.sem["rows_ready"], TPC * (c + 1))
        for j in range(TPC):
            t = c * TPC + j
            last = pe.transpose(bank(g, c)[:, j * D:(j + 1) * D], n.rows[:, t * D:(t + 1) * D], g.ident[:, :])
        last.then_inc(n.sem["turned"], 1)


def ln_scalar(act, g, n, whole=None):
    for c in range(NCH):
        act.wait_ge(n.sem["turned"], c + 1)
        if whole is not None:
            act.activation(whole[:, c * CH:(c + 1) * CH], bank(g, c), ACT.Copy)
        act.activation(n.hi[:, c * CH:(c + 1) * CH], bank(g, c), ACT.Copy).then_inc(n.sem["hi_ready"], 1)


def ln_lo_vector(dve, g, n):
    for c in range(NCH):
        dve.wait_ge(n.sem["hi_ready"], c + 1)
        dve.tensor_tensor(n.lo[:, c * CH:(c + 1) * CH], bank(g, c), n.hi[:, c * CH:(c + 1) * CH].bitcast(F32),
                          ALU.subtract).then_inc(n.sem["lo_ready"], 1)


def router_alloc(nc, ctx, p):
    def per_expert(name, dt=F32):
        return sb(nc, ctx, p + "rt_" + name, B * E, dt)

    def per_token(name):
        return sb(nc, ctx, p + "rt_" + name, B)

    m = Bag()
    m.raw = sb(nc, ctx, p + "rt_raw", E)
    m.w_both = sb(nc, ctx, p + "rt_w_both", 2 * E, F32R)
    m.bias = sb(nc, ctx, p + "rt_bias", E)
    m.logit = per_expert("logit")
    m.score = per_expert("score")
    m.eq = per_expert("eq")
    m.oh1 = per_expert("oh1")
    m.oh2 = per_expert("oh2")
    m.rest = per_expert("rest")
    m.gate = per_expert("gate")
    m.prob = per_expert("prob")
    m.top1 = per_token("top1")
    m.top2 = per_token("top2")
    m.pick = per_token("pick")
    m.diff = per_token("diff")
    m.ratio = per_token("ratio")
    m.w1 = per_token("w1")
    m.w2 = per_token("w2")
    m.den = per_token("den")
    m.gate3 = sb(nc, ctx, p + "gate3", B * NB3 * E, BF16)
    m.wide = [sb(nc, ctx, f"{p}gate_wide{i}", CH) for i in range(2)]
    m.sem = sems(nc, p + "rt_", "loaded w_hi w_lo logits step diff expd gate3 turned copied wide wide_used copied0 copied1")
    return m


def router_sync(sp, r, w_dram, bias_dram):
    sp.dma_start(r.raw[:, :], w_dram).then_inc(r.sem["loaded"], 16)
    if bias_dram is not None:
        sp.dma_start(r.bias[:, :], bias_dram.partition_broadcast(128)).then_inc(r.sem["loaded"], 16)


def router_split_vector(dve, r, has_bias):
    s = r.sem
    dve.wait_ge(s["loaded"], 32 if has_bias else 16)
    dve.tensor_copy(r.w_both[:, 0:E], r.raw[:, :]).then_inc(s["w_hi"], 1)
    dve.wait_ge(s["w_hi"], 1)
    dve.tensor_tensor(r.w_both[:, E:2 * E], r.raw[:, :], r.w_both[:, 0:E].bitcast(F32), ALU.subtract).then_inc(s["w_lo"], 1)


def router_tensor(pe, g, n, r, where):
    pe.wait_ge(r.sem["w_lo"], 1)
    for t in range(B):
        if t % TPC == 0:
            pe.wait_ge(n.sem["lo_ready"], t // TPC + 1)
        tok = slice(t * D, (t + 1) * D)
        out = bank(g, where)[:, t * 2 * E:(t + 1) * 2 * E]
        pe.matmul(out, n.hi[:, tok], r.w_both[:, :], start=True, stop=False, skip_group_check=True)
        last = pe.matmul(out[:, 0:E], n.lo[:, tok], r.w_both[:, 0:E], start=False, stop=True, skip_group_check=True)
    last.then_inc(r.sem["logits"], 1)


def by_expert(a):
    return a[:, 0:B * E].rearrange("p (t e) -> p t e", e=E)


def over_experts(a):
    return a[:, 0:B].unsqueeze(2).to_broadcast([128, B, E])


def over_tokens(a):
    return a[:, 0:E].unsqueeze(1).to_broadcast([128, B, E])


def router_pick(link, dve, g, r, score, top, onehot):
    link(dve.tensor_reduce(top[:, :], by_expert(score), AX.X, ALU.max))
    link(dve.tensor_tensor(by_expert(r.eq), by_expert(score), over_experts(top), ALU.is_ge))
    link(dve.tensor_tensor(by_expert(r.eq), by_expert(r.eq), over_tokens(g.priority), ALU.mult))
    link(dve.tensor_reduce(r.pick[:, :], by_expert(r.eq), AX.X, ALU.max))
    link(dve.tensor_tensor(by_expert(onehot), by_expert(r.eq), over_experts(r.pick), ALU.is_equal))


def router_vector(dve, g, r, kind, where):
    s = r.sem
    count = [0]

    def link(ins):
        count[0] += 1
        ins.then_inc(s["step"], 1)
        dve.wait_ge(s["step"], count[0])

    dve.wait_ge(s["logits"], 1)
    parts = bank(g, where)[:, 0:2 * B * E].rearrange("p (t n e) -> p n t e", n=2, e=E)
    if kind == "pair_bias":
        link(dve.tensor_tensor(by_expert(r.logit), parts[:, 1], over_tokens(r.bias), ALU.add))
    else:
        link(dve.tensor_copy(by_expert(r.logit), parts[:, 1]))
    link(dve.tensor_tensor(by_expert(r.logit), by_expert(r.logit), parts[:, 0], ALU.add))
    score = r.logit
    if kind in ("bias", "all"):
        link(dve.tensor_reduce(r.top1[:, :], by_expert(r.logit), AX.X, ALU.max))
        dve.tensor_tensor(by_expert(r.rest), by_expert(r.logit), over_experts(r.top1),
                          ALU.subtract).then_inc(s["diff"], 1)
        dve.wait_ge(s["expd"], 1)
        link(dve.tensor_reduce(r.den[:, :], by_expert(r.prob), AX.X, ALU.add))
        link(dve.reciprocal(r.w1[:, :], r.den[:, :]))
        link(dve.tensor_tensor(by_expert(r.prob), by_expert(r.prob), over_experts(r.w1), ALU.mult))
        if kind == "bias":
            link(dve.tensor_tensor(by_expert(r.score), by_expert(r.prob), over_tokens(r.bias), ALU.add))
            score = r.score
    if kind == "all":
        link(dve.tensor_copy(r.gate[:, :], r.prob[:, :]))
        split_gate(link, dve, r)
        return
    router_pick(link, dve, g, r, score, r.top1, r.oh1)
    link(dve.scalar_tensor_tensor(out=r.rest[:, :], in0=r.oh1[:, :], scalar=-BIG, in1=score[:, :],
                                  op0=ALU.mult, op1=ALU.add))
    router_pick(link, dve, g, r, r.rest, r.top2, r.oh2)
    if kind == "bias":
        link(dve.tensor_tensor(r.oh1[:, :], r.oh1[:, :], r.oh2[:, :], ALU.add))
        link(dve.tensor_tensor(r.gate[:, :], r.oh1[:, :], r.prob[:, :], ALU.mult))
    else:
        dve.tensor_tensor(r.diff[:, :], r.top2[:, :], r.top1[:, :], ALU.subtract).then_inc(s["diff"], 1)
        dve.wait_ge(s["expd"], 1)
        link(dve.tensor_scalar(r.den[:, :], r.ratio[:, :], 1.0, None, ALU.add))
        link(dve.reciprocal(r.w1[:, :], r.den[:, :]))
        link(dve.tensor_tensor(r.w2[:, :], r.w1[:, :], r.ratio[:, :], ALU.mult))
        link(dve.tensor_tensor(by_expert(r.oh1), by_expert(r.oh1), over_experts(r.w1), ALU.mult))
        link(dve.tensor_tensor(by_expert(r.oh2), by_expert(r.oh2), over_experts(r.w2), ALU.mult))
        link(dve.tensor_tensor(r.gate[:, :], r.oh1[:, :], r.oh2[:, :], ALU.add))
    split_gate(link, dve, r)


def split_gate(link, dve, r):
    parts = r.gate3[:, :].rearrange("p (t n e) -> p n t e", n=NB3, e=E)
    link(dve.tensor_copy(parts[:, 0], by_expert(r.gate)))
    link(dve.tensor_tensor(by_expert(r.rest), by_expert(r.gate), parts[:, 0], ALU.subtract))
    link(dve.tensor_copy(parts[:, 1], by_expert(r.rest)))
    link(dve.tensor_tensor(by_expert(r.eq), by_expert(r.rest), parts[:, 1], ALU.subtract))
    dve.tensor_copy(parts[:, 2], by_expert(r.eq)).then_inc(r.sem["gate3"], 1)


def router_scalar(act, r, kind):
    act.wait_ge(r.sem["diff"], 1)
    if kind in ("bias", "all"):
        act.activation(r.prob[:, :], r.rest[:, :], ACT.Exp).then_inc(r.sem["expd"], 1)
    else:
        act.activation(r.ratio[:, :], r.diff[:, :], ACT.Exp).then_inc(r.sem["expd"], 1)


GATE0 = 6


def turn_gates_tensor(pe, g, r):
    pe.wait_ge(r.sem["gate3"], 1)
    for t in range(B):
        out = bank(g, GATE0 + t // 8).bitcast(BF16)[0:NB3 * E, (t % 8) * D:(t % 8 + 1) * D]
        last = pe.transpose(out, r.gate3[:, t * NB3 * E:(t + 1) * NB3 * E], g.ident_b[:, :])
    last.then_inc(r.sem["turned"], 1)


def turn_gates_vector(dve, g, r):
    dve.wait_ge(r.sem["turned"], 1)
    for k in range(2):
        dve.tensor_copy(g.gate_t[0:NB3 * E, k * 8 * D:(k + 1) * 8 * D],
                        bank(g, GATE0 + k).bitcast(BF16)[0:NB3 * E, :]).then_inc(r.sem["copied"], 1)


def widen_tensor(pe, g, r, expert, c, free, count):
    pe.wait_ge(r.sem["copied"], 2)
    pe.wait_ge(free, count)
    pe.matmul(bank(g, GATE0 + c % 2), g.pick_expert[:, ds(expert * 128, 128)], g.gate_t[:, c * CH:(c + 1) * CH],
              start=True, stop=True).then_inc(r.sem["wide"], 1)


def add_alloc(nc, ctx, p):
    a = Bag()
    a.sem = sems(nc, p + "add_", "turned added")
    return a


def add_tensor(pe, g, a, acc, ready):
    for c in range(NCH):
        for sem, count in ready(c):
            pe.wait_ge(sem, count)
        for j in range(TPC):
            t = c * TPC + j
            last = pe.transpose(bank(g, c)[:, j * D:(j + 1) * D], acc[:, t * D:(t + 1) * D], g.ident[:, :])
        last.then_inc(a.sem["turned"], 1)


def add_vector(dve, g, a, out, base):
    for c in range(NCH):
        tok = slice(c * CH, (c + 1) * CH)
        dve.wait_ge(a.sem["turned"], c + 1)
        dve.tensor_tensor(out[:, tok], bank(g, c), base[:, tok], ALU.add).then_inc(a.sem["added"], 1)
def steps_of(ep, n_experts):
    return [(ep, i, c) for i in range(min(2, n_experts)) for c in range(NCH)]


def next_step(ep, i, c):
    return (ep, i, c + 1) if c < NCH - 1 else (ep, 1, 0) if i == 0 else (ep + 1, 0, 0)


def ahead(step, k, n_experts, last):
    if last and steps_of(step[0], n_experts).index(step) + k >= min(2, n_experts) * NCH:
        return None
    for _ in range(k):
        step = next_step(*step)
    return step


def index(ep, i, c):
    return ep * (2 * NCH) + (i * NCH + c)


def turn(ep, i, c):
    return ep * NCH + (i * (NCH // 2) + c // 2)


def over_experts_loop(eng, n_experts, body):
    if n_experts > 2:
        with eng.Fori(0, n_experts // 2 - 1) as ep:
            body(ep, False)
        body(n_experts // 2 - 1, True)
    else:
        body(0, True)


def load_expert_weights(sp, s, raw, dram, n_experts):
    def load(ep, i):
        sp.wait_ge(s[f"w_lo{i}"], ep)
        sp.dma_start(raw[i][:, :], dram[ds(ep * 2 + i, 1)].rearrange("o p n -> p (o n)")).then_inc(s[f"raw{i}"], 16)

    if n_experts == 1:
        load(0, 0)
        return
    with sp.Fori(0, n_experts // 2) as ep:
        for i in range(2):
            load(ep, i)


def split_weights_hi(dve, s, w_hi, raw, ep, i, bias=None):
    dve.wait_ge(s[f"raw{i}"], 16 * (ep + 1))
    if i or not isinstance(ep, int) or ep:
        dve.wait_ge(s["down1"], ep * NCH + (2 * i - 2))
    words = w_hi[i].shape[1]
    if bias is not None:
        if i or not isinstance(ep, int) or ep:
            dve.wait_ge(s["part1"], ep * NCH + (2 * i - 2))
        dve.tensor_copy(bias[i][:, :], raw[i][:, words:]).then_inc(s[f"bias{i}"], 1)
    dve.tensor_copy(w_hi[i][:, :], raw[i][:, 0:words]).then_inc(s[f"w_hi{i}"], 1)


def split_weights_lo(pool, s, w_hi, w_lo, raw, ep, i):
    pool.wait_ge(s[f"w_hi{i}"], ep + 1)
    pool.tensor_tensor(w_lo[i][:, :], raw[i][:, 0:w_hi[i].shape[1]], w_hi[i][:, :].bitcast(F32),
                       ALU.subtract).then_inc(s[f"w_lo{i}"], 1)


FB = 4
W_DENSE = 2 * FB * D
OUT0 = 4


def dense_alloc(nc, ctx, p, n_experts):
    two = range(2)
    m = Bag()
    m.raw = [sb(nc, ctx, f"{p}raw{i}", W_DENSE + FB + 1) for i in two]
    m.w_hi = [sb(nc, ctx, f"{p}w_hi{i}", W_DENSE, F32R) for i in two]
    m.w_lo = [sb(nc, ctx, f"{p}w_lo{i}", W_DENSE, F32R) for i in two]
    m.h = [sb(nc, ctx, f"{p}h{i}", FB * CH) for i in two]
    m.h_hi = [sb(nc, ctx, f"{p}h_hi{i}", FB * CH, F32R) for i in two]
    m.h_lo = [sb(nc, ctx, f"{p}h_lo{i}", FB * CH, F32R) for i in two]
    m.part = [sb(nc, ctx, f"{p}part{i}", CH) for i in two]
    m.acc = sb(nc, ctx, p + "acc", T)
    m.bias = [sb(nc, ctx, f"{p}bias{i}", FB + 1) for i in two]
    m.sem = sems(nc, p, "bias0 bias1 raw0 raw1 w_hi0 w_hi1 w_lo0 w_lo1 up act0 act1 act2 act3 "
                             "h_hi h_lo0 h_lo1 down0 down1 part0 part1 zeroed acc0 acc1")
    return m


def dense_tensor(pe, g, n, r, m, n_experts, first_gate):
    s = m.sem

    def up(ep, i, c):
        pe.wait_ge(s[f"w_lo{i}"], ep + 1)
        for f in range(FB):
            pe.wait_ge(s[f"act{f}"], index(ep, i, c))
            w = slice(f * D, (f + 1) * D)
            tok = slice(c * CH, (c + 1) * CH)
            product3(pe, bank(g, f), m.w_hi[i][:, w], m.w_lo[i][:, w], n.hi[:, tok], n.lo[:, tok]).then_inc(s["up"], 1)

    def down(ep, i, c):
        q = c % 2
        pe.wait_ge(s[f"part{q}"], turn(ep, i, c))
        for f in range(FB):
            pe.wait_ge(s[f"h_lo{q}"], turn(ep, i, c) * FB + (f + 1))
            w = slice((FB + f) * D, (FB + f + 1) * D)
            h = slice(f * CH, (f + 1) * CH)
            last = product3(pe, bank(g, OUT0 + q), m.w_hi[i][:, w], m.w_lo[i][:, w], m.h_hi[q][:, h],
                            m.h_lo[q][:, h], first=f == 0, last=f == FB - 1)
        last.then_inc(s[f"down{q}"], 1)

    def body(ep, last):
        steps = steps_of(ep, n_experts)
        for step in steps:
            if not (last and step == steps[-1]):
                up(*next_step(*step))
            down(*step)
            _, i, c = step
            widen_tensor(pe, g, r, ep * 2 + (i + first_gate), c, r.sem[f"copied{c % 2}"], turn(*step))

    up(0, 0, 0)
    turn_gates_tensor(pe, g, r)
    over_experts_loop(pe, n_experts, body)


def dense_scalar(act, g, m, func, n_experts):
    s = m.sem

    def activate(ep, i, c, f):
        q = c % 2
        act.wait_ge(s["up"], index(ep, i, c) * FB + (f + 1))
        if f == 0:
            act.wait_ge(s[f"h_lo{q}"], turn(ep, i, c) * FB)
        if f == 0 and c == 0:
            act.wait_ge(s[f"bias{i}"], ep + 1)
        act.activation(m.h[q][:, f * CH:(f + 1) * CH], bank(g, f), func,
                       bias=m.bias[i][:, f:f + 1]).then_inc(s[f"act{f}"], 1)

    def split_hi(ep, i, c, f):
        q = c % 2
        if f == 0:
            act.wait_ge(s[f"down{q}"], turn(ep, i, c))
        act.wait_ge(s[f"act{f}"], index(ep, i, c) + 1)
        h = slice(f * CH, (f + 1) * CH)
        act.activation(m.h_hi[q][:, h], m.h[q][:, h], ACT.Copy).then_inc(s["h_hi"], 1)

    def body(ep, last):
        for step in steps_of(ep, n_experts):
            activate(*step, 0)
            for f in range(1, FB):
                activate(*step, f)
                split_hi(*step, f - 1)
            split_hi(*step, FB - 1)

    over_experts_loop(act, n_experts, body)


def dense_vector(dve, g, r, m, n_experts, kind, where):
    s = m.sem

    def split_lo(ep, i, c):
        q = c % 2
        for f in range(FB):
            dve.wait_ge(s["h_hi"], index(ep, i, c) * FB + (f + 1))
            h = slice(f * CH, (f + 1) * CH)
            dve.tensor_tensor(m.h_lo[q][:, h], m.h[q][:, h], m.h_hi[q][:, h].bitcast(F32),
                              ALU.subtract).then_inc(s[f"h_lo{q}"], 1)

    def copy_gate(ep, i, c):
        q = c % 2
        dve.wait_ge(r.sem["wide"], index(ep, i, c) + 1)
        dve.wait_ge(s[f"part{q}"], turn(ep, i, c))
        dve.tensor_copy(r.wide[q][:, :], bank(g, GATE0 + q)).then_inc(r.sem[f"copied{q}"], 1)

    def gated(ep, i, c):
        q = c % 2
        if c == 0:
            dve.wait_ge(s[f"bias{i}"], ep + 1)
        dve.wait_ge(s[f"down{q}"], turn(ep, i, c) + 1)
        dve.wait_ge(r.sem[f"copied{q}"], turn(ep, i, c) + 1)
        dve.wait_ge(s[f"acc{q}"], turn(ep, i, c))
        dve.scalar_tensor_tensor(out=m.part[q][:, :], in0=bank(g, OUT0 + q), scalar=m.bias[i][:, FB:FB + 1],
                                 in1=r.wide[q][:, :],
                                 op0=ALU.add, op1=ALU.mult).then_inc(s[f"part{q}"], 1)

    def body(ep, last):
        steps = steps_of(ep, n_experts)
        for step in steps:
            _, i, c = step
            if not (last and step == steps[-1]):
                split_lo(*next_step(*step))
            if c == 1 and i == 0 and n_experts > 1:
                split_weights_hi(dve, s, m.w_hi, m.raw, ep, 1, m.bias)
            if c == 1 and i == 1 and not last:
                split_weights_hi(dve, s, m.w_hi, m.raw, ep + 1, 0, m.bias)
            copy_gate(*step)
            gated(*step)

    router_vector(dve, g, r, kind, where)
    turn_gates_vector(dve, g, r)
    split_lo(0, 0, 0)
    over_experts_loop(dve, n_experts, body)


def start_gpsimd(pool, g, n, m):
    pool.memset(m.acc[:, :], 0.0).then_inc(m.sem["zeroed"], 1)
    ln_gpsimd(pool, g, n)
    split_weights_lo(pool, m.sem, m.w_hi, m.w_lo, m.raw, 0, 0)


def dense_gpsimd(pool, m, n_experts):
    s = m.sem

    def accumulate(ep, i, c):
        q = c % 2
        pool.wait_ge(s[f"part{q}"], turn(ep, i, c) + 1)
        pool.wait_ge(s[f"acc{q}"], turn(ep, i, c))
        tok = slice(c * CH, (c + 1) * CH)
        pool.tensor_tensor(m.acc[:, tok], m.acc[:, tok], m.part[q][:, :], ALU.add).then_inc(s[f"acc{q}"], 1)

    def body(ep, last):
        for step in steps_of(ep, n_experts):
            _, i, c = step
            if c == 1 and i == 0 and n_experts > 1:
                split_weights_lo(pool, s, m.w_hi, m.w_lo, m.raw, ep, 1)
            if c == 1 and i == 1 and not last:
                split_weights_lo(pool, s, m.w_hi, m.w_lo, m.raw, ep + 1, 0)
            accumulate(*step)

    pool.wait_ge(s["zeroed"], 1)
    over_experts_loop(pool, n_experts, body)


def sums_of(m, n_experts):
    return lambda c: [(m.sem[f"acc{c % 2}"], 2 * n_experts - 1 + c // 2)]


def stage_l0_ffn(nc, g, w):
    p = "f0_"
    with ExitStack() as ctx:
        n, r, a = ln_alloc(nc, ctx, p), router_alloc(nc, ctx, p), add_alloc(nc, ctx, p)
        m = dense_alloc(nc, ctx, p, E)
        gamma, beta = sb(nc, ctx, p + "gamma", D), sb(nc, ctx, p + "beta", D)
        s = sems(nc, p, "affine x_beta scaled summed")
        z = Bag()
        z.stats, z.mv, z.var, z.rstd, z.rows = n.stats, n.mv, n.var, n.rstd, n.rows
        z.sem = sems(nc, p + "z_", "stats_done aggr_done var_ready rstd_ready rows_ready")
        block = ctx.enter_context(nc.Block())

        @block.sync
        def _(sp):
            router_sync(sp, r, w["f0_wr"], w["f0_br"])
            sp.dma_start(gamma[:, :], w["f0_gamma"].partition_broadcast(128)).then_inc(s["affine"], 16)
            sp.dma_start(beta[:, :], w["f0_beta"].partition_broadcast(128)).then_inc(s["affine"], 16)
            load_expert_weights(sp, m.sem, m.raw, w["f0_w"], E)

        @block.gpsimd
        def _(pool):
            start_gpsimd(pool, g, n, m)
            pool.wait_ge(s["affine"], 32)
            pool.wait_ge(n.sem["rows_ready"], B)
            x = g.x[:, :].rearrange("p (t d) -> p t d", d=D)
            pool.tensor_tensor(x, x, beta[:, :].unsqueeze(1).to_broadcast([128, B, D]), ALU.add).then_inc(s["x_beta"], 1)
            dense_gpsimd(pool, m, E)
            ln_gpsimd(pool, g, z)

        @block.tensor
        def _(pe):
            ln_tensor(pe, g, n)
            router_tensor(pe, g, n, r, GATE0)
            dense_tensor(pe, g, n, r, m, E, 0)
            add_tensor(pe, g, a, m.acc, sums_of(m, E))

        @block.scalar
        def _(act):
            ln_scalar(act, g, n)
            router_scalar(act, r, "pair_bias")
            dense_scalar(act, g, m, ACT.Relu, E)

        @block.vector
        def _(dve):
            ln_rows_vector(dve, g, n, g.x)
            router_split_vector(dve, r, True)
            split_weights_hi(dve, m.sem, m.w_hi, m.raw, 0, 0, m.bias)
            ln_lo_vector(dve, g, n)
            dense_vector(dve, g, r, m, E, "pair_bias", GATE0)

            def affine(c):
                tok = slice(c * CH, (c + 1) * CH)
                rows = n.rows[:, tok].rearrange("p (t d) -> p t d", d=D)
                ln_scale_vector(dve, z, n.rows, c)
                dve.wait_ge(z.sem["rows_ready"], (c + 1) * TPC)
                dve.tensor_tensor(rows, rows, gamma[:, :].unsqueeze(1).to_broadcast([128, TPC, D]), ALU.mult).then_inc(s["scaled"], 1)
                dve.wait_ge(s["scaled"], c + 1)
                dve.tensor_tensor(g.x[:, tok], g.x[:, tok], n.rows[:, tok], ALU.add).then_inc(s["summed"], 1)

            dve.wait_ge(s["affine"], 32)
            dve.wait_ge(s["x_beta"], 1)
            for c in range(NCH):
                tok = slice(c * CH, (c + 1) * CH)
                dve.wait_ge(a.sem["turned"], c + 1)
                dve.tensor_tensor(n.rows[:, tok], bank(g, c), n.rows[:, tok], ALU.add).then_inc(a.sem["added"], 1)
                dve.wait_ge(a.sem["added"], c + 1)
                ln_stats_vector(dve, z, n.rows, c)
                if c:
                    affine(c - 1)
            affine(NCH - 1)
            dve.wait_ge(s["summed"], NCH)


def stage_l3_ffn(nc, g, w):
    p = "f3_"
    with ExitStack() as ctx:
        n, r, a = ln_alloc(nc, ctx, p), router_alloc(nc, ctx, p), add_alloc(nc, ctx, p)
        m = dense_alloc(nc, ctx, p, 1)
        block = ctx.enter_context(nc.Block())

        @block.sync
        def _(sp):
            router_sync(sp, r, w["f3_wr"], None)
            load_expert_weights(sp, m.sem, m.raw, w["f3_w"], 1)

        @block.gpsimd
        def _(pool):
            start_gpsimd(pool, g, n, m)
            dense_gpsimd(pool, m, 1)

        @block.tensor
        def _(pe):
            ln_tensor(pe, g, n)
            router_tensor(pe, g, n, r, GATE0)
            dense_tensor(pe, g, n, r, m, 1, E - 1)
            add_tensor(pe, g, a, m.acc, sums_of(m, 1))

        @block.scalar
        def _(act):
            ln_scalar(act, g, n)
            router_scalar(act, r, "all")
            dense_scalar(act, g, m, ACT.Gelu, 1)

        @block.vector
        def _(dve):
            ln_rows_vector(dve, g, n, g.x)
            router_split_vector(dve, r, False)
            split_weights_hi(dve, m.sem, m.w_hi, m.raw, 0, 0, m.bias)
            ln_lo_vector(dve, g, n)
            dense_vector(dve, g, r, m, 1, "all", GATE0)
            add_vector(dve, g, a, g.x, g.x)
            dve.wait_ge(a.sem["added"], NCH)


def gated_alloc(nc, ctx, p, hidden, gate_input):
    two = range(2)
    m = Bag()
    m.hidden, m.gate_input = hidden, gate_input
    m.sizes = [min(128, hidden - k) for k in range(0, hidden, 128)]
    nb = m.nb = len(m.sizes)
    m.lead = 1 if gate_input else 2
    m.split_at = 1 if gate_input else 0
    words = 2 * hidden + nb * D
    m.raw = [sb(nc, ctx, f"{p}raw{i}", words) for i in two]
    m.w_hi = [sb(nc, ctx, f"{p}w_hi{i}", words, F32R) for i in two]
    m.w_lo = [sb(nc, ctx, f"{p}w_lo{i}", words, F32R) for i in two]
    m.silu = [sb(nc, ctx, f"{p}silu{i}", CH) for i in two]
    m.h = [sb(nc, ctx, f"{p}h{i}", nb * CH) for i in two]
    m.h_hi = [sb(nc, ctx, f"{p}h_hi{i}", nb * CH, F32R) for i in two]
    m.h_lo = [sb(nc, ctx, f"{p}h_lo{i}", nb * CH, F32R) for i in two]
    m.part = [sb(nc, ctx, f"{p}part{i}", CH) for i in two]
    if gate_input:
        m.x = [sb(nc, ctx, f"{p}xg{i}", CH) for i in two]
        m.x_hi = [sb(nc, ctx, f"{p}xg_hi{i}", CH, F32R) for i in two]
        m.x_lo = [sb(nc, ctx, f"{p}xg_lo{i}", CH, F32R) for i in two]
        m.x_all = sb(nc, ctx, p + "x_all", T)
    m.acc = sb(nc, ctx, p + "acc", T)
    m.sem = sems(nc, p, "raw0 raw1 w_hi0 w_hi1 w_lo0 w_lo1 up silu used0 used1 h_hi h_lo0 h_lo1 down0 down1 "
                        "x0 x1 x_hi0 x_hi1 x_lo0 x_lo1 part0 part1 acc0 acc1 zeroed")
    return m


def gated_tensor(pe, g, n, r, m):
    s, nb = m.sem, m.nb

    def up(ep, i, c):
        pe.wait_ge(s[f"w_lo{i}"], ep + 1)
        q = c % 2
        if m.gate_input:
            pe.wait_ge(s[f"x_lo{q}"], turn(ep, i, c) + 1)
            x_hi, x_lo = m.x_hi[q][:, :], m.x_lo[q][:, :]
        else:
            x_hi, x_lo = n.hi[:, c * CH:(c + 1) * CH], n.lo[:, c * CH:(c + 1) * CH]
        for j, size in enumerate(m.sizes):
            k = (i * NCH + c) * nb + j
            pe.wait_ge(s[f"used{k % 2}"], ep * (nb * NCH) + k // 2)
            for half in range(2):
                cols = slice(half * m.hidden + j * 128, half * m.hidden + j * 128 + size)
                last = product3(pe, bank(g, 2 * (k % 2) + half)[0:size, :], m.w_hi[i][:, cols], m.w_lo[i][:, cols],
                                x_hi, x_lo)
            last.then_inc(s["up"], 1)

    def down(ep, i, c):
        q = c % 2
        pe.wait_ge(s[f"acc{q}"] if m.gate_input else s[f"part{q}"], turn(ep, i, c))
        for j, size in enumerate(m.sizes):
            pe.wait_ge(s[f"h_lo{q}"], turn(ep, i, c) * nb + (j + 1))
            cols = slice(2 * m.hidden + j * D, 2 * m.hidden + (j + 1) * D)
            h = slice(j * CH, (j + 1) * CH)
            last = product3(pe, bank(g, OUT0 + q), m.w_hi[i][0:size, cols], m.w_lo[i][0:size, cols], m.h_hi[q][0:size, h],
                            m.h_lo[q][0:size, h], first=j == 0, last=j == nb - 1)
        last.then_inc(s[f"down{q}"], 1)

    def widen(ep, i, c):
        free = s[f"x{c % 2}"] if m.gate_input else r.sem[f"copied{c % 2}"]
        widen_tensor(pe, g, r, ep * 2 + i, c, free, turn(ep, i, c))

    def body(ep, last):
        for step in steps_of(ep, E):
            to_widen, to_raise = ahead(step, 2, E, last), ahead(step, m.lead, E, last)
            if m.gate_input and to_widen:
                widen(*to_widen)
            if to_raise:
                up(*to_raise)
            down(*step)
            if not m.gate_input:
                widen(*step)

    if m.gate_input:
        turn_gates_tensor(pe, g, r)
        widen(0, 0, 0)
        widen(0, 0, 1)
        up(0, 0, 0)
    else:
        up(0, 0, 0)
        up(0, 0, 1)
        turn_gates_tensor(pe, g, r)
    over_experts_loop(pe, E, body)


def gated_scalar(act, g, r, m, kind):
    s, nb = m.sem, m.nb

    def silu(ep, i, c, j):
        k = (i * NCH + c) * nb + j
        size = m.sizes[j]
        act.wait_ge(s["up"], ep * (2 * nb * NCH) + k + 1)
        act.wait_ge(s[f"used{k % 2}"], ep * (nb * NCH) + k // 2)
        act.activation(m.silu[k % 2][0:size, :], bank(g, 2 * (k % 2))[0:size, :], ACT.Silu).then_inc(s["silu"], 1)

    def split_hi(ep, i, c, j):
        q, k = c % 2, (i * NCH + c) * nb + j
        size, h = m.sizes[j], slice(j * CH, (j + 1) * CH)
        if j == 0:
            act.wait_ge(s[f"down{q}"], turn(ep, i, c))
        act.wait_ge(s[f"used{k % 2}"], ep * (nb * NCH) + (k // 2 + 1))
        act.activation(m.h_hi[q][0:size, h], m.h[q][0:size, h], ACT.Copy).then_inc(s["h_hi"], 1)

    def input_hi(ep, i, c):
        q = c % 2
        act.wait_ge(s[f"x{q}"], turn(ep, i, c) + 1)
        if not isinstance(ep, int) or ep or i or c > 1:
            act.wait_ge(s["up"], index(ep, i, c) * nb - nb)
        act.activation(m.x_hi[q][:, :], m.x[q][:, :], ACT.Copy).then_inc(s[f"x_hi{q}"], 1)

    def copy_gate(ep, i, c):
        q = c % 2
        act.wait_ge(r.sem["wide"], index(ep, i, c) + 1)
        act.wait_ge(s[f"part{q}"], turn(ep, i, c))
        act.activation(r.wide[q][:, :], bank(g, GATE0 + q), ACT.Copy).then_inc(r.sem[f"copied{q}"], 1)

    def hidden(step, to_gate):
        for j in range(nb):
            silu(*step, j)
            if j == 1 and to_gate:
                input_hi(*to_gate)
            if j > 0:
                split_hi(*step, j - 1)
        split_hi(*step, nb - 1)

    def body_input(ep, last):
        for step in steps_of(ep, E):
            later, to_gate = ahead(step, 1, E, last), ahead(step, 2, E, last)
            if later:
                hidden(later, to_gate)

    def body_output(ep, last):
        for step in steps_of(ep, E):
            if ahead(step, 2, E, last):
                silu(*ahead(step, 2, E, last), 0)
            if ahead(step, 1, E, last):
                split_hi(*ahead(step, 1, E, last), 0)
            copy_gate(*step)

    if m.gate_input:
        router_scalar(act, r, kind)
        input_hi(0, 0, 0)
        hidden((0, 0, 0), (0, 0, 1))
        over_experts_loop(act, E, body_input)
    else:
        silu(0, 0, 0, 0)
        silu(0, 0, 1, 0)
        split_hi(0, 0, 0, 0)
        router_scalar(act, r, kind)
        over_experts_loop(act, E, body_output)


def gated_vector(dve, g, r, m, kind, where):
    s, nb = m.sem, m.nb

    def multiply(ep, i, c, j):
        q, k = c % 2, (i * NCH + c) * nb + j
        size, h = m.sizes[j], slice(j * CH, (j + 1) * CH)
        dve.wait_ge(s["silu"], ep * (2 * nb * NCH) + k + 1)
        dve.wait_ge(s[f"h_lo{q}"], turn(ep, i, c) * nb)
        dve.tensor_tensor(m.h[q][0:size, h], m.silu[k % 2][0:size, :], bank(g, 2 * (k % 2) + 1)[0:size, :],
                          ALU.mult).then_inc(s[f"used{k % 2}"], 1)

    def split_lo(ep, i, c, j):
        q = c % 2
        size, h = m.sizes[j], slice(j * CH, (j + 1) * CH)
        dve.wait_ge(s["h_hi"], index(ep, i, c) * nb + (j + 1))
        dve.tensor_tensor(m.h_lo[q][0:size, h], m.h[q][0:size, h], m.h_hi[q][0:size, h].bitcast(F32),
                          ALU.subtract).then_inc(s[f"h_lo{q}"], 1)

    def gate_input(ep, i, c):
        q = c % 2
        dve.wait_ge(r.sem["wide"], index(ep, i, c) + 1)
        dve.wait_ge(s[f"x_lo{q}"], turn(ep, i, c))
        dve.tensor_tensor(m.x[q][:, :], m.x_all[:, c * CH:(c + 1) * CH], bank(g, GATE0 + q), ALU.mult).then_inc(s[f"x{q}"], 1)

    def gate_output(ep, i, c):
        q = c % 2
        dve.wait_ge(s[f"down{q}"], turn(ep, i, c) + 1)
        dve.wait_ge(r.sem[f"copied{q}"], turn(ep, i, c) + 1)
        dve.wait_ge(s[f"acc{q}"], turn(ep, i, c))
        dve.tensor_tensor(m.part[q][:, :], bank(g, OUT0 + q), r.wide[q][:, :], ALU.mult).then_inc(s[f"part{q}"], 1)

    def accumulate(ep, i, c):
        q, tok = c % 2, slice(c * CH, (c + 1) * CH)
        dve.wait_ge(s[f"down{q}"], turn(ep, i, c) + 1)
        dve.wait_ge(s[f"acc{q}"], turn(ep, i, c))
        dve.tensor_tensor(m.acc[:, tok], m.acc[:, tok], bank(g, OUT0 + q), ALU.add).then_inc(s[f"acc{q}"], 1)

    def split_weights(ep, i, c, last):
        if c == m.split_at and i == 0:
            split_weights_hi(dve, s, m.w_hi, m.raw, ep, 1)
        if c == m.split_at and i == 1 and not last:
            split_weights_hi(dve, s, m.w_hi, m.raw, ep + 1, 0)

    def hidden(step, to_gate):
        for j in range(nb):
            multiply(*step, j)
            if j == 0 and to_gate:
                gate_input(*to_gate)
            if j > 0:
                split_lo(*step, j - 1)
        split_lo(*step, nb - 1)

    def body_input(ep, last):
        for step in steps_of(ep, E):
            later, to_gate = ahead(step, 1, E, last), ahead(step, 2, E, last)
            if later:
                hidden(later, to_gate)
            split_weights(*step, last)
            accumulate(*step)

    def body_output(ep, last):
        for step in steps_of(ep, E):
            if ahead(step, 2, E, last):
                multiply(*ahead(step, 2, E, last), 0)
            if ahead(step, 1, E, last):
                split_lo(*ahead(step, 1, E, last), 0)
            split_weights(*step, last)
            gate_output(*step)

    if m.gate_input:
        router_vector(dve, g, r, kind, where)
        turn_gates_vector(dve, g, r)
        gate_input(0, 0, 0)
        dve.wait_ge(s["zeroed"], 1)
        hidden((0, 0, 0), (0, 0, 1))
        over_experts_loop(dve, E, body_input)
    else:
        multiply(0, 0, 0, 0)
        multiply(0, 0, 1, 0)
        split_lo(0, 0, 0, 0)
        router_vector(dve, g, r, kind, where)
        turn_gates_vector(dve, g, r)
        over_experts_loop(dve, E, body_output)


def gated_gpsimd(pool, m):
    s = m.sem

    def input_lo(ep, i, c):
        q = c % 2
        pool.wait_ge(s[f"x_hi{q}"], turn(ep, i, c) + 1)
        pool.tensor_tensor(m.x_lo[q][:, :], m.x[q][:, :], m.x_hi[q][:, :].bitcast(F32),
                           ALU.subtract).then_inc(s[f"x_lo{q}"], 1)

    def accumulate(ep, i, c):
        q, tok = c % 2, slice(c * CH, (c + 1) * CH)
        pool.wait_ge(s[f"part{q}"], turn(ep, i, c) + 1)
        pool.wait_ge(s[f"acc{q}"], turn(ep, i, c))
        pool.tensor_tensor(m.acc[:, tok], m.acc[:, tok], m.part[q][:, :], ALU.add).then_inc(s[f"acc{q}"], 1)

    def body(ep, last):
        for step in steps_of(ep, E):
            _, i, c = step
            if m.gate_input and ahead(step, 2, E, last):
                input_lo(*ahead(step, 2, E, last))
            if c == m.split_at and i == 0:
                split_weights_lo(pool, s, m.w_hi, m.w_lo, m.raw, ep, 1)
            if c == m.split_at and i == 1 and not last:
                split_weights_lo(pool, s, m.w_hi, m.w_lo, m.raw, ep + 1, 0)
            if not m.gate_input:
                accumulate(*step)

    if m.gate_input:
        input_lo(0, 0, 0)
        input_lo(0, 0, 1)
    over_experts_loop(pool, E, body)


def stage_gated(nc, g, w, p, hidden, kind):
    with ExitStack() as ctx:
        n, r, a = ln_alloc(nc, ctx, p), router_alloc(nc, ctx, p), add_alloc(nc, ctx, p)
        m = gated_alloc(nc, ctx, p, hidden, kind == "bias")
        block = ctx.enter_context(nc.Block())

        @block.sync
        def _(sp):
            router_sync(sp, r, w[p + "wr"], w[p + "br"] if kind == "bias" else None)
            load_expert_weights(sp, m.sem, m.raw, w[p + "w"], E)

        @block.gpsimd
        def _(pool):
            start_gpsimd(pool, g, n, m)
            pool.wait_ge(m.sem["zeroed"], 1)
            gated_gpsimd(pool, m)

        @block.tensor
        def _(pe):
            ln_tensor(pe, g, n)
            router_tensor(pe, g, n, r, GATE0)
            gated_tensor(pe, g, n, r, m)
            add_tensor(pe, g, a, m.acc, sums_of(m, E))

        @block.scalar
        def _(act):
            ln_scalar(act, g, n, m.x_all if m.gate_input else None)
            gated_scalar(act, g, r, m, kind)

        @block.vector
        def _(dve):
            ln_rows_vector(dve, g, n, g.x)
            router_split_vector(dve, r, kind == "bias")
            split_weights_hi(dve, m.sem, m.w_hi, m.raw, 0, 0)
            ln_lo_vector(dve, g, n)
            gated_vector(dve, g, r, m, kind, GATE0)
            add_vector(dve, g, a, g.x, g.x)
            dve.wait_ge(a.sem["added"], NCH)


HIDDEN1, HIDDEN2 = 128, 352


def stage_l1_ffn(nc, g, w):
    stage_gated(nc, g, w, "f1_", HIDDEN1, "pair")


def stage_l2_ffn(nc, g, w):
    stage_gated(nc, g, w, "f2_", HIDDEN2, "bias")


TB = BANK // B
TAIL = (0, 1, 2, 3)
KEEP_UP = 384
W_IN, W_GATE, W_STATE, W_INPUT, W_OUT = range(5)


def stage_l1_recurrence(nc, g, w):
    p = "a1_"
    with ExitStack() as ctx:
        n, a = ln_alloc(nc, ctx, p), add_alloc(nc, ctx, p)
        raw = sb(nc, ctx, p + "w_raw", 5 * D)
        w_hi, w_lo = sb(nc, ctx, p + "w_hi", 5 * D, F32R), sb(nc, ctx, p + "w_lo", 5 * D, F32R)
        bias = sb(nc, ctx, p + "bias", 5)
        ctxt, kv, r = sb(nc, ctx, p + "ctx", T), sb(nc, ctx, p + "kv", T), sb(nc, ctx, p + "r", T)
        ret = sb(nc, ctx, p + "ret", T)
        inp, inp_hi, inp_lo = sb(nc, ctx, p + "inp", T), sb(nc, ctx, p + "inp_hi", T, F32R), sb(nc, ctx, p + "inp_lo", T, F32R)
        tanh, gate, keep = sb(nc, ctx, p + "tanh", T), sb(nc, ctx, p + "gate", T), sb(nc, ctx, p + "keep", T)
        u = kv
        state = sb(nc, ctx, p + "state", B * (S + 1))
        gs = [sb(nc, ctx, f"{p}gs{i}", B) for i in range(2)]
        part_hi, part_lo = n.hi, n.lo
        s = sems(nc, p, "w raw bias ctx kv r w_hi w_lo half zero ret ret_hi ret_lo inp_mm inp inp_hi inp_lo gate_mm "
                             "tanh gate keep u u_hi u_lo fixed gs step state st_hi st_lo out_mm out")
        states = state[:, :].rearrange("p (b t) -> p b t", t=S + 1)
        gates = gate[:, :].rearrange("p (b t) -> p b t", t=S)
        acc = inp
        out_by_time = acc[:, :].rearrange("p (b t) -> p t b", t=S)
        block = ctx.enter_context(nc.Block())

        def weight(x, k):
            return x[:, k * D:(k + 1) * D]

        def by_time(x, k):
            return x[:, :].rearrange("p (b t) -> p t b", t=S)[:, k * TB:(k + 1) * TB, :]

        def chunk(x, c):
            return x[:, c * CH:(c + 1) * CH]

        def time_major(x):
            return x.rearrange("p (t b) -> p t b", b=B)

        def tail_at(t, task):
            k, rest = divmod(t - TAIL[task], TB)
            return k - 1 if rest == 0 and k >= 1 else None

        @block.sync
        def _(sp):
            sp.dma_start(ctxt[:, :], w["ctx_t"]).then_inc(s["ctx"], 16)
            sp.dma_start(raw[:, :], w["a1_w"]).then_inc(s["raw"], 16)
            sp.dma_start(bias[:, 0:4], w["a1_bias"]).then_inc(s["bias"], 16)

        @block.gpsimd
        def _(pool):
            ln_gpsimd(pool, g, n)
            pool.wait_ge(s["w_hi"], 1)
            pool.tensor_tensor(w_lo[:, :], raw[:, :], w_hi[:, :].bitcast(F32), ALU.subtract).then_inc(s["w_lo"], 1)

        @block.vector
        def _(dve):
            dve.memset(states[:, :, 0], 0.0).then_inc(s["zero"], 1)
            ln_rows_vector(dve, g, n, g.x)
            dve.wait_ge(s["raw"], 16)
            dve.tensor_copy(w_hi[:, :], raw[:, :]).then_inc(s["w_hi"], 1)
            dve.wait_ge(s["bias"], 16)
            dve.tensor_scalar(bias[:, 4:5], bias[:, 1:2], 0.5, None, ALU.mult).then_inc(s["half"], 1)

            def retain(c):
                dve.wait_ge(s["kv"], c + 1)
                for b in range(c * TPC, (c + 1) * TPC):
                    dve.tensor_tensor_scan(r[:, b * S:(b + 1) * S], bias[:, 3:4].to_broadcast([128, S]), kv[:, b * S:(b + 1) * S],
                                           0.0, ALU.mult, ALU.add).then_inc(s["r"], 1)
                dve.wait_ge(s["r"], (c + 1) * TPC)
                dve.wait_ge(n.sem["turned"], c + 1)
                dve.tensor_tensor(chunk(ret, c), bank(g, c), chunk(r, c), ALU.mult).then_inc(s["ret"], 1)

            def retained_lo(c):
                dve.wait_ge(s["ret_hi"], c + 1)
                dve.tensor_tensor(chunk(part_lo, c), chunk(ret, c), chunk(part_hi, c).bitcast(F32),
                                  ALU.subtract).then_inc(s["ret_lo"], 1)

            def input_lo(c):
                dve.wait_ge(s["inp_hi"], c + 1)
                dve.tensor_tensor(chunk(inp_lo, c), chunk(inp, c), chunk(inp_hi, c).bitcast(F32),
                                  ALU.subtract).then_inc(s["inp_lo"], 1)

            def gates_of(c):
                dve.wait_ge(s["tanh"], c + 1)
                dve.tensor_scalar(chunk(keep, c), chunk(tanh, c), -0.5, 0.5, ALU.mult, ALU.add).then_inc(s["keep"], 1)
                dve.tensor_scalar(chunk(gate, c), chunk(tanh, c), 0.5, 0.5, ALU.mult, ALU.add).then_inc(s["gate"], 1)
                dve.wait_ge(s["keep"], c + 1)
                dve.tensor_tensor(chunk(u, c), chunk(keep, c), chunk(inp, c), ALU.mult).then_inc(s["u"], 1)

            def u_lo(c):
                dve.wait_ge(s["u_hi"], c + 1)
                dve.tensor_tensor(chunk(part_lo, c), chunk(u, c), chunk(part_hi, c).bitcast(F32), ALU.subtract).then_inc(s["u_lo"], 1)

            retain(0)
            for c in range(1, NCH):
                retain(c)
                retained_lo(c - 1)
            retained_lo(NCH - 1)
            for c in range(NCH):
                input_lo(c)
            gates_of(0)
            for c in range(1, NCH):
                gates_of(c)
                u_lo(c - 1)
            u_lo(NCH - 1)
            dve.wait_ge(s["gate"], NCH)
            dve.wait_ge(s["zero"], 1)

            def states_lo(k):
                dve.wait_ge(s["st_hi"], k + 1)
                dve.tensor_tensor(time_major(chunk(part_lo, k)), states[:, :, 1 + k * TB:1 + (k + 1) * TB].rearrange("p b t -> p t b"),
                                  time_major(chunk(part_hi, k)).bitcast(F32), ALU.subtract).then_inc(s["st_lo"], 1)

            for t in range(S):
                dve.wait_ge(s["state"], t)
                dve.tensor_tensor(gs[t % 2][:, :], gates[:, :, t], states[:, :, t], ALU.mult).then_inc(s["gs"], 1)
                if tail_at(t, 1) is not None:
                    states_lo(tail_at(t, 1))
            states_lo(NCH - 1)
            add_vector(dve, g, a, g.x, g.x)
            dve.wait_ge(a.sem["added"], NCH)

        @block.scalar
        def _(act):
            act.wait_ge(s["ctx"], 16)
            for c in range(NCH):
                act.activation(chunk(kv, c), chunk(ctxt, c), ACT.Square).then_inc(s["kv"], 1)
            for c in range(NCH):
                act.wait_ge(s["ret"], c + 1)
                act.activation(chunk(part_hi, c), chunk(ret, c), ACT.Copy).then_inc(s["ret_hi"], 1)

            def inputs(c):
                act.wait_ge(s["inp_mm"], c + 1)
                act.activation(chunk(inp, c), bank(g, NCH + c), ACT.Identity, bias=bias[:, 0:1]).then_inc(s["inp"], 1)
                act.activation(chunk(inp_hi, c), bank(g, NCH + c), ACT.Identity, bias=bias[:, 0:1]).then_inc(s["inp_hi"], 1)

            def tanh_of(c):
                act.wait_ge(s["half"], 1)
                act.wait_ge(s["gate_mm"], c + 1)
                act.activation(chunk(tanh, c), bank(g, c), ACT.Tanh, bias=bias[:, 4:5], scale=0.5).then_inc(s["tanh"], 1)

            def u_hi(c):
                act.wait_ge(s["u"], c + 1)
                act.activation(chunk(part_hi, c), chunk(u, c), ACT.Copy).then_inc(s["u_hi"], 1)

            act.wait_ge(s["bias"], 16)
            inputs(0)
            inputs(1)
            tanh_of(0)
            inputs(2)
            tanh_of(1)
            inputs(3)
            tanh_of(2)
            u_hi(0)
            tanh_of(3)
            for c in range(1, NCH):
                u_hi(c)

            def states_hi(k):
                act.wait_ge(s["state"], (k + 1) * TB)
                act.activation(time_major(chunk(part_hi, k)), states[:, :, 1 + k * TB:1 + (k + 1) * TB].rearrange("p b t -> p t b"),
                               ACT.Copy).then_inc(s["st_hi"], 1)

            def outputs(k):
                act.wait_ge(s["out_mm"], k + 1)
                act.activation(out_by_time[:, k * TB:(k + 1) * TB, :], time_major(bank(g, k)), ACT.Identity,
                               bias=bias[:, 2:3]).then_inc(s["out"], 1)

            for t in range(S):
                act.wait_ge(s["step"], t + 1)
                act.activation(states[:, :, t + 1], g.psum[:, NCH * BANK + t * B:NCH * BANK + (t + 1) * B], ACT.Tanh).then_inc(s["state"], 1)
                if tail_at(t, 0) is not None:
                    states_hi(tail_at(t, 0))
                if tail_at(t, 3) is not None:
                    outputs(tail_at(t, 3))
            states_hi(NCH - 1)
            outputs(NCH - 1)

        @block.tensor
        def _(pe):
            ln_tensor(pe, g, n)
            pe.wait_ge(s["w_lo"], 1)

            def inputs(c):
                pe.wait_ge(s["ret_lo"], c + 1)
                product3(pe, bank(g, NCH + c), weight(w_hi, W_IN), weight(w_lo, W_IN), chunk(part_hi, c), chunk(part_lo, c)).then_inc(s["inp_mm"], 1)

            def gates_of(c):
                pe.wait_ge(s["inp_lo"], c + 1)
                product3(pe, bank(g, c), weight(w_hi, W_GATE), weight(w_lo, W_GATE), chunk(inp_hi, c), chunk(inp_lo, c)).then_inc(s["gate_mm"], 1)

            for c in range(NCH):
                inputs(c)
            for c in range(NCH):
                gates_of(c)
            for k in range(NCH):
                pe.matmul(bank(g, NCH + k), weight(w_hi, W_INPUT), by_time(inp_hi, k), start=True, stop=False, skip_group_check=True)
                for x, y in ((weight(w_hi, W_INPUT), inp_lo), (weight(w_lo, W_INPUT), inp_hi)):
                    pe.matmul(bank(g, NCH + k), x, by_time(y, k), start=False, stop=False, skip_group_check=True)
            pe.wait_ge(s["u_lo"], NCH)
            for k in range(NCH):
                for x, y in ((weight(w_hi, W_STATE), part_hi), (weight(w_hi, W_STATE), part_lo), (weight(w_lo, W_STATE), part_hi)):
                    pe.matmul(bank(g, NCH + k), x, by_time(y, k), start=False, stop=False, skip_group_check=True)

            def outputs(k):
                pe.wait_ge(s["st_lo"], k + 1)
                product3(pe, bank(g, k), weight(w_hi, W_OUT), weight(w_lo, W_OUT), chunk(part_hi, k), chunk(part_lo, k)).then_inc(s["out_mm"], 1)

            for t in range(S):
                pe.wait_ge(s["gs"], t + 1)
                pe.matmul(g.psum[:, NCH * BANK + t * B:NCH * BANK + (t + 1) * B], weight(raw, W_STATE), gs[t % 2][:, :],
                          start=False, stop=False, skip_group_check=True).then_inc(s["step"], 1)
                for _ in range(2):
                    pe.matmul(bank(g, NCH - 1)[:, 0:KEEP_UP], g.ident_b[:, :], g.pick_expert[:, 0:KEEP_UP], start=True, stop=True)
                if tail_at(t, 2) is not None:
                    outputs(tail_at(t, 2))
            outputs(NCH - 1)
            add_tensor(pe, g, a, acc, lambda c: [(s["out"], NCH)])


HG = 4
NG = HEADS // HG
DH = D // HEADS
ST = 3 * HG * DH
VW = 32
UP = 2 * NG
PAIRS = B // 2
WQ, WK, WV, WO = 0, NG * ST, 2 * NG * ST, 2 * NG * ST + D
W_SMALL = WO + D
LOWEST = -3.4028234663852886e38


def stage_small_attention(nc, g, w, p, gated):
    with ExitStack() as ctx:
        n = ln_alloc(nc, ctx, p)
        raw = sb(nc, ctx, p + "w_raw", W_SMALL)
        w_hi, w_lo = sb(nc, ctx, p + "w_hi", W_SMALL, F32R), sb(nc, ctx, p + "w_lo", W_SMALL, F32R)
        bias = sb(nc, ctx, p + "bias", 2 * NG + 1)
        bv = sb(nc, ctx, p + "bv", D)
        ctxt = sb(nc, ctx, p + "ctx", T)
        ctx_hi, ctx_lo = sb(nc, ctx, p + "ctx_hi", T, F32R), sb(nc, ctx, p + "ctx_lo", T, F32R)
        gated_keys = [sb(nc, ctx, f"{p}gated_keys{i}", CH, rows=ST) for i in range(2)] if gated else None
        q_all, k_all = (sb(nc, ctx, p + x, NG * T, F32R, ST) for x in ("q_all", "k_all"))
        v_all = sb(nc, ctx, p + "v_all", T)
        q_now = [sb(nc, ctx, f"{p}q_now{i}", NG * S, F32R, ST) for i in range(2)]
        k_now = [sb(nc, ctx, f"{p}k_now{i}", HG * S, F32R, ST) for i in range(4)]
        v_now = [sb(nc, ctx, f"{p}v_now{i}", HEADS * VW) for i in range(2)]
        top = [sb(nc, ctx, f"{p}top{i}", HG) for i in range(2)]
        probs = [sb(nc, ctx, f"{p}probs{i}", HG * S) for i in range(4)]
        probs_t = [sb(nc, ctx, f"{p}probs_t{i}", HG * S) for i in range(4)]
        pv = [sb(nc, ctx, f"{p}pv{i}", NG * S) for i in range(2)]
        rden = [sb(nc, ctx, f"{p}rden{i}", HEADS) for i in range(2)]
        o_rows = [sb(nc, ctx, f"{p}o_rows{i}", D) for i in range(2)]
        o_hi, o_lo = sb(nc, ctx, p + "o_hi", 2 * S, F32R), sb(nc, ctx, p + "o_lo", 2 * S, F32R)
        y = sb(nc, ctx, p + "y", 2 * S)
        s = sems(nc, p, "guarded raw bias ctx w_hi w_lo c_hi c_lo qk_mm k_gated qk_hi qk_lo v_mm v_all v_init "
                             "q_now k_now v_now scores top shifted probs turned probs_t pv pv_out back rden o_rows "
                             "o_turned o_hi o_lo y_mm y y_turned added")
        e = Bag()
        if gated:
            e = Bag()
            e.raw = sb(nc, ctx, p + "e_raw", B * 32)
            e.rows = sb(nc, ctx, p + "e_rows", B)
            e.cols = sb(nc, ctx, p + "e_cols", S, rows=B)
            e.top = sb(nc, ctx, p + "e_top", 1, rows=B)
            e.rtop = sb(nc, ctx, p + "e_rtop", 1, rows=B)
            e.gate = sb(nc, ctx, p + "e_gate", S, rows=B)
            e.wide = sb(nc, ctx, p + "e_wide", T)
            e.sem = sems(nc, p + "e_", "raw rows turned step gate spread wide")
        block = ctx.enter_context(nc.Block())
        S_BANK, PV_BANK, T_BANK, M_BANK, N_BANK = 0, 2, 4, 6, 7
        softmax_scale = float(DH) ** -0.5

        def heads(a, width):
            return a[:, :].rearrange("p (h c) -> p h c", c=width)

        @block.sync
        def _(sp):
            sp.dma_start(raw[:, :], w[p + "w"]).then_inc(s["raw"], 16)
            sp.dma_start(ctxt[:, :], w["ctx_t"]).then_inc(s["ctx"], 16)
            sp.dma_start(bias[:, :], w[p + "bias"]).then_inc(s["bias"], 16)
            sp.dma_start(bv[:, :], w[p + "bv"].partition_broadcast(128)).then_inc(s["bias"], 16)
            if gated:
                sp.dma_start(e.raw[:, :].rearrange("p (b f) -> p b f", b=B), w["energy"].rearrange("b s f -> s b f")).then_inc(e.sem["raw"], 16)

        def seq_of(i, k):
            return i * 2 + k // NG

        def stack(j, c):
            return (q_all if j < NG else k_all)[:, ds(c * CH + (j % NG) * T, CH)]

        @block.gpsimd
        def _(pool):
            ln_gpsimd(pool, g, n)
            for c in range(NCH):
                cols = slice(c * CH, (c + 1) * CH)
                pool.wait_ge(s["c_hi"], c + 1)
                pool.tensor_tensor(ctx_lo[:, cols], ctxt[:, cols], ctx_hi[:, cols].bitcast(F32), ALU.subtract).then_inc(s["c_lo"], 1)
            pool.wait_ge(s["w_hi"], 1)
            pool.tensor_tensor(w_lo[:, :], raw[:, :], w_hi[:, :].bitcast(F32), ALU.subtract).then_inc(s["w_lo"], 1)
            for q in range(2):
                pool.memset(v_now[q][:, :], 0.0).then_inc(s["v_init"], 1)
            pool.wait_ge(s["v_init"], 2)
            for q in range(2):
                pool.memset(heads(v_now[q], VW)[:, :, DH:DH + 1], 1.0).then_inc(s["v_init"], 1)
            pool.wait_ge(s["qk_lo"], 2 * NG * NCH)

            def place_keys(i):
                for k in range(UP):
                    pool.wait_ge(s["scores"], floor0(i * UP + (k - 3)))
                    u = k % NG
                    keys = k_all[:, ds(u * T + seq_of(i, k) * S, S)].unsqueeze(1).to_broadcast([ST, HG, S])
                    own = g.head_rows[0:ST, :].unsqueeze(2).to_broadcast([ST, HG, S])
                    pool.tensor_tensor(heads(k_now[k % 4], S), keys.bitcast(F32), own, ALU.mult).then_inc(s["k_now"], 1)

            place_keys(0)
            with pool.Fori(1, PAIRS) as i:
                place_keys(i)

        @block.tensor
        def _(pe):
            ln_tensor(pe, g, n)
            if gated:
                pe.wait_ge(e.sem["rows"], 1)
                pe.transpose(bank(g, N_BANK)[0:B, 0:S], e.rows[:, :], g.ident[:, :]).then_inc(e.sem["turned"], 1)
            pe.wait_ge(s["w_lo"], 1)
            for b in range(B):
                if b % TPC == 0:
                    pe.wait_ge(s["c_lo"], b // TPC + 1)
                if gated and b == B - TPC:
                    pe.wait_ge(e.sem["step"], 1)
                tok = slice(b * S, (b + 1) * S)
                last = product3(pe, bank(g, 4 + b // TPC)[:, (b % TPC) * D:(b % TPC + 1) * D], ctx_hi[:, tok], ctx_lo[:, tok],
                                w_hi[:, WV:WV + D], w_lo[:, WV:WV + D])
                if b % TPC == TPC - 1:
                    last.then_inc(s["v_mm"], 1)
            pe.wait_ge(n.sem["lo_ready"], NCH)
            pe.wait_ge(s["v_all"], NCH)
            if gated:
                pe.wait_ge(e.sem["gate"], 1)
                for b in range(B):
                    last = pe.matmul(bank(g, 4 + b // TPC)[:, (b % TPC) * S:(b % TPC + 1) * S],
                                     g.ident[0:B, b:b + 1].to_broadcast([B, 128]), e.gate[:, :], start=True, stop=True)
                    if b % TPC == TPC - 1:
                        last.then_inc(e.sem["spread"], 1)

            def stacks(c):
                for j in range(2 * NG):
                    pe.wait_ge(s["qk_lo"], floor0(c * (2 * NG) + (j - 3)))
                    x_hi, x_lo = (n.hi, n.lo) if j < NG else (ctx_hi, ctx_lo)
                    col = j * ST
                    product3(pe, bank(g, j % 4)[0:ST, :], w_hi[:, col:col + ST], w_lo[:, col:col + ST],
                             x_hi[:, ds(c * CH, CH)], x_lo[:, ds(c * CH, CH)]).then_inc(s["qk_mm"], 1)

            over_chunks(pe, stacks)
            pe.wait_ge(s["qk_lo"], 2 * NG * NCH)
            if gated:
                pe.wait_ge(e.sem["wide"], NCH)

            def scores(i, k):
                unit = i * UP + k
                if k % NG == 0:
                    pe.wait_ge(s["q_now"], seq_of(i, k) + 1)
                pe.wait_ge(s["k_now"], unit + 1)
                if not (isinstance(i, int) and i == 0 and k < 2):
                    pe.wait_ge(s["shifted"], unit - 1)
                u = k % NG
                pe.matmul(bank(g, S_BANK + k % 2), q_now[k // NG][:, u * S:(u + 1) * S], k_now[k % 4][:, :],
                          start=True, stop=True).then_inc(s["scores"], 1)

            def turn_probs(i, k):
                unit = i * UP + k
                pe.wait_ge(s["probs"], unit + 1)
                if not (isinstance(i, int) and i == 0 and k < 2):
                    pe.wait_ge(s["probs_t"], unit - 1)
                for j in range(HG):
                    cols = slice(j * S, (j + 1) * S)
                    last = pe.transpose(bank(g, T_BANK + k % 2)[:, cols], probs[k % 4][:, cols], g.ident[:, :])
                last.then_inc(s["turned"], 1)

            def weigh(i, k):
                unit, q, u = i * UP + k, k // NG, k % NG
                pe.wait_ge(s["probs_t"], unit + 1)
                if u == 0:
                    pe.wait_ge(s["v_now"], seq_of(i, k) + 1)
                    if not (isinstance(i, int) and i == 0):
                        pe.wait_ge(s["pv_out"], seq_of(i, k) - 1)
                for j in range(HG):
                    h = u * HG + j
                    last = pe.matmul(bank(g, PV_BANK + q)[j * VW:(j + 1) * VW, u * S:(u + 1) * S],
                                     v_now[q][:, h * VW:(h + 1) * VW], probs_t[k % 4][:, j * S:(j + 1) * S],
                                     start=True, stop=True, tile_position=(0, j * VW))
                last.then_inc(s["pv"], 1)

            def back(i, q):
                pe.wait_ge(s["pv_out"], i * 2 + q + 1)
                for u in range(NG):
                    cols = slice(u * S, (u + 1) * S)
                    last = pe.transpose(bank(g, M_BANK)[:, cols], pv[q][:, cols], g.ident[:, :])
                last.then_inc(s["back"], 1)

            def turn_out(i, q):
                pe.wait_ge(s["o_rows"], i * 2 + q + 1)
                pe.transpose(bank(g, N_BANK)[:, 0:S], o_rows[q][:, :], g.ident[:, :]).then_inc(s["o_turned"], 1)

            def project(i):
                pe.wait_ge(s["o_lo"], i * 2 + 2)
                product3(pe, bank(g, M_BANK)[:, 0:2 * S], w_hi[:, WO:WO + D], w_lo[:, WO:WO + D], o_hi[:, :],
                         o_lo[:, :]).then_inc(s["y_mm"], 1)

            def turn_y(i):
                pe.wait_ge(s["y"], i + 1)
                for q in range(2):
                    last = pe.transpose(bank(g, N_BANK)[:, q * S:(q + 1) * S], y[:, q * S:(q + 1) * S], g.ident[:, :])
                last.then_inc(s["y_turned"], 1)

            def body(i, first, last):
                for k in range(UP):
                    scores(i, k)
                    if k >= 2:
                        turn_probs(i, k - 2)
                    elif not first:
                        turn_probs(i - 1, UP - 2 + k)
                    if k >= 3:
                        weigh(i, k - 3)
                    elif not first:
                        weigh(i - 1, UP - 3 + k)
                    if not first:
                        if k == 0:
                            turn_out(i - 1, 0)
                        if k == 3:
                            back(i - 1, 1)
                        if k == 4:
                            turn_out(i - 1, 1)
                        if k == 5:
                            project(i - 1)
                        if k == 6:
                            turn_y(i - 1)
                    if k == 7:
                        back(i, 0)
                if last:
                    turn_out(i, 0)
                    turn_probs(i, UP - 2)
                    weigh(i, UP - 3)
                    turn_probs(i, UP - 1)
                    weigh(i, UP - 2)
                    weigh(i, UP - 1)
                    back(i, 1)
                    turn_out(i, 1)
                    project(i)
                    turn_y(i)

            in_pairs(pe, body)

        @block.scalar
        def _(act):
            act.wait_ge(s["ctx"], 16)
            for c in range(NCH):
                cols = slice(c * CH, (c + 1) * CH)
                act.activation(ctx_hi[:, cols], ctxt[:, cols], ACT.Copy).then_inc(s["c_hi"], 1)
            ln_scalar(act, g, n)
            act.wait_ge(s["bias"], 32)

            def high_parts(c):
                for j in range(2 * NG):
                    if gated and j >= NG:
                        act.wait_ge(s["k_gated"], c * NG + (j - NG + 1))
                        act.activation(stack(j, c), gated_keys[j % 2][:, :], ACT.Copy).then_inc(s["qk_hi"], 1)
                    else:
                        act.wait_ge(s["qk_mm"], c * (2 * NG) + (j + 1))
                        act.activation(stack(j, c), bank(g, j % 4)[0:ST, :], ACT.Identity, bias=bias[0:ST, j:j + 1]).then_inc(s["qk_hi"], 1)

            over_chunks(act, high_parts)

            def exponentials(i, k):
                unit = i * UP + k
                act.wait_ge(s["shifted"], unit + 1)
                act.activation(probs[k % 4][:, :], probs[k % 4][:, :], ACT.Exp, scale=softmax_scale).then_inc(s["probs"], 1)

            def copy_turned(i, k):
                unit = i * UP + k
                act.wait_ge(s["turned"], unit + 1)
                if not (isinstance(i, int) and i == 0 and k < 4):
                    act.wait_ge(s["pv"], unit - 3)
                act.activation(probs_t[k % 4][:, :], bank(g, T_BANK + k % 2), ACT.Copy).then_inc(s["probs_t"], 1)

            def place_values(i, q):
                if not (isinstance(i, int) and i == 0):
                    act.wait_ge(s["pv"], i * UP + (q - 1) * NG)
                act.activation(heads(v_now[q], VW)[:, :, 0:DH], v_all[:, ds(i * (2 * S) + q * S, D)].rearrange("p (h c) -> p h c", c=DH),
                               ACT.Copy).then_inc(s["v_now"], 1)

            def copy_weighed(i, q):
                act.wait_ge(s["pv"], i * UP + (q + 1) * NG)
                act.activation(pv[q][:, :], bank(g, PV_BANK + q), ACT.Copy).then_inc(s["pv_out"], 1)

            def out_hi(i, q):
                act.wait_ge(s["o_turned"], i * 2 + q + 1)
                act.activation(o_hi[:, q * S:(q + 1) * S], bank(g, N_BANK)[:, 0:S], ACT.Copy).then_inc(s["o_hi"], 1)

            def copy_y(i):
                act.wait_ge(s["y_mm"], i + 1)
                act.activation(y[:, :], bank(g, M_BANK)[:, 0:2 * S], ACT.Identity, bias=bias[:, 2 * NG:2 * NG + 1]).then_inc(s["y"], 1)

            def body(i, first, last):
                for k in range(UP):
                    if k >= 2:
                        copy_turned(i, k - 2)
                    elif not first:
                        copy_turned(i - 1, UP - 2 + k)
                    if k in (1, 5):
                        place_values(i, k // NG)
                    exponentials(i, k)
                    if not first:
                        if k == 0:
                            out_hi(i - 1, 0)
                        if k == 2:
                            copy_weighed(i - 1, 1)
                        if k == 4:
                            out_hi(i - 1, 1)
                        if k == 5:
                            copy_y(i - 1)
                    if k == 6:
                        copy_weighed(i, 0)
                if last:
                    out_hi(i, 0)
                    copy_turned(i, UP - 2)
                    copy_turned(i, UP - 1)
                    copy_weighed(i, 1)
                    out_hi(i, 1)
                    copy_y(i)

            act.wait_ge(s["v_init"], 4)
            act.wait_ge(s["v_all"], NCH)
            in_pairs(act, body)

        @block.vector
        def _(dve):
            ln_rows_vector(dve, g, n, g.x)
            dve.wait_ge(s["raw"], 16)
            dve.tensor_copy(w_hi[:, :], raw[:, :]).then_inc(s["w_hi"], 1)
            ln_lo_vector(dve, g, n)
            if gated:
                es = e.sem
                dve.wait_ge(es["raw"], 16)
                dve.tensor_reduce(e.rows[:, :], e.raw[:, :].rearrange("p (b f) -> p b f", b=B), AX.X, ALU.add,
                                  apply_absolute_value=True).then_inc(es["rows"], 1)
                dve.wait_ge(es["turned"], 1)
                dve.tensor_scalar(e.cols[:, :], bank(g, N_BANK)[0:B, 0:S], 1.0 / 32, None, ALU.mult).then_inc(es["step"], 1)
                dve.wait_ge(es["step"], 1)
                dve.tensor_reduce(e.top[:, :], e.cols[:, :], AX.X, ALU.max).then_inc(es["step"], 1)
                dve.wait_ge(es["step"], 2)
                dve.tensor_scalar(e.top[:, :], e.top[:, :], 1e-8, None, ALU.add).then_inc(es["step"], 1)
                dve.wait_ge(es["step"], 3)
                dve.reciprocal(e.rtop[:, :], e.top[:, :]).then_inc(es["step"], 1)
                dve.wait_ge(es["step"], 4)
                dve.tensor_scalar(e.cols[:, :], e.cols[:, :], e.rtop[:, 0:1], 0.1, ALU.mult, ALU.is_gt).then_inc(es["step"], 1)
                dve.wait_ge(es["step"], 5)
                dve.tensor_scalar(e.gate[:, :], e.cols[:, :], 0.9, 0.1, ALU.mult, ALU.add).then_inc(es["gate"], 1)
            dve.wait_ge(s["bias"], 32)
            for c in range(NCH):
                cols = slice(c * CH, (c + 1) * CH)
                dve.wait_ge(s["v_mm"], c + 1)
                dve.tensor_tensor(v_all[:, cols].rearrange("p (t d) -> p t d", d=D), bank(g, 4 + c).rearrange("p (t d) -> p t d", d=D),
                                  bv[:, :].unsqueeze(1).to_broadcast([128, TPC, D]), ALU.add).then_inc(s["v_all"], 1)
            if gated:
                for c in range(NCH):
                    dve.wait_ge(e.sem["spread"], c + 1)
                    dve.tensor_copy(e.wide[:, c * CH:(c + 1) * CH], bank(g, 4 + c)).then_inc(e.sem["wide"], 1)
                dve.wait_ge(e.sem["wide"], NCH)

            def gate_keys(c, j):
                dve.wait_ge(s["qk_mm"], c * (2 * NG) + (j + 1))
                dve.wait_ge(s["qk_lo"], c * (2 * NG) + (j - 1))
                dve.scalar_tensor_tensor(out=gated_keys[j % 2][:, :], in0=bank(g, j % 4)[0:ST, :], scalar=bias[0:ST, j:j + 1],
                                         in1=e.wide[0:ST, ds(c * CH, CH)], op0=ALU.add, op1=ALU.mult).then_inc(s["k_gated"], 1)

            def low_part(c, j):
                rows = slice(ST // 3, 2 * ST // 3) if j < NG else slice(2 * ST // 3, ST)
                low = stack(j, c)[rows]
                dve.wait_ge(s["qk_hi"], c * (2 * NG) + (j + 1))
                if gated and j >= NG:
                    dve.tensor_tensor(low, gated_keys[j % 2][rows, :], low.bitcast(F32), ALU.subtract).then_inc(s["qk_lo"], 1)
                else:
                    dve.scalar_tensor_tensor(out=low, in0=bank(g, j % 4)[rows, :], scalar=bias[rows, j:j + 1], in1=low.bitcast(F32),
                                             op0=ALU.add, op1=ALU.subtract).then_inc(s["qk_lo"], 1)

            def low_parts(c):
                for j in range(NG):
                    low_part(c, j)
                if gated:
                    gate_keys(c, NG)
                for j in range(NG, 2 * NG):
                    if gated and j + 1 < 2 * NG:
                        gate_keys(c, j + 1)
                    low_part(c, j)

            over_chunks(dve, low_parts)

            def place_queries(i, q):
                if not (isinstance(i, int) and i == 0):
                    dve.wait_ge(s["scores"], i * UP + (q - 1) * NG)
                dve.tensor_copy(q_now[q][:, :].rearrange("p (u t) -> p u t", u=NG),
                                q_all[:, :].rearrange("p (u t) -> p u t", u=NG)[:, :, ds(i * (2 * S) + q * S, S)]).then_inc(s["q_now"], 1)

            def shift(i, k):
                unit = i * UP + k
                psum = bank(g, S_BANK + k % 2).rearrange("p (h t) -> p h t", t=S)
                dve.wait_ge(s["scores"], unit + 1)
                dve.tensor_reduce(top[k % 2][:, :], psum, AX.X, ALU.max).then_inc(s["top"], 1)
                dve.wait_ge(s["top"], unit + 1)
                if not (isinstance(i, int) and i == 0 and k < 4):
                    dve.wait_ge(s["turned"], unit - 3)
                dve.tensor_tensor(heads(probs[k % 4], S), psum, top[k % 2][:, :].unsqueeze(2).to_broadcast([128, HG, S]),
                                  ALU.subtract).then_inc(s["shifted"], 1)

            def normalize(i, q):
                back = bank(g, M_BANK).rearrange("p (h c) -> p h c", c=VW)
                seq = i * 2 + q
                dve.wait_ge(s["back"], seq + 1)
                dve.reciprocal(rden[q][:, :], back[:, :, DH]).then_inc(s["rden"], 1)
                dve.wait_ge(s["rden"], seq + 1)
                wide_rden = rden[q][:, :].unsqueeze(2).to_broadcast([128, HEADS, DH])
                if gated:
                    dve.tensor_scalar(rden[q][:, :], rden[q][:, :], 0.0, None, ALU.max).then_inc(s["guarded"], 1)
                    dve.wait_ge(s["guarded"], seq + 1)
                    dve.scalar_tensor_tensor(out=heads(o_rows[q], DH), in0=back[:, :, 0:DH], scalar=LOWEST, in1=wide_rden,
                                             op0=ALU.max, op1=ALU.mult).then_inc(s["o_rows"], 1)
                else:
                    dve.tensor_tensor(heads(o_rows[q], DH), back[:, :, 0:DH], wide_rden, ALU.mult).then_inc(s["o_rows"], 1)

            def out_lo(i, q):
                cols = slice(q * S, (q + 1) * S)
                dve.wait_ge(s["o_hi"], i * 2 + q + 1)
                dve.tensor_tensor(o_lo[:, cols], bank(g, N_BANK)[:, 0:S], o_hi[:, cols].bitcast(F32),
                                  ALU.subtract).then_inc(s["o_lo"], 1)

            def add_y(i):
                dve.wait_ge(s["y_turned"], i + 1)
                tok = ds(i * (2 * S), 2 * S)
                dve.tensor_tensor(g.x[:, tok], g.x[:, tok], bank(g, N_BANK)[:, 0:2 * S], ALU.add).then_inc(s["added"], 1)

            def body(i, first, last):
                for k in range(UP):
                    if not first:
                        if k == 0:
                            normalize(i - 1, 0)
                        if k == 1:
                            out_lo(i - 1, 0)
                        if k == 4:
                            normalize(i - 1, 1)
                        if k == 5:
                            out_lo(i - 1, 1)
                        if k == 7:
                            add_y(i - 1)
                    shift(i, k)
                    if k == 1:
                        place_queries(i, 1)
                    if k == 6 and not last:
                        place_queries(i + 1, 0)
                if last:
                    normalize(i, 0)
                    out_lo(i, 0)
                    normalize(i, 1)
                    out_lo(i, 1)
                    add_y(i)

            dve.wait_ge(s["qk_lo"], 2 * NG * NCH)
            place_queries(0, 0)
            in_pairs(dve, body)
            dve.wait_ge(s["added"], PAIRS)


def over_chunks(eng, body):
    body(0)
    with eng.Fori(1, NCH) as c:
        body(c)


def in_pairs(eng, body):
    body(0, True, False)
    with eng.Fori(0, PAIRS // 2 - 1) as i:
        body(i * 2 + 1, False, False)
        body(i * 2 + 2, False, False)
    body(PAIRS - 1, False, True)


def stage_l2_attention(nc, g, w):
    stage_small_attention(nc, g, w, "a2_", True)


def stage_l3_attention(nc, g, w):
    stage_small_attention(nc, g, w, "a3_", False)


D0 = 64
INNER = HEADS * D0
NBLK = INNER // 128
UG = 4
UNITS = 2 * HEADS // UG
RUNS = UNITS // 2
GROUPS = 12
MASKED = -2.0 ** 100
WQ0, WK0, WV0, WO0 = 0, INNER, 2 * INNER, 3 * INNER
S0, T0, O0, J0, Y0 = 0, 2, 4, 5, 7


def stage_l0_attention(nc, g, w):
    p = "a0_"
    with ExitStack() as ctx:
        n = ln_alloc(nc, ctx, p)
        ctxt = sb(nc, ctx, p + "ctx", T)
        ctx_hi, ctx_lo = sb(nc, ctx, p + "ctx_hi", T, F32R), sb(nc, ctx, p + "ctx_lo", T, F32R)
        w_hi, w_lo = sb(nc, ctx, p + "w_hi", 4 * INNER, F32R), sb(nc, ctx, p + "w_lo", 4 * INNER, F32R)
        qk = [sb(nc, ctx, f"{p}qk{i}", 2 * NBLK * 2 * S) for i in range(2)]
        v = [sb(nc, ctx, f"{p}v{i}", 2 * INNER) for i in range(2)]
        ctx_now = [[sb(nc, ctx, f"{p}ctx_now{x}{i}", 2 * S, F32R) for x in ("hi", "lo")] for i in range(2)]
        raw = qk[1]
        bo = sb(nc, ctx, p + "bo", 1)
        mask_words, mask = sb(nc, ctx, p + "mask_words", T // 4, I32), sb(nc, ctx, p + "mask", T, BF16)
        neg_top = [sb(nc, ctx, f"{p}neg_top{i}", UG) for i in range(2)]
        den = [sb(nc, ctx, f"{p}den{i}", UG) for i in range(2)]
        rden = [sb(nc, ctx, f"{p}rden{i}", UG) for i in range(2)]
        probs = [sb(nc, ctx, f"{p}probs{i}", UG * S) for i in range(4)]
        probs_t = [sb(nc, ctx, f"{p}probs_t{i}", UG * S) for i in range(4)]
        o_hi, o_lo = sb(nc, ctx, p + "o_hi", NBLK * 2 * S, F32R), sb(nc, ctx, p + "o_lo", NBLK * 2 * S, F32R)
        y = sb(nc, ctx, p + "y", 2 * S)
        s = sems(nc, p, "raw ctx bo mask w_hi w_lo w_lo_qk c_hi c_lo c_now masked proj proj_act proj_dve scores neg_top probs rden "
                             "normed turned probs_t weighed o_hi o_lo y_mm y y_turned added")
        block = ctx.enter_context(nc.Block())

        def q_of(par):
            return qk[par][:, 0:NBLK * 2 * S].rearrange("p (b q t) -> p b q t", b=NBLK, q=2)

        def k_of(par):
            return qk[par][:, NBLK * 2 * S:].rearrange("p (b q t) -> p b q t", b=NBLK, q=2)

        def group_out(par, m):
            if m < 8:
                c0 = (m % 2) * NBLK * 2 * S + (m // 2) * CH
                return qk[par][:, c0:c0 + CH]
            return v[par][:, (m - 8) * CH:(m - 7) * CH]

        def blocks4(o, k):
            return o[:, :].rearrange("p (b q t) -> p b q t", b=NBLK, q=2)[:, 4 * (k // 2):4 * (k // 2) + 4, k % 2]

        def four(a):
            return a.rearrange("p (h t) -> p h t", t=S)

        def in_two_pairs(eng, body):
            body(0, True, False)
            with eng.Fori(1, PAIRS // 2 - 1) as dp:
                body(dp, False, False)
            body(PAIRS // 2 - 1, False, True)

        @block.sync
        def _(sp):
            sp.dma_start(ctxt[:, :], w["ctx_t"]).then_inc(s["ctx"], 16)
            for k in range(4):
                cols = slice(k * INNER, (k + 1) * INNER)
                sp.dma_start(raw[:, cols], w["a0_w"][:, cols]).then_inc(s["raw"], 16)
            sp.dma_start(bo[:, :], w["a0_bo"]).then_inc(s["bo"], 16)
            sp.dma_start(mask_words[:, :].rearrange("p (b t) -> p b t", b=B), w["mask"].rearrange("b s t -> s b t")).then_inc(s["mask"], 16)

        @block.gpsimd
        def _(pool):
            ln_gpsimd(pool, g, n)
            for c in range(NCH):
                cols = slice(c * CH, (c + 1) * CH)
                pool.wait_ge(s["c_hi"], c + 1)
                pool.tensor_tensor(ctx_lo[:, cols], ctxt[:, cols], ctx_hi[:, cols].bitcast(F32), ALU.subtract).then_inc(s["c_lo"], 1)
            for k in (2, 3):
                cols = slice(k * INNER, (k + 1) * INNER)
                pool.wait_ge(s["w_hi"], k + 1)
                pool.tensor_tensor(w_lo[:, cols], raw[:, cols], w_hi[:, cols].bitcast(F32), ALU.subtract).then_inc(s["w_lo"], 1)

            def normalize(c, k):
                pool.wait_ge(s["rden"], c + (k + 1))
                pool.wait_ge(s["probs"], c + (k + 1))
                pool.tensor_tensor(four(probs[k % 4][:, :]), four(probs[k % 4][:, :]),
                                   rden[k % 2][:, :].unsqueeze(2).to_broadcast([128, UG, S]), ALU.mult).then_inc(s["normed"], 1)

            with pool.Fori(0, PAIRS) as i:
                for k in range(UNITS):
                    normalize(i * UNITS, k)

        @block.tensor
        def _(pe):
            ln_tensor(pe, g, n)
            pe.wait_ge(n.sem["lo_ready"], NCH)
            pe.wait_ge(s["c_lo"], NCH)
            pe.wait_ge(s["w_lo_qk"], 2)

            def project(pair, par, m):
                out = bank(g, J0 + m % 2)
                done = s["proj_dve"] if m % 2 else s["proj_act"]
                pe.wait_ge(done, floor0(pair * (GROUPS // 2) + m // 2))
                if m < 8:
                    x_hi, x_lo = (ctx_hi, ctx_lo) if m % 2 else (n.hi, n.lo)
                    for b in range(2):
                        col = (m % 2) * INNER + (2 * (m // 2) + b) * 128
                        tok = ds(pair * (2 * S), 2 * S)
                        last = product3(pe, out[:, b * 2 * S:(b + 1) * 2 * S], w_hi[:, col:col + 128], w_lo[:, col:col + 128],
                                        x_hi[:, tok], x_lo[:, tok])
                else:
                    q, half = (m - 8) // 2, m % 2
                    pe.wait_ge(s["c_now"], pair * 2 + 2)
                    c_hi, c_lo = ctx_now[par][0][:, q * S:(q + 1) * S], ctx_now[par][1][:, q * S:(q + 1) * S]
                    cols = slice(WV0 + half * CH, WV0 + (half + 1) * CH)
                    last = product3(pe, out, c_hi, c_lo, w_hi[:, cols], w_lo[:, cols])
                last.then_inc(s["proj"], 1)

            def scores(pair, par, k):
                unit = pair * UNITS + k
                pe.wait_ge(s["probs"], floor0(unit - 1))
                if k == 0:
                    pe.wait_ge(s["proj_act"], pair * (GROUPS // 2) + 4)
                    pe.wait_ge(s["proj_dve"], pair * (GROUPS // 2) + 4)
                q, half, out = k // 2 % 2, k % 2, bank(g, S0 + k % 2)
                hide = mask[:, ds(pair * (2 * S) + q * S, S)].unsqueeze(1).to_broadcast([128, UG, S])
                pe.matmul(four(out), g.ident_b[:, :], hide, start=True, stop=False, skip_group_check=True)
                rows = slice(half * D0, (half + 1) * D0)
                for j in range(UG):
                    b = 4 * (k // 4) + j
                    last = pe.matmul(out[:, j * S:(j + 1) * S], q_of(par)[rows, b, q], k_of(par)[rows, b, q],
                                     start=False, stop=True, skip_group_check=True)
                last.then_inc(s["scores"], 1)

            def turn_probs(pair, k):
                unit = pair * UNITS + k
                pe.wait_ge(s["normed"], unit + 1)
                pe.wait_ge(s["probs_t"], floor0(unit - 1))
                for j in range(UG):
                    cols = slice(j * S, (j + 1) * S)
                    last = pe.transpose(bank(g, T0 + k % 2)[:, cols], probs[k % 4][:, cols], g.ident[:, :])
                last.then_inc(s["turned"], 1)

            def weigh(pair, par, r):
                pe.wait_ge(s["probs_t"], pair * UNITS + (2 * r + 2))
                if r == 0:
                    pe.wait_ge(s["proj_act"], pair * (GROUPS // 2) + GROUPS // 2)
                    pe.wait_ge(s["proj_dve"], pair * (GROUPS // 2) + GROUPS // 2)
                pe.wait_ge(s["o_lo"], floor0(pair * RUNS + r))
                for j in range(UG):
                    for half in range(2):
                        h = 2 * (4 * (r // 2) + j) + half
                        col = (r % 2) * INNER + h * D0
                        last = pe.matmul(bank(g, O0)[half * D0:(half + 1) * D0, j * S:(j + 1) * S], v[par][:, col:col + D0],
                                         probs_t[2 * (r % 2) + half][:, j * S:(j + 1) * S], start=True, stop=True,
                                         tile_position=(0, half * D0))
                last.then_inc(s["weighed"], 1)

            def project_out(pair):
                pe.wait_ge(s["o_lo"], pair * RUNS + RUNS)
                pe.wait_ge(s["added"], floor0(pair * 1))
                for b in range(NBLK):
                    ws, cols = slice(WO0 + b * D, WO0 + (b + 1) * D), slice(b * 2 * S, (b + 1) * 2 * S)
                    last = product3(pe, bank(g, Y0)[:, 0:2 * S], w_hi[:, ws], w_lo[:, ws], o_hi[:, cols], o_lo[:, cols],
                                    first=b == 0, last=b == NBLK - 1)
                last.then_inc(s["y_mm"], 1)

            def turn_y(pair):
                pe.wait_ge(s["y"], pair + 1)
                for q in range(2):
                    last = pe.transpose(bank(g, Y0)[:, (2 + q) * S:(3 + q) * S], y[:, q * S:(q + 1) * S], g.ident[:, :])
                last.then_inc(s["y_turned"], 1)

            def one_pair(pair, par, first, last):
                for k in range(UNITS):
                    scores(pair, par, k)
                    if not last:
                        for m in groups_at(k):
                            project(pair + 1, 1 - par, m)
                    if k >= 2:
                        turn_probs(pair, k - 2)
                    elif not first:
                        turn_probs(pair - 1, UNITS - 2 + k)
                    if k in (0, 2) and not first:
                        weigh(pair - 1, 1 - par, 2 + k // 2)
                    if k in (4, 6):
                        weigh(pair, par, k // 2 - 2)
                    if k == 3 and not first:
                        project_out(pair - 1)
                    if k == 5 and not first:
                        turn_y(pair - 1)
                if last:
                    turn_probs(pair, UNITS - 2)
                    turn_probs(pair, UNITS - 1)
                    weigh(pair, par, 2)
                    weigh(pair, par, 3)
                    project_out(pair)
                    turn_y(pair)

            for m in range(GROUPS):
                if m == 8:
                    pe.wait_ge(s["w_lo"], 1)
                project(0, 0, m)
            pe.wait_ge(s["masked"], 1)
            pe.wait_ge(s["w_lo"], 2)
            in_two_pairs(pe, lambda dp, first, last: (one_pair(dp * 2, 0, first, False), one_pair(dp * 2 + 1, 1, False, last)))

        @block.scalar
        def _(act):
            act.wait_ge(s["ctx"], 16)
            for c in range(NCH):
                cols = slice(c * CH, (c + 1) * CH)
                act.activation(ctx_hi[:, cols], ctxt[:, cols], ACT.Copy).then_inc(s["c_hi"], 1)
            ln_scalar(act, g, n)

            def read_out(pair, par, m, first):
                act.wait_ge(s["proj"], pair * GROUPS + (m + 1))
                act.wait_ge(s["scores"], floor0(pair * UNITS - UNITS)) if m < 8 else act.wait_ge(s["weighed"], floor0(pair * RUNS - RUNS))
                if first and par:
                    act.wait_ge(s["w_lo"], 2)
                act.activation(group_out(par, m), bank(g, J0), ACT.Copy, scale=D0 ** -0.5 if m < 8 else 1.0).then_inc(s["proj_act"], 1)

            def exponentials(pair, k):
                unit = pair * UNITS + k
                act.wait_ge(s["neg_top"], unit + 1)
                act.wait_ge(s["rden"], floor0(unit - 1))
                act.wait_ge(s["turned"], floor0(unit - 3))
                for j in range(UG):
                    cols = slice(j * S, (j + 1) * S)
                    last = act.activation(probs[k % 4][:, cols], bank(g, S0 + k % 2)[:, cols], ACT.Exp,
                                          bias=neg_top[k % 2][:, j:j + 1], accum_out=den[k % 2][:, j:j + 1])
                last.then_inc(s["probs"], 1)

            def copy_turned(pair, k):
                act.wait_ge(s["turned"], pair * UNITS + (k + 1))
                act.wait_ge(s["weighed"], floor0(pair * RUNS + (k // 2 - 1)))
                act.activation(probs_t[k % 4][:, :], bank(g, T0 + k % 2), ACT.Copy).then_inc(s["probs_t"], 1)

            def out_hi(pair, r):
                act.wait_ge(s["weighed"], pair * RUNS + (r + 1))
                act.wait_ge(s["y_mm"], pair * 1)
                act.activation(blocks4(o_hi, r), four(bank(g, O0)), ACT.Copy).then_inc(s["o_hi"], 1)

            def copy_y(pair):
                act.wait_ge(s["y_mm"], pair + 1)
                act.wait_ge(s["y_turned"], pair * 1)
                act.activation(y[:, :], bank(g, Y0)[:, 0:2 * S], ACT.Identity, bias=bo[:, 0:1]).then_inc(s["y"], 1)

            def one_pair(pair, par, first, last):
                for k in range(UNITS):
                    exponentials(pair, k)
                    if not last:
                        for m in groups_at(k):
                            if m % 2 == 0:
                                read_out(pair + 1, 1 - par, m, first)
                    if k >= 2:
                        copy_turned(pair, k - 2)
                    elif not first:
                        copy_turned(pair - 1, UNITS - 2 + k)
                    if k in (0, 2) and not first:
                        out_hi(pair - 1, 2 + k // 2)
                    if k in (4, 6):
                        out_hi(pair, k // 2 - 2)
                    if k == 4 and not first:
                        copy_y(pair - 1)
                if last:
                    copy_turned(pair, UNITS - 2)
                    copy_turned(pair, UNITS - 1)
                    out_hi(pair, 2)
                    out_hi(pair, 3)
                    copy_y(pair)

            for m in range(0, GROUPS, 2):
                read_out(0, 0, m, True)
            act.wait_ge(s["bo"], 16)
            in_two_pairs(act, lambda dp, first, last: (one_pair(dp * 2, 0, first, False), one_pair(dp * 2 + 1, 1, False, last)))

        @block.vector
        def _(dve):
            ln_rows_vector(dve, g, n, g.x)
            dve.wait_ge(s["raw"], 64)
            for k in range(4):
                cols = slice(k * INNER, (k + 1) * INNER)
                dve.tensor_copy(w_hi[:, cols], raw[:, cols]).then_inc(s["w_hi"], 1)
            ln_lo_vector(dve, g, n)
            for k in range(2):
                cols = slice(k * INNER, (k + 1) * INNER)
                dve.wait_ge(s["w_hi"], k + 1)
                dve.tensor_tensor(w_lo[:, cols], raw[:, cols], w_hi[:, cols].bitcast(F32), ALU.subtract).then_inc(s["w_lo_qk"], 1)

            def context_now(pair, par):
                tok = ds(pair * (2 * S), 2 * S)
                dve.wait_ge(s["proj"], floor0(pair * GROUPS - GROUPS))
                for x, y_ in zip(ctx_now[par], (ctx_hi, ctx_lo)):
                    dve.tensor_copy(x[:, :], y_[:, tok]).then_inc(s["c_now"], 1)

            def read_out(pair, par, m, first):
                dve.wait_ge(s["proj"], pair * GROUPS + (m + 1))
                dve.wait_ge(s["scores"], floor0(pair * UNITS - UNITS)) if m < 8 else dve.wait_ge(s["weighed"], floor0(pair * RUNS - RUNS))
                if first and par:
                    dve.wait_ge(s["w_lo"], 2)
                dve.tensor_copy(group_out(par, m), bank(g, J0 + 1)).then_inc(s["proj_dve"], 1)

            def largest(pair, k):
                unit = pair * UNITS + k
                dve.wait_ge(s["scores"], unit + 1)
                dve.wait_ge(s["probs"], floor0(unit - 1))
                dve.tensor_reduce(neg_top[k % 2][:, :], four(bank(g, S0 + k % 2)), AX.X, ALU.max, negate=True).then_inc(s["neg_top"], 1)

            def invert(pair, k):
                unit = pair * UNITS + k
                dve.wait_ge(s["probs"], unit + 1)
                dve.wait_ge(s["normed"], floor0(unit - 1))
                dve.reciprocal(rden[k % 2][:, :], den[k % 2][:, :]).then_inc(s["rden"], 1)

            def out_lo(pair, r):
                dve.wait_ge(s["o_hi"], pair * RUNS + (r + 1))
                dve.tensor_tensor(blocks4(o_lo, r), four(bank(g, O0)), blocks4(o_hi, r).bitcast(F32), ALU.subtract).then_inc(s["o_lo"], 1)

            def add_y(pair):
                dve.wait_ge(s["y_turned"], pair + 1)
                tok = ds(pair * (2 * S), 2 * S)
                dve.tensor_tensor(g.x[:, tok], g.x[:, tok], bank(g, Y0)[:, 2 * S:4 * S], ALU.add).then_inc(s["added"], 1)

            def one_pair(pair, par, first, last):
                for k in range(UNITS):
                    largest(pair, k)
                    if not last:
                        for m in groups_at(k):
                            if m % 2:
                                read_out(pair + 1, 1 - par, m, first)
                    if k == 1 and not last:
                        context_now(pair + 1, 1 - par)
                    if k >= 1:
                        invert(pair, k - 1)
                    elif not first:
                        invert(pair - 1, UNITS - 1)
                    if k in (0, 2) and not first:
                        out_lo(pair - 1, 2 + k // 2)
                    if k in (4, 6):
                        out_lo(pair, k // 2 - 2)
                    if k == 5 and not first:
                        add_y(pair - 1)
                if last:
                    invert(pair, UNITS - 1)
                    out_lo(pair, 2)
                    out_lo(pair, 3)
                    add_y(pair)

            dve.wait_ge(s["mask"], 16)
            dve.tensor_scalar(mask[:, :], mask_words[:, :].bitcast(U8), MASKED, None, ALU.mult).then_inc(s["masked"], 1)
            dve.wait_ge(s["c_lo"], NCH)
            context_now(0, 0)
            for m in range(1, GROUPS, 2):
                read_out(0, 0, m, True)
            in_two_pairs(dve, lambda dp, first, last: (one_pair(dp * 2, 0, first, False), one_pair(dp * 2 + 1, 1, False, last)))
            dve.wait_ge(s["added"], PAIRS)


def groups_at(k):
    return ((0,), (1, 2), (3,), (4, 5), (6,), (7, 8), (9,), (10, 11))[k]

STAGES = {"a0": stage_l0_attention, "f0": stage_l0_ffn, "a1": stage_l1_recurrence, "f1": stage_l1_ffn,
          "a2": stage_l2_attention, "f2": stage_l2_ffn, "a3": stage_l3_attention, "f3": stage_l3_ffn}


def build(nc, w, out, stages):
    with ExitStack() as ctx:
        g = Bag()
        g.psum = ctx.enter_context(nc.psum_tensor("psum", [128, 8 * BANK], F32))
        g.x = sb(nc, ctx, "x_rows", T)
        g.ident = sb(nc, ctx, "ident", 128)
        g.ident_b = sb(nc, ctx, "ident_b", 128, BF16)
        g.pick_expert = sb(nc, ctx, "pick_expert", E * 128, BF16)
        g.gate_t = sb(nc, ctx, "gate_t", T, BF16)
        g.head_rows = sb(nc, ctx, "head_rows", HG)
        g.priority = sb(nc, ctx, "priority", E)
        g.minus_half = sb(nc, ctx, "minus_half", B)
        loaded, ready = ctx.enter_context(nc.semaphore("g_loaded")), ctx.enter_context(nc.semaphore("g_ready"))
        with ExitStack() as first, nc.Block() as block:
            pick_raw = sb(nc, first, "pick_raw", E * 128)

            @block.sync
            def _(sp):
                sp.dma_start(g.x[:, :].rearrange("p (b d) -> p b d", b=B), w["x"].rearrange("b s d -> s b d")).then_inc(loaded, 16)
                sp.dma_start(g.ident[:, :], w["ident"]).then_inc(loaded, 16)
                sp.dma_start(pick_raw[:, :], w["pick_expert"]).then_inc(loaded, 16)
                sp.dma_start(g.priority[:, :], w["priority"]).then_inc(loaded, 16)
                sp.dma_start(g.head_rows[:, :], w["head_rows"]).then_inc(loaded, 16)
                sp.wait_ge(loaded, 80)

            @block.vector
            def _(dve):
                dve.memset(g.minus_half[:, :], -0.5).then_inc(ready, 1)
                dve.memset(g.gate_t[:, :], 0.0).then_inc(ready, 1)
                dve.wait_ge(loaded, 80)
                dve.tensor_copy(g.ident_b[:, :], g.ident[:, :]).then_inc(ready, 1)
                dve.tensor_copy(g.pick_expert[:, :], pick_raw[:, :]).then_inc(ready, 1)
                dve.wait_ge(ready, 4)
        for name in stages:
            with nc.cleanup_on_exit():
                STAGES[name](nc, g, w)
        stored = ctx.enter_context(nc.semaphore("g_stored"))
        with nc.Block() as block:
            @block.sync
            def _(sp):
                sp.dma_start(out.rearrange("b s d -> s b d"), g.x[:, :].rearrange("p (b d) -> p b d", b=B)).then_inc(stored, 16)
                sp.wait_ge(stored, 16)


def layouts(a):
    import numpy as np
    w = {"x": a["x"]}
    w["ident"] = np.eye(128, dtype=np.float32)
    w["pick_expert"] = np.zeros((128, E * 128), np.float32)
    w["pick_expert"][:NB3 * E] = np.tile(np.repeat(np.eye(E), 128, axis=1), (NB3, 1))
    w["priority"] = np.tile(np.arange(E, 0, -1, dtype=np.float32), (128, 1))

    def blocks(m):
        return m.reshape(-1, 128, m.shape[-1]).transpose(1, 0, 2).reshape(128, -1)

    w["f0_wr"], w["f0_br"] = a["L0_ffn_Wr"].T, a["L0_ffn_br"]
    w["f0_w"] = np.stack([np.concatenate([a["L0_ffn_W1"][e].T, blocks(a["L0_ffn_W2"][e].T),
                                          a["L0_ffn_b1"][e].reshape(FB, 128).T, a["L0_ffn_b2"][e][:, None]], 1) for e in range(E)])
    w["f0_gamma"], w["f0_beta"] = a["L0_ffn_gamma"], a["L0_ffn_beta"]
    w["ctx_t"] = a["ctx_1024"].reshape(T, D).T
    w["a1_w"] = np.concatenate([a["L1_xattn_" + k].T for k in ("Wi", "Wg", "A", "Bm", "Wo")], 1)
    w["a1_bias"] = np.stack([a["L1_xattn_bi"], a["L1_xattn_bg"], a["L1_xattn_bo"],
                             np.repeat(a["L1_xattn_decay"][0, :, 0], D // HEADS)], 1)
    w["head_rows"] = np.tile(np.repeat(np.eye(HG, dtype=np.float32), DH, axis=0), (128 // (HG * DH), 1))
    w["a0_w"] = np.concatenate([a["L0_xattn_Wq"], a["L0_xattn_Wk"], a["L0_xattn_Wv"], blocks(a["L0_xattn_Wo"])], 1)
    w["a0_bo"] = a["L0_xattn_bo"][:, None]
    w["mask"] = a["mask_BxSxS2_bk1"].view(np.int32)
    w["energy"] = a["ctxb_2048x32"]
    for p, k in (("a2_", "L2_xattn_"), ("a3_", "L3_xattn_")):
        def stacked(m):
            return np.tile(m.reshape(-1, NG, 1, HG * DH), (1, 1, 3, 1)).reshape(m.shape[0], -1)
        w[p + "w"] = np.concatenate([stacked(a[k + "Wq"]), stacked(a[k + "Wk"]), a[k + "Wv"], a[k + "Wo"]], 1)
        bias = np.zeros((128, 2 * NG + 1), np.float32)
        bias[:ST, :NG] = stacked(a[k + "bq"][None]).reshape(NG, ST).T
        bias[:ST, NG:2 * NG] = stacked(a[k + "bk"][None]).reshape(NG, ST).T
        bias[:, 2 * NG] = a[k + "bo"]
        w[p + "bias"], w[p + "bv"] = bias, a[k + "bv"]
    w["f3_wr"] = a["L3_ffn_Wr"].T
    w["f3_w"] = np.concatenate([a["L3_ffn_W1"][E - 1], blocks(a["L3_ffn_W2"][E - 1]),
                                a["L3_ffn_b1"][E - 1].reshape(FB, 128).T, a["L3_ffn_b2"][E - 1][:, None]], 1)[None]
    w["f1_wr"] = a["L1_ffn_router_w"].T
    w["f1_w"] = np.concatenate([a["L1_ffn_up_proj"], a["L1_ffn_down_proj"]], 2)
    w["f2_wr"], w["f2_br"] = a["L2_ffn_gate_w"].T, a["L2_ffn_expert_bias"]
    rows = np.zeros((E, -(-HIDDEN2 // 128) * 128, D), np.float32)
    rows[:, :HIDDEN2] = a["L2_ffn_w2"]
    w["f2_w"] = np.stack([np.concatenate([a["L2_ffn_w1"][e], a["L2_ffn_w3"][e], blocks(rows[e])], 1) for e in range(E)])
    return w


def kernel(**inputs):
    import numpy as np
    from concourse import bacc
    from concourse.bass_utils import run_bass_kernel_spmd

    w = {k: np.ascontiguousarray(v) for k, v in layouts({k: np.asarray(v) for k, v in inputs.items()}).items()}
    nc = bacc.Bacc("TRN2", target_bir_lowering=False, num_devices=1)
    aps = {k: nc.dram_tensor(f"in_{k}", v.shape, mybir.dt.from_np(v.dtype), kind="ExternalInput").ap() for k, v in w.items()}
    out = nc.dram_tensor("out_x", (B, S, D), F32, kind="ExternalOutput").ap()
    build(nc, aps, out, list(STAGES))
    r = run_bass_kernel_spmd(nc, [{f"in_{k}": v for k, v in w.items()}], core_ids=[0])
    return r.results[0]["out_x"]
```
